# Optimizing a Trainium2 kernel written in Bass

```python
import numpy as np
import jax
import jax.numpy as jnp

def _softmax(x, axis=-1):
    return jax.nn.softmax(x, axis=axis)

def _gelu(x):
    return jax.nn.gelu(x, approximate=True)

def _silu(x):
    return jax.nn.silu(x)

def _sigmoid(x):
    return jax.nn.sigmoid(x)

def _layernorm(x, axis=-1, eps=1e-05):
    m = jnp.mean(x, axis=axis, keepdims=True)
    v = jnp.var(x, axis=axis, keepdims=True)
    return (x - m) / jnp.sqrt(v + eps)

def _scatter_add(tgt, idx, src, axis=0):
    return tgt.at[idx].add(src)

def _segment_sum(src, seg, n):
    return jax.ops.segment_sum(src, seg, n)
kernel_name = 'mk_xattn_ffn_d2_seqx_r8_35ece4'

def setup_inputs(seed: int=0):
    np.random.seed(seed)
    _w = jnp.asarray

    def _rec_inputs():
        import jax
        import jax.numpy as jnp
        _rk = jax.random.key(seed)
        x = -0.0005207 + 1.001 * jax.random.normal(jax.random.fold_in(_rk, 1), (16, 128, 128), jnp.float32)
        _lenS = 128 - jax.random.randint(jax.random.fold_in(_rk, 7), (16,), 0, max(1, 128 // 4) + 1, jnp.int32)
        _lenS2 = 120 - jax.random.randint(jax.random.fold_in(_rk, 8), (16,), 0, max(1, 120 // 4) + 1, jnp.int32)
        _ctx_1024P = jax.random.normal(jax.random.fold_in(_rk, 11), (16, 16, 128), jnp.float32)
        _ctx_1024c = jax.random.dirichlet(jax.random.fold_in(_rk, 511), 0.3 * jnp.ones((16,), jnp.float32), (16, 120))
        _ctx_1024t = jnp.einsum('bsk,bkd->bsd', _ctx_1024c, _ctx_1024P)
        _ctx_1024t = _ctx_1024t * jax.lax.rsqrt(jnp.mean(jnp.square(_ctx_1024t)) + 1e-12) * 0.953939
        ctx_1024 = -0.000514642 + 1.00011 * (_ctx_1024t + 0.3 * jax.random.normal(jax.random.fold_in(_rk, 611), (16, 120, 128), jnp.float32))
        return (x, ctx_1024)
    x, ctx_1024 = _rec_inputs()

    def _L0_xattn_setup():
        import jax, jax.numpy as jnp
        import numpy as np
        import math
        B, S, D, H = (1, 256, 128, 16)
        DK = D // H
        DH = 64
        LOG_T_MIN = math.log(0.1)
        LOG_T_MAX = math.log(10.0)

        def _linear(x, W, b):
            return x @ W.T + b
        key = jax.random.key(seed)
        ks = jax.random.split(key, 20)
        p = 0.02
        return {'query': jax.random.normal(ks[0], (B, S, D), jnp.float32), 'key': jax.random.normal(ks[1], (B, S, D), jnp.float32), 'value': jax.random.normal(ks[2], (B, S, D), jnp.float32), 'Wq': jax.random.normal(ks[3], (D, D), jnp.float32) * p, 'bq': jax.random.normal(ks[4], (D,), jnp.float32) * p, 'Wk': jax.random.normal(ks[5], (D, D), jnp.float32) * p, 'bk': jax.random.normal(ks[6], (D,), jnp.float32) * p, 'Wv': jax.random.normal(ks[7], (D, D), jnp.float32) * p, 'bv': jax.random.normal(ks[8], (D,), jnp.float32) * p, 'Wo': jax.random.normal(ks[9], (D, D), jnp.float32) * p, 'bo': jax.random.normal(ks[10], (D,), jnp.float32) * p, 'w1': jax.random.normal(ks[11], (DH, 3), jnp.float32) * 0.3, 'b1': jax.random.normal(ks[12], (DH,), jnp.float32) * 0.1, 'w2': jax.random.normal(ks[13], (DH, DH), jnp.float32) * 0.1, 'b2': jax.random.normal(ks[14], (DH,), jnp.float32) * 0.1, 'w3': jax.random.normal(ks[15], (1, DH), jnp.float32) * 0.1, 'b3': jnp.full((1,), (LOG_T_MIN + LOG_T_MAX) / 2, jnp.float32)}
    _L0_xattn_all = _L0_xattn_setup()
    _L0_xattn_in = {k: v for k, v in _L0_xattn_all.items() if k in ('Wq', 'bq', 'Wk', 'bk', 'Wv', 'bv', 'Wo', 'bo', 'w1', 'b1', 'w2', 'b2', 'w3', 'b3')}
    del _L0_xattn_all

    def _L0_ffn_setup():
        import jax, jax.numpy as jnp
        import numpy as np
        DIM = 128
        HIDDEN = 256
        N_EXPERTS = 8
        TOP_K = 2
        EPS = 1e-06

        def rms_norm(x, scale, eps=EPS):
            ms = jnp.mean(jnp.square(x.astype(jnp.float32)), axis=-1, keepdims=True)
            s = scale.astype(jnp.float32) * jax.lax.rsqrt(ms + eps)
            return x * s.astype(x.dtype)

        def moe_linear(xf, ids, W):
            E = W.shape[0]
            out = jnp.zeros((xf.shape[0], W.shape[1]), dtype=xf.dtype)
            for e in range(E):
                out = out + jnp.where((ids == e)[:, None], xf @ W[e].T, 0.0)
            return out
        key = jax.random.key(seed)
        k1, k2, k3, k4 = jax.random.split(key, 4)
        x = jax.random.normal(k1, (4, 512, DIM), dtype=jnp.float32)
        norm_scale = jnp.ones((DIM,), dtype=jnp.float32)
        w_router = jax.random.normal(k2, (N_EXPERTS, DIM), dtype=jnp.float32) / np.sqrt(DIM)
        lim_up = np.sqrt(6.0 / (DIM + 2 * HIDDEN))
        w_up = jax.random.uniform(k3, (N_EXPERTS, 2 * HIDDEN, DIM), dtype=jnp.float32, minval=-lim_up, maxval=lim_up)
        lim_dn = np.sqrt(6.0 / (HIDDEN + DIM))
        w_down = jax.random.uniform(k4, (N_EXPERTS, DIM, HIDDEN), dtype=jnp.float32, minval=-lim_dn, maxval=lim_dn)
        return {'x': x, 'norm_scale': norm_scale, 'w_router': w_router, 'w_up': w_up, 'w_down': w_down}
    _L0_ffn_all = _L0_ffn_setup()
    _L0_ffn_in = {k: v for k, v in _L0_ffn_all.items() if k in ('norm_scale', 'w_router', 'w_up', 'w_down')}
    del _L0_ffn_all

    def _L1_xattn_setup():
        import jax, jax.numpy as jnp
        import numpy as np
        B, L, D_MODEL = (2, 256, 128)
        HEADS, DH, K = (8, 128, 64)
        DILATIONS = np.array([1, 1, 2, 2, 4, 4, 8, 8], dtype=np.int32)
        key = jax.random.key(seed)
        ks = jax.random.split(key, 8)
        s_in = 1.0 / np.sqrt(D_MODEL)
        s_c = 1.0 / np.sqrt(HEADS * DH)
        return {'query': jax.random.normal(ks[0], (B, L, D_MODEL), dtype=jnp.float32), 'key': jax.random.normal(ks[1], (B, L, D_MODEL), dtype=jnp.float32), 'value': jax.random.normal(ks[2], (B, L, D_MODEL), dtype=jnp.float32), 'Wq': jax.random.uniform(ks[3], (HEADS, DH, D_MODEL), minval=-s_in, maxval=s_in), 'bq': jnp.zeros((HEADS, DH), dtype=jnp.float32), 'Wk': jax.random.uniform(ks[4], (HEADS, DH, D_MODEL), minval=-s_in, maxval=s_in), 'bk': jnp.zeros((HEADS, DH), dtype=jnp.float32), 'Wv': jax.random.uniform(ks[5], (HEADS, DH, D_MODEL), minval=-s_in, maxval=s_in), 'bv': jnp.zeros((HEADS, DH), dtype=jnp.float32), 'Wc': jax.random.uniform(ks[6], (D_MODEL, HEADS * DH), minval=-s_c, maxval=s_c), 'bc': jnp.zeros((D_MODEL,), dtype=jnp.float32)}
    _L1_xattn_all = _L1_xattn_setup()
    _L1_xattn_in = {k: v for k, v in _L1_xattn_all.items() if k in ('Wq', 'bq', 'Wk', 'bk', 'Wv', 'bv', 'Wc', 'bc')}
    del _L1_xattn_all

    def _L1_ffn_setup():
        import jax, jax.numpy as jnp
        import numpy as np
        D_MODEL = 128
        D_FF = 512
        N_EXPERTS = 8
        TOP_K = 2
        D_FF_PER = D_FF // N_EXPERTS
        B, T = (4, 256)
        key = jax.random.key(seed)
        ks = jax.random.split(key, 7)
        b1_bound = 1.0 / np.sqrt(D_MODEL)
        b2_bound = 1.0 / np.sqrt(D_FF_PER)
        return {'x': jax.random.normal(ks[0], (B, T, D_MODEL), dtype=jnp.float32), 'router_w': jax.random.uniform(ks[1], (D_MODEL, N_EXPERTS), minval=-b1_bound, maxval=b1_bound, dtype=jnp.float32), 'router_b': jax.random.uniform(ks[2], (N_EXPERTS,), minval=-b1_bound, maxval=b1_bound, dtype=jnp.float32), 'W1': jax.random.uniform(ks[3], (N_EXPERTS, D_MODEL, D_FF_PER), minval=-b1_bound, maxval=b1_bound, dtype=jnp.float32), 'b1': jax.random.uniform(ks[4], (N_EXPERTS, D_FF_PER), minval=-b1_bound, maxval=b1_bound, dtype=jnp.float32), 'W2': jax.random.uniform(ks[5], (N_EXPERTS, D_FF_PER, D_MODEL), minval=-b2_bound, maxval=b2_bound, dtype=jnp.float32), 'b2': jax.random.uniform(ks[6], (N_EXPERTS, D_MODEL), minval=-b2_bound, maxval=b2_bound, dtype=jnp.float32)}
    _L1_ffn_all = _L1_ffn_setup()
    _L1_ffn_in = {k: v for k, v in _L1_ffn_all.items() if k in ('router_w', 'router_b', 'W1', 'b1', 'W2', 'b2')}
    del _L1_ffn_all
    return {'x': x, 'ctx_1024': ctx_1024, 'L0_xattn_Wq': _L0_xattn_in['Wq'], 'L0_xattn_bq': _L0_xattn_in['bq'], 'L0_xattn_Wk': _L0_xattn_in['Wk'], 'L0_xattn_bk': _L0_xattn_in['bk'], 'L0_xattn_Wv': _L0_xattn_in['Wv'], 'L0_xattn_bv': _L0_xattn_in['bv'], 'L0_xattn_Wo': _L0_xattn_in['Wo'], 'L0_xattn_bo': _L0_xattn_in['bo'], 'L0_xattn_w1': _L0_xattn_in['w1'], 'L0_xattn_b1': _L0_xattn_in['b1'], 'L0_xattn_w2': _L0_xattn_in['w2'], 'L0_xattn_b2': _L0_xattn_in['b2'], 'L0_xattn_w3': _L0_xattn_in['w3'], 'L0_xattn_b3': _L0_xattn_in['b3'], 'L0_ffn_norm_scale': _L0_ffn_in['norm_scale'], 'L0_ffn_w_router': _L0_ffn_in['w_router'], 'L0_ffn_w_up': _L0_ffn_in['w_up'], 'L0_ffn_w_down': _L0_ffn_in['w_down'], 'L1_xattn_Wq': _L1_xattn_in['Wq'], 'L1_xattn_bq': _L1_xattn_in['bq'], 'L1_xattn_Wk': _L1_xattn_in['Wk'], 'L1_xattn_bk': _L1_xattn_in['bk'], 'L1_xattn_Wv': _L1_xattn_in['Wv'], 'L1_xattn_bv': _L1_xattn_in['bv'], 'L1_xattn_Wc': _L1_xattn_in['Wc'], 'L1_xattn_bc': _L1_xattn_in['bc'], 'L1_ffn_router_w': _L1_ffn_in['router_w'], 'L1_ffn_router_b': _L1_ffn_in['router_b'], 'L1_ffn_W1': _L1_ffn_in['W1'], 'L1_ffn_b1': _L1_ffn_in['b1'], 'L1_ffn_W2': _L1_ffn_in['W2'], 'L1_ffn_b2': _L1_ffn_in['b2']}

def reference(x, ctx_1024, L0_xattn_Wq, L0_xattn_bq, L0_xattn_Wk, L0_xattn_bk, L0_xattn_Wv, L0_xattn_bv, L0_xattn_Wo, L0_xattn_bo, L0_xattn_w1, L0_xattn_b1, L0_xattn_w2, L0_xattn_b2, L0_xattn_w3, L0_xattn_b3, L0_ffn_norm_scale, L0_ffn_w_router, L0_ffn_w_up, L0_ffn_w_down, L1_xattn_Wq, L1_xattn_bq, L1_xattn_Wk, L1_xattn_bk, L1_xattn_Wv, L1_xattn_bv, L1_xattn_Wc, L1_xattn_bc, L1_ffn_router_w, L1_ffn_router_b, L1_ffn_W1, L1_ffn_b1, L1_ffn_W2, L1_ffn_b2):
    import jax
    import jax.numpy as jnp

    def _L0_xattn_ref(query, key, value, Wq, bq, Wk, bk, Wv, bv, Wo, bo, w1, b1, w2, b2, w3, b3):
        import jax, jax.numpy as jnp
        import numpy as np
        import math
        B, S, D, H = (1, 256, 128, 16)
        DK = D // H
        DH = 64
        LOG_T_MIN = math.log(0.1)
        LOG_T_MAX = math.log(10.0)

        def _linear(x, W, b):
            return x @ W.T + b
        b, sq, d = query.shape
        sk = key.shape[1]
        h, dk = (H, DK)
        Q = _linear(query, Wq, bq).reshape(b, sq, h, dk).transpose(0, 2, 1, 3)
        K = _linear(key, Wk, bk).reshape(b, sk, h, dk).transpose(0, 2, 1, 3)
        V = _linear(value, Wv, bv).reshape(b, sk, h, dk).transpose(0, 2, 1, 3)
        qk = jnp.einsum('bhqd,bhkd->bhqk', Q, K)
        scores = qk / math.sqrt(dk)
        mean_sim = scores.mean(axis=(-2, -1))
        max_sim = scores.max(axis=-1).mean(axis=-1)
        probs = jax.nn.softmax(scores, axis=-1)
        entropy_proxy = jnp.var(probs, axis=-1, ddof=1).mean(axis=-1)
        feats = jnp.stack([mean_sim, max_sim, entropy_proxy], axis=-1)
        hidden = jax.nn.gelu(_linear(feats, w1, b1), approximate=False)
        hidden = jax.nn.gelu(_linear(hidden, w2, b2), approximate=False)
        log_t = jnp.clip(_linear(hidden, w3, b3), LOG_T_MIN, LOG_T_MAX)
        t = jnp.exp(log_t)[..., None]
        attn_scores = qk / (2.0 * t)
        attn = jax.nn.softmax(attn_scores, axis=-1)
        attn = jnp.nan_to_num(attn, nan=0.0)
        out = jnp.einsum('bhqk,bhkd->bhqd', attn, V)
        out = out.transpose(0, 2, 1, 3).reshape(b, sq, d)
        return _linear(out, Wo, bo)

    def _L0_ffn_ref(x, norm_scale, w_router, w_up, w_down):
        import jax, jax.numpy as jnp
        import numpy as np
        DIM = 128
        HIDDEN = 256
        N_EXPERTS = 8
        TOP_K = 2
        EPS = 1e-06

        def rms_norm(x, scale, eps=EPS):
            ms = jnp.mean(jnp.square(x.astype(jnp.float32)), axis=-1, keepdims=True)
            s = scale.astype(jnp.float32) * jax.lax.rsqrt(ms + eps)
            return x * s.astype(x.dtype)

        def moe_linear(xf, ids, W):
            E = W.shape[0]
            out = jnp.zeros((xf.shape[0], W.shape[1]), dtype=xf.dtype)
            for e in range(E):
                out = out + jnp.where((ids == e)[:, None], xf @ W[e].T, 0.0)
            return out
        B, S, D = x.shape
        skip = x
        xn = rms_norm(x, norm_scale)
        scores = (xn @ w_router.T).astype(jnp.float32)
        scores_topk, idx = jax.lax.top_k(scores, TOP_K)
        weights = jax.nn.softmax(scores_topk, axis=-1)
        xf = jnp.broadcast_to(xn[..., None, :], (B, S, TOP_K, D)).reshape(-1, D)
        ids = idx.reshape(-1)
        up = moe_linear(xf, ids, w_up)
        u, gate = jnp.split(up, 2, axis=-1)
        h = u * jax.nn.silu(gate)
        down = moe_linear(h, ids, w_down)
        down = down.reshape(B, S, TOP_K, D)
        out = jnp.sum(down * weights[..., None].astype(down.dtype), axis=-2)
        return out + skip

    def _L1_xattn_ref(query, key, value, Wq, bq, Wk, bk, Wv, bv, Wc, bc):
        import jax, jax.numpy as jnp
        import numpy as np
        B, L, D_MODEL = (2, 256, 128)
        HEADS, DH, K = (8, 128, 64)
        DILATIONS = np.array([1, 1, 2, 2, 4, 4, 8, 8], dtype=np.int32)
        Lq = query.shape[-2]
        q = jnp.einsum('bld,hed->bhle', query, Wq) + bq[:, None, :]
        k = jnp.einsum('bld,hed->bhle', key, Wk) + bk[:, None, :]
        v = jnp.einsum('bld,hed->bhle', value, Wv) + bv[:, None, :]
        offsets = jnp.arange(K) - (K - 1) // 2
        dil = jnp.asarray(DILATIONS)
        idx = jnp.arange(Lq)[None, :, None] + offsets[None, None, :] * dil[:, None, None]
        valid = (idx >= 0) & (idx < Lq)
        idxc = jnp.clip(idx, 0, Lq - 1)
        gather = jax.vmap(lambda xh, ih: xh[:, ih], in_axes=(1, 0), out_axes=1)
        k_win = gather(k, idxc)
        v_win = gather(v, idxc)
        scores = jnp.einsum('bhld,bhlkd->bhlk', q, k_win)
        scores = jnp.where(valid[None], scores, jnp.asarray(-1000000000.0, scores.dtype))
        attn = jax.nn.softmax(scores, axis=-1)
        out = jnp.einsum('bhlk,bhlkd->bhld', attn, v_win)
        out = out.transpose(0, 2, 1, 3).reshape(out.shape[0], Lq, HEADS * DH)
        return out @ Wc.T + bc

    def _L1_ffn_ref(x, router_w, router_b, W1, b1, W2, b2):
        import jax, jax.numpy as jnp
        import numpy as np
        D_MODEL = 128
        D_FF = 512
        N_EXPERTS = 8
        TOP_K = 2
        D_FF_PER = D_FF // N_EXPERTS
        B, T = (4, 256)
        router_logits = x @ router_w + router_b
        routing_weights = jax.nn.softmax(router_logits, axis=-1)
        top_k_weights, top_k_indices = jax.lax.top_k(routing_weights, TOP_K)
        top_k_weights = top_k_weights / jnp.sum(top_k_weights, axis=-1, keepdims=True)
        routing_mask = jnp.zeros_like(routing_weights)
        routing_mask = jnp.take_along_axis(routing_mask, top_k_indices, axis=-1)
        b_idx = jnp.arange(x.shape[0])[:, None, None]
        t_idx = jnp.arange(x.shape[1])[None, :, None]
        routing_mask = jnp.zeros_like(routing_weights).at[b_idx, t_idx, top_k_indices].set(top_k_weights)
        h1 = jnp.einsum('btd,nde->btne', x, W1) + b1
        h1 = jax.nn.gelu(h1, approximate=False)
        out_per_expert = jnp.einsum('btne,nef->btnf', h1, W2) + b2
        output = jnp.sum(out_per_expert * routing_mask[..., None], axis=-2)
        return output
    x = x + _L0_xattn_ref(_layernorm(x, axis=-1), ctx_1024, ctx_1024, L0_xattn_Wq, L0_xattn_bq, L0_xattn_Wk, L0_xattn_bk, L0_xattn_Wv, L0_xattn_bv, L0_xattn_Wo, L0_xattn_bo, L0_xattn_w1, L0_xattn_b1, L0_xattn_w2, L0_xattn_b2, L0_xattn_w3, L0_xattn_b3)
    x = x + _L0_ffn_ref(_layernorm(x, axis=-1), L0_ffn_norm_scale, L0_ffn_w_router, L0_ffn_w_up, L0_ffn_w_down)
    x = x + _L1_xattn_ref(_layernorm(x, axis=-1), ctx_1024, ctx_1024, L1_xattn_Wq, L1_xattn_bq, L1_xattn_Wk, L1_xattn_bk, L1_xattn_Wv, L1_xattn_bv, L1_xattn_Wc, L1_xattn_bc)
    x = x + _L1_ffn_ref(_layernorm(x, axis=-1), L1_ffn_router_w, L1_ffn_router_b, L1_ffn_W1, L1_ffn_b1, L1_ffn_W2, L1_ffn_b2)
    return x

_drawn_inputs = setup_inputs


def setup_inputs(seed=0):
    import zlib

    import numpy as np

    out = dict(_drawn_inputs(seed))
    spreads = {'L0_ffn_norm_scale': (1.0, 0.2),
     'L1_xattn_bq': (0.0, 0.1),
     'L1_xattn_bk': (0.0, 0.8),
     'L1_xattn_bv': (0.0, 0.289),
     'L1_xattn_bc': (0.0, 0.1)}
    factors = {'L0_xattn_Wq': 8.0,
     'L0_xattn_bq': 8.0,
     'L0_xattn_Wk': 8.0,
     'L0_xattn_bk': 8.0,
     'L0_xattn_bv': 7.146,
     'L0_xattn_w1': 8.0,
     'L0_xattn_b1': 8.0,
     'L0_xattn_w2': 8.0,
     'L0_xattn_b2': 8.0,
     'L0_xattn_w3': 8.0,
     'L1_ffn_router_b': 3.41,
     'L1_ffn_b1': 8.0}
    for name, (base, spread) in spreads.items():
        noise = np.random.default_rng([zlib.crc32(name.encode()), seed]).standard_normal(out[name].shape)
        drawn = base * np.exp(spread * noise) if base else spread * noise
        out[name] = jnp.asarray(drawn.astype(out[name].dtype))
    for name, factor in factors.items():
        out[name] = (out[name] * factor).astype(out[name].dtype)
    return out
```

```python
import math
from contextlib import ExitStack

import numpy as np

import concourse.bass as bass
from concourse import mybir

F32 = mybir.dt.float32
BF16 = mybir.dt.bfloat16
U32 = mybir.dt.uint32
ALU = mybir.AluOpType
ACT = mybir.ActivationFunctionType
AX_X = mybir.AxisListType.X

P = 128

NB, LQ, LK, D = 16, 128, 120, 128
H0, DK0 = 16, 8
DH0 = 64
NE = 8
HID0 = 256
H1, E1 = 8, 128
K1, DILATIONS = 64, (1, 2, 4, 8)
F1 = 64
LOG_T_MIN, LOG_T_MAX = math.log(0.1), math.log(10.0)
LN_EPS, RMS_EPS = 1e-5, 1e-6
NEG = -1.0e9
BH = NB * H0
HALF0 = H0 // 2
UP_TILES = 2 * HID0 // P
DN_TILES = HID0 // P
H1_TILES = NE * F1 // P


def shape_constants():
    ident = np.eye(P, dtype=np.float32)
    part = np.arange(P)[:, None]
    headmask = (part // DK0 == np.arange(H0)[None, :]).astype(np.float32)
    mask = np.full((LQ, len(DILATIONS), LK), NEG, np.float64)
    for n, dil in enumerate(DILATIONS):
        count = np.zeros((LQ, LK))
        for l in range(LQ):
            for o in range(K1):
                at = l + (o - (K1 - 1) // 2) * dil
                if 0 <= at < LQ:
                    count[l, min(at, LK - 1)] += 1
        mask[:, n][count > 0] = np.log(count[count > 0])
    iota = np.tile(np.arange(NE, dtype=np.float32), (P, 1))
    sel = np.zeros((P, 3, P), np.float32)
    for c, w in enumerate((1.0 / (LQ * LK * math.sqrt(DK0)), -1.0 / LQ, 1.0 / LQ)):
        sel[c, c, :] = w
    cols, at, parts = {}, 0, []
    for name, a in (("ident", ident), ("headmask", headmask), ("headscale", headmask / math.sqrt(DK0)),
                    ("window", mask.reshape(LQ, -1)),
                    ("iota", iota), ("sel", sel.reshape(P, -1))):
        cols[name] = (at, at + a.shape[1])
        at += a.shape[1]
        parts.append(a.astype(np.float32))
    return cols, np.ascontiguousarray(np.concatenate(parts, axis=1))


def software_pipeline(eng, stages, n=NB, peel=4):
    assert all(lag <= peel - 2 for lag, _ in stages) and (n - peel) % 2 == 0

    def step(b, parity):
        for lag, stage in stages:
            if not isinstance(b, int) or 0 <= b - lag < n:
                stage(b - lag, (parity - lag) % 2)

    for b in range(peel):
        step(b, b % 2)
    with eng.Fori(0, (n - peel) // 2) as i:
        for parity in range(2):
            step(i * 2 + (peel + parity), parity)
    for b in range(n, n + peel):
        step(b, b % 2)


def reused(eng, sem, b, per=1):
    if not isinstance(b, int) or b >= 2:
        eng.wait_ge(sem, (b - 1) * per)


def build(nc, cols, t, out):
    with ExitStack() as ctx:
        def sb(name, shape, dt=F32):
            return ctx.enter_context(nc.sbuf_tensor(name, shape, dt))[:]

        def sem(name):
            return ctx.enter_context(nc.semaphore(name))

        psum = ctx.enter_context(nc.psum_tensor("psum", [P, 8, 512], F32))
        BANK_KEEP, BANK_TAIL = 7, 6

        cst = sb("cst", [P, cols["sel"][1]])
        ident = cst[:, slice(*cols["ident"])]
        headmask = cst[:, slice(*cols["headmask"])]
        headscale = cst[:, slice(*cols["headscale"])]
        window = cst[:, slice(*cols["window"])].rearrange("p (n k) -> p n k", n=len(DILATIONS))
        iota = cst[:, slice(*cols["iota"])]
        sel = cst[:, slice(*cols["sel"])].rearrange("p (c q) -> p c q", c=3)
        x = sb("x", [P, NB, D])
        ctxT = sb("ctxT", [P, NB, LK])
        qT = sb("qT", [P, NB, LQ])
        kT = sb("kT", [P, NB, LK])
        v0 = sb("v0", [LK, NB, D])
        xT = sb("xT", [P, NB, LQ])
        gate = sb("gate", [P, NB, NE])
        bnout = sb("bnout", [P, BH, 6])
        rowneg = sb("rowneg", [P, BH])
        negmax = sb("negmax", [P, 2, H0])
        qsum = sb("qsum", [P, NB])
        ksum = sb("ksum", [P, NB])
        invt = sb("invt", [P, BH])
        invtT = sb("invtT", [P, NB])
        small = sb("small", [P, 8, BH])
        ones = sb("ones", [P, P])
        onesb = sb("onesb", [P, LK], BF16)
        w4T = sb("w4T", [P, 4, D])
        upT = sb("upT", [P, NE * UP_TILES, P])
        dnT = sb("dnT", [P, NE * DN_TILES, D])
        routerT = sb("routerT", [P, NE])
        w1f = sb("w1f", [P, 3, DH0])
        w1T = sb("w1T", [3, DH0])
        w2T = sb("w2T", [DH0, DH0])
        w3c = sb("w3c", [DH0, P])
        qk1 = sb("qk1", [P, H1, D])
        vo1 = sb("vo1", [P, H1, D])
        cvec = sb("cvec", [P, H1])
        uvec = sb("uvec", [P, H1])
        ubias = sb("ubias", [P, H1])
        bout1 = sb("bout1", [1, D])
        router1 = sb("router1", [P, NE])
        ew1 = sb("ew1", [P, NE, F1])
        ew2 = sb("ew2", [P, H1_TILES, D])
        b2rows = sb("b2rows", [P, D])
        gateT = sb("gateT", [P, P])
        vecs = sb("vecs", [P, 16])
        bq0, bk0, b1c, b2c, b3c, nscale = (vecs[:, i:i + 1] for i in range(6))
        b1e = vecs[:, 6:6 + H1_TILES]
        bv0 = sb("bv0", [LK, D])
        bo0 = sb("bo0", [1, D])
        bc1 = sb("bc1", [1, D])
        rb1 = sb("rb1", [P, NE])
        bqk1 = sb("bqk1", [P, 3, H1])
        nat0 = sb("nat0", [P, 5, D])
        wsm = sb("wsm", [P, 3 + DH0 + DH0])
        eps = sb("eps", [P, 4])
        carried = sb("carried", [P, 8])
        bn6 = sb("bn6", [P, 2, 6])
        mv = sb("mv", [P, 2, 2])
        rstd = sb("rstd", [P, 2, 4])
        mean0 = sb("mean0", [P, NB, 2])
        rstd0 = sb("rstd0", [P, NB])
        xn = sb("xn", [P, 2, D])
        xnT = sb("xnT", [P, 2, LQ])
        work = sb("work", [P, 13312])

        def area(at, n):
            return work[:, at:at + n]

        W_UP, W_DN, W_L1, W_C = 2048, 6144, 8192, 11264
        upN = area(W_UP, 4096).rearrange("p (t d) -> p t d", d=D)
        dnN = area(W_DN, 2048).rearrange("p (e h) -> p e h", e=NE)
        l1N = area(W_L1, 3072).rearrange("p (w h d) -> p w h d", w=3, h=H1)
        wcN = area(W_C, 1024).rearrange("p (h e) -> p h e", h=H1)
        wcT = area(W_C + 1024, 1024).rearrange("p (h o) -> p h o", h=H1)
        wa = sb("wa", [P, 8688])
        kexp = wa[:, 0:3840].rearrange("p (z h k) -> p z h k", z=2, h=H0)
        prob = wa[:, 3840:7680].rearrange("p (z h k) -> p z h k", z=2, h=H0)
        craw = wa[0:LK, 7680:7936].rearrange("p (z d) -> p z d", z=2)
        xc = wa[:, 7936:8432].rearrange("p (z c) -> p z c", z=2)
        qs = wa[:, 8432:8688].rearrange("p (z q) -> p z q", z=2)
        mrow = wa[:, 0:H0 * LQ].bitcast(BF16).rearrange("p (z c) -> p z c", z=2)
        vpad = wa[0:LK, 2048:3328].rearrange("p (z g c) -> p z g c", z=2, g=4)
        opad = sb("opad", [LK, 160])
        qexp = area(0, 4096).rearrange("p (z h q) -> p z h q", z=2, h=H0)
        probT = area(4096, 4096)[0:LK].rearrange("p (z h q) -> p z h q", z=2, h=H0)
        ktS = area(8192, 240).rearrange("p (z k) -> p z k", z=2)
        qsc = area(8432, 256).rearrange("p (z q) -> p z q", z=2)
        rden = area(8688, 256).rearrange("p (z q) -> p z q", z=2)
        oT = area(8944, 256).rearrange("p (z q) -> p z q", z=2)
        xr = area(9200, 256).rearrange("p (z d) -> p z d", z=2)
        mparts = sb("mparts", [P, 2, 2, LQ], BF16)
        silu = area(0, 512).rearrange("p (z c) -> p z c", z=2)
        hT = area(512, 512).rearrange("p (z c) -> p z c", z=2)
        q2 = area(1024, 2048).rearrange("p (z h q) -> p z h q", z=2, h=H1)
        s1 = area(3072, 1920).rearrange("p (z h k) -> p z h k", z=2, h=H1)
        e1 = area(4992, 1920).rearrange("p (z h k) -> p z h k", z=2, h=H1)
        a1 = area(6912, 1920).rearrange("p (z h k) -> p z h k", z=2, h=H1)
        a1T = area(8832, 2048)[0:LK].rearrange("p (z h q) -> p z h q", z=2, h=H1)
        vw = area(10880, 2048)[0:LK].rearrange("p (z h d) -> p z h d", z=2, h=H1)
        cS = area(12928, 240).rearrange("p (z k) -> p z k", z=2)
        d8 = sb("d8", [P, 2, 6, H1])
        h1 = wa[:, 0:1024].rearrange("p (z m q) -> p z m q", z=2, m=H1_TILES)
        b2blk = wa[:, 1024:1280].rearrange("p (z d) -> p z d", z=2)
        yacc = wa[:, 1280:1536].rearrange("p (z d) -> p z d", z=2)
        lg = small[:, 1, 0:P].rearrange("p (b e) -> p b e", b=NB)
        mx8 = small[:, 1, P:2 * P].rearrange("p (b e) -> p b e", b=NB)
        ix8 = sb("ix8", [P, NB, 8], U32)
        rt = sb("rt", [P, 6, NB])
        u1s = small[:, 2, 0:P].rearrange("p (b h) -> p b h", b=NB)
        oh = small[:, 0, :].rearrange("p (j b e) -> p j b e", j=2, b=NB)
        mscratch = nc.dram_tensor("mscratch", (2, NB, H0, LQ), BF16, kind="Internal").ap()

        def banks(a, n, parts=P):
            return psum[0:parts, a:a + n, :]

        keep = psum[:, BANK_KEEP, :]
        logits0 = keep[:, 0:128].rearrange("p (b e) -> p b e", b=NB)
        u1 = keep[:, 128:256].rearrange("p (b e) -> p b e", b=NB)
        logits1 = keep[:, 256:384].rearrange("p (b e) -> p b e", b=NB)
        tail_ps = psum[:, BANK_TAIL, 0:LQ]

        ld_first, ld_x, ld_w, ld_ctx = sem("ld_first"), sem("ld_x"), sem("ld_w"), [sem("ld_ctx0"), sem("ld_ctx1")]
        ld_m = [sem("ld_m0"), sem("ld_m1")]
        consts_set = sem("consts_set")
        w0_ps, w0_sb = sem("w0_ps"), sem("w0_sb")
        wt_ps, wt_sb = sem("wt_ps"), [sem("wt_sb0"), sem("wt_sb1")]
        ln0_st, ln0_ag, ln0_eps, ln0_r = sem("ln0_st"), sem("ln0_ag"), sem("ln0_eps"), sem("ln0_r")
        a_xn, a_tps, a_xc, a_ctx, a_qkv, a_q, a_k, a_v, a_kexp, a_qkeep = (
            sem("a_" + n) for n in ("xn", "tps", "xc", "ctx", "qkv", "q", "k", "v", "kexp", "qkeep"))
        a_nkeep = sem("a_nkeep")
        a_s, a_max, a_neg, a_exp, a_bn = (sem("a_" + n) for n in ("s", "max", "neg", "exp", "bn"))
        m_dve, m_pe, m_act, m_store = sem("m_dve"), sem("m_pe"), sem("m_act"), sem("m_store")
        b_kt, b_v, b_qsc, b_qexp, b_s, b_exp, b_od, b_rden, b_oT, b_y, b_x1, b_x = (
            sem("b_" + n) for n in ("kt", "v", "qsc", "qexp", "s", "exp", "od", "rden", "oT", "y", "x1", "x"))
        tails = {ph: {n: sem(f"{ph}t_{n}") for n in ("bn", "ag", "pool", "r", "xn", "xr", "tp", "ev", "lg", "keep")}
                 for ph in "bcd"}
        mrow_zero = sem("mrow_zero")
        r_dve, r_act, gates_set = sem("r_dve"), sem("r_act"), sem("gates_set")
        c_up, c_silu, c_h, c_dn, c_acc = (sem("c_" + n) for n in ("up", "silu", "h", "dn", "acc"))
        d_cs, d_q, d_q2, d_s, d_sm, d_max, d_mu, d_sh, d_exp, d_rs, d_a, d_tp, d_aT, d_vwp, d_vw, d_y, d_x = (
            sem("d_" + n) for n in ("cs", "q", "q2", "s", "sm", "max", "mu", "sh", "exp", "rs", "a", "tp",
                                    "aT", "vwp", "vw", "y", "x"))
        d_u = sem("d_u")
        e_gt, e_gts, e_h, e_g, e_b2, e_y, e_acc = (
            sem("e_" + n) for n in ("gt", "gts", "h", "g", "b2", "y", "acc"))
        e_out = [sem("e_out0"), sem("e_out1")]

        N_FIRST, N_W = 9, 26 + NB
        block = ctx.enter_context(nc.Block())

        @block.sync
        def _(sp):
            sp.dma_start(cst[:, :], t["consts"]).then_inc(ld_first, 16)
            for i, n in enumerate(("L0_xattn_Wq", "L0_xattn_Wk", "L0_xattn_Wv", "L0_xattn_Wo")):
                sp.dma_start(nat0[:, i, :], t[n]).then_inc(ld_first, 16)
            sp.dma_start(bq0, t["L0_xattn_bq"].rearrange("(p c) -> p c", c=1)).then_inc(ld_first, 16)
            sp.dma_start(bk0, t["L0_xattn_bk"].rearrange("(p c) -> p c", c=1)).then_inc(ld_first, 16)
            sp.dma_start(bv0[:, :], t["L0_xattn_bv"].rearrange("(a d) -> a d", a=1).to_broadcast([LK, D])
                         ).then_inc(ld_first, 16)
            sp.dma_start(bo0[:, :], t["L0_xattn_bo"].rearrange("(a d) -> a d", a=1)).then_inc(ld_first, 16)

            def load_ctx(b, z):
                reused(sp, a_tps, b)
                sp.dma_start(craw[:, z, :], t["ctx_1024"][b]).then_inc(ld_ctx[z], 16)

            software_pipeline(sp, [(0, load_ctx)])

            sp.wait_ge(m_store, 32)
            sp.wait_ge(mrow_zero, 1)

            def load_m(b, z):
                reused(sp, b_s, b, 2)
                sp.dma_start(mrow[0:2, z, :], mscratch[:, b].rearrange("c h q -> c (h q)")).then_inc(ld_m[z], 16)

            software_pipeline(sp, [(0, load_m)])

            def store(b, z):
                sp.wait_ge(e_acc, (b + 1) * (NE + 1))
                sp.dma_start(out[b], yacc[:, z, :]).then_inc(e_out[z], 16)

            software_pipeline(sp, [(0, store)])
            for z in range(2):
                sp.wait_ge(e_out[z], 16 * NB // 2)

        def weight_groups():
            groups = []
            for g in range(NE * UP_TILES // 4):
                groups.append((upT[:, 4 * g:4 * g + 4, :], [("turn", upN[:, 4 * g + i, :]) for i in range(4)]))
            for g in range(NE * DN_TILES // 4):
                groups.append((dnT[:, 4 * g:4 * g + 4, :],
                               [("turn", dnN[:, 2 * g + i // 2, (i % 2) * P:(i % 2 + 1) * P]) for i in range(4)]))
            for g in range(H1 // 4):
                groups.append((wcT[:, 4 * g:4 * g + 4, :], [("turn", wcN[:, 4 * g + i, :]) for i in range(4)]))
            for g in range(H1 // 4):
                groups.append((qk1[:, 4 * g:4 * g + 4, :],
                               [("prod", l1N[:, 0, 4 * g + i, :], l1N[:, 1, 4 * g + i, :]) for i in range(4)]))
            for g in range(H1 // 4):
                groups.append((vo1[:, 4 * g:4 * g + 4, :],
                               [("prod", l1N[:, 2, 4 * g + i, :], wcT[:, 4 * g + i, :]) for i in range(4)]))
            return groups

        WC_GROUPS = range(12, 14)
        N_GROUPS = 18
        RING_W = 4

        def weight_copies(ns, eng, which):
            for g, (dst, _) in enumerate(weight_groups()):
                if g % 2 == which:
                    eng.wait_ge(wt_ps, g + 1)
                    src = psum[:, g % RING_W, :].rearrange("p (i d) -> p i d", d=D)
                    (ns.tensor_copy(dst, src) if which == 0 else ns.copy(dst, src)).then_inc(wt_sb[which], 1)

        M_CLIPPED, M_PARTS = 17, 22
        R_DIFF, R_COUNT = 4, 13

        @block.scalar
        def _(act):
            for i in range(4):
                act.dma_start(x[:, 4 * i:4 * i + 4, :], t["x"][4 * i:4 * i + 4].rearrange("b t d -> t b d")
                              ).then_inc(ld_x, 16)
            up_rows = t["L0_ffn_w_up"].rearrange("e (t p) d -> p (e t) d", p=P)
            loads = [
                (wsm[0:DH0, 0:3], t["L0_xattn_w1"]),
                (wsm[0:DH0, 3:3 + DH0], t["L0_xattn_w2"]),
                (wsm[0:1, 3 + DH0:3 + 2 * DH0], t["L0_xattn_w3"]),
                (b1c[0:DH0], t["L0_xattn_b1"].rearrange("(p c) -> p c", c=1)),
                (b2c[0:DH0], t["L0_xattn_b2"].rearrange("(p c) -> p c", c=1)),
                (b3c, t["L0_xattn_b3"].rearrange("(a c) -> a c", a=1).to_broadcast([P, 1])),
                (nscale, t["L0_ffn_norm_scale"].rearrange("(p c) -> p c", c=1)),
                (nat0[0:NE, 4, :], t["L0_ffn_w_router"]),
                (upN[:, 0:16], up_rows[:, 0:16]),
                (upN[:, 16:32], up_rows[:, 16:32]),
                (dnN, t["L0_ffn_w_down"].rearrange("e p h -> p e h")),
                (l1N[:, 0], t["L1_xattn_Wq"].rearrange("h e d -> e h d")),
                (l1N[:, 1], t["L1_xattn_Wk"].rearrange("h e d -> e h d")),
                (l1N[:, 2], t["L1_xattn_Wv"].rearrange("h e d -> e h d")),
                (wcN, t["L1_xattn_Wc"].rearrange("o (h e) -> o h e", h=H1)),
                (bqk1[:, 0], t["L1_xattn_bq"].rearrange("h e -> e h")),
                (bqk1[:, 1], t["L1_xattn_bk"].rearrange("h e -> e h")),
                (bqk1[:, 2], t["L1_xattn_bv"].rearrange("h e -> e h")),
                (bc1[:, :], t["L1_xattn_bc"].rearrange("(a d) -> a d", a=1)),
                (router1[:, :], t["L1_ffn_router_w"]),
                (rb1[:, :], t["L1_ffn_router_b"].rearrange("(a d) -> a d", a=1).to_broadcast([P, NE])),
                (ew1[:, :, :], t["L1_ffn_W1"].rearrange("n d e -> d n e")),
                (ew2[0:F1], t["L1_ffn_W2"].rearrange("(m j) f d -> j f m d", j=2)[0]),
                (ew2[F1:P], t["L1_ffn_W2"].rearrange("(m j) f d -> j f m d", j=2)[1]),
                (b1e[0:F1], t["L1_ffn_b1"].rearrange("(m j) f -> j f m", j=2)[0]),
                (b1e[F1:P], t["L1_ffn_b1"].rearrange("(m j) f -> j f m", j=2)[1]),
            ] + [(b2rows[NE * b:NE * (b + 1), :], t["L1_ffn_b2"]) for b in range(NB)]
            assert len(loads) == N_W
            for dst, src in loads:
                act.dma_start(dst, src, allow_slow_non_contiguous=True).then_inc(ld_w, 16)

            act.wait_ge(ld_first, 16 * N_FIRST)

            def a_project(b, z):
                act.wait_ge(a_qkv, b + 1)
                reused(act, a_s, b, 2)
                reused(act, a_qkeep, b)
                nc.scalar.activation(qs[:, z, :], psum[:, 1, 0:LQ], ACT.Identity, bias=bq0,
                                     accum_out=qsum[:, bass.ds(b, 1)]).then_inc(a_q, 1)
                nc.scalar.activation(kT[:, b, :], psum[:, 1, LQ:LQ + LK], ACT.Identity, bias=bk0,
                                     accum_out=ksum[:, bass.ds(b, 1)]).then_inc(a_k, 1)

            def a_softmax(half):
                def run(b, z):
                    act.wait_ge(a_neg, b * 2 + half + 1)
                    if half == 0:
                        reused(act, a_bn, b, 2)
                    for h in range(HALF0):
                        hh = half * HALF0 + h
                        e = nc.scalar.activation(
                            prob[:, z, hh, :], psum[:, 3 + 2 * half + h // 4, (h % 4) * LK:(h % 4 + 1) * LK],
                            ACT.Exp, bias=negmax[:, z, hh:hh + 1])
                    e.then_inc(a_exp, 1)
                return run

            software_pipeline(act, [(3, a_softmax(0)), (1, a_project), (3, a_softmax(1))], peel=6)

            weight_copies(nc.scalar, act, 1)

            act.wait_ge(m_pe, 5)
            nc.scalar.activation(small[0:DH0, 6, :], psum[0:DH0, 4, 0:BH], ACT.Gelu, bias=b1c[0:DH0]
                                 ).then_inc(m_act, 1)
            act.wait_ge(m_pe, 6)
            nc.scalar.activation(small[0:DH0, 7, :], psum[0:DH0, 5, 0:BH], ACT.Gelu, bias=b2c[0:DH0]
                                 ).then_inc(m_act, 1)
            act.wait_ge(m_dve, M_CLIPPED)
            nc.scalar.activation(invt[:, :], small[:, 1, :], ACT.Exp, scale=-1.0).then_inc(m_act, 1)
            act.wait_ge(m_dve, M_PARTS)
            for half in range(2):
                act.dma_start(mscratch[:, 8 * half:8 * half + 8].rearrange("c b h q -> (b h) c q"),
                              mparts[:, half, :, :]).then_inc(m_store, 16)

            def b_softmax(half):
                def run(b, z):
                    act.wait_ge(b_s, b * 2 + half + 1)
                    if half == 0:
                        reused(act, b_od, b)
                    nc.scalar.activation(
                        probT[:, z, half * HALF0:(half + 1) * HALF0, :].rearrange("p h q -> p (h q)"),
                        psum[0:LK, 2 * half:2 * half + 2, :].rearrange("p a c -> p (a c)"), ACT.Exp
                    ).then_inc(b_exp, 1)
                return run

            def tail_evict(ph):
                s = tails[ph]

                def run(b, z):
                    act.wait_ge(s["tp"], b + 1)
                    reused(act, s["keep"], b)
                    reused(act, s["lg"], b)
                    if ph == "b":
                        nc.scalar.mul(xnT[:, z, :], tail_ps, nscale).then_inc(s["ev"], 1)
                    else:
                        nc.scalar.copy(xnT[:, z, :], tail_ps).then_inc(s["ev"], 1)
                return run

            software_pipeline(act, [(5, tail_evict("b")), (1, b_softmax(0)), (1, b_softmax(1))], peel=8)

            def route_exp(n):
                act.wait_ge(r_dve, R_DIFF + n * R_COUNT)
                nc.scalar.activation(rt[:, 1, :], rt[:, 0, :], ACT.Exp).then_inc(r_act, 1)

            route_exp(0)

            def c_gates(experts):
                def run(b, z):
                    for e in experts:
                        act.wait_ge(c_up, b * NE + e + 1)
                        nc.scalar.activation(silu[:, e % 2, :], psum[:, e % 2, HID0:2 * HID0], ACT.Silu
                                             ).then_inc(c_silu, 1)
                return run

            software_pipeline(act, [(0, c_gates([0])), (3, tail_evict("c")), (0, c_gates(range(1, NE)))], peel=6)

            def d_vw_copy(b, z):
                act.wait_ge(d_vwp, b + 1)
                reused(act, d_y, b)
                nc.scalar.copy(vw[:, z].rearrange("p h d -> p (h d)"),
                               psum[0:LK, 4:6, :].rearrange("p a c -> p (a c)")).then_inc(d_vw, 1)

            def d_softmax(b, z):
                act.wait_ge(d_sh, b + 1)
                reused(act, d_a, b)
                for h in range(H1):
                    e = nc.scalar.activation(e1[:, z, h, :], s1[:, z, h, :], ACT.Exp, bias=d8[:, z, 3, h:h + 1],
                                             accum_out=d8[:, z, 4, h:h + 1])
                e.then_inc(d_exp, 1)

            def d_aT_copy(b, z):
                act.wait_ge(d_tp, b + 1)
                nc.scalar.copy(a1T[:, z].rearrange("p h q -> p (h q)"),
                               psum[0:LK, 4:6, :].rearrange("p a c -> p (a c)")).then_inc(d_aT, 1)

            software_pipeline(act, [(6, tail_evict("d")), (3, d_vw_copy), (1, d_softmax), (3, d_aT_copy)], peel=8)
            route_exp(1)

            def e_gelu(b, z):
                act.wait_ge(e_h, b + 1)
                reused(act, e_y, b)
                for m in range(H1_TILES):
                    g = nc.scalar.activation(h1[:, z, m, :], psum[:, z, m * LQ:(m + 1) * LQ], ACT.Gelu,
                                             bias=b1e[:, m:m + 1])
                g.then_inc(e_g, 1)

            software_pipeline(act, [(0, e_gelu)])

        @block.gpsimd
        def _(pool):
            nc.gpsimd.memset(eps[:, 0:1], -0.5)
            nc.gpsimd.memset(eps[:, 1:2], LN_EPS)
            nc.gpsimd.memset(eps[:, 2:3], RMS_EPS).then_inc(consts_set, 1)
            nc.gpsimd.memset(onesb[:, :], 0.0).then_inc(consts_set, 1)
            nc.gpsimd.memset(opad[:, :], 0.0).then_inc(consts_set, 1)
            pool.wait_ge(consts_set, 4)
            nc.gpsimd.memset(onesb[0:2, :], 1.0)
            nc.gpsimd.memset(opad.rearrange("p (i c) -> p i c", c=40)[:, :, 0:DK0], 1.0).then_inc(consts_set, 1)
            half_power = eps[:, 0:1]

            pool.wait_ge(ln0_ag, 1)
            nc.gpsimd.tensor_scalar(rstd0[:, :], mean0[:, :, 1], LN_EPS, None, ALU.add).then_inc(ln0_eps, 1)
            pool.wait_ge(ln0_eps, 1)
            nc.gpsimd.tensor_tensor(rstd0[:, :], rstd0[:, :], half_power.to_broadcast([P, NB]), ALU.pow
                                    ).then_inc(ln0_r, 1)

            pool.wait_ge(ld_first, 16 * N_FIRST)

            def a_keep_context(b, z):
                pool.wait_ge(a_xc, b + 1)
                nc.gpsimd.tensor_copy(ctxT[:, b, :], xc[:, z, LQ:LQ + LK]).then_inc(a_ctx, 1)

            def a_keep(b, z):
                pool.wait_ge(a_q, b + 1)
                nc.gpsimd.tensor_copy(qT[:, b, :], qs[:, z, :]).then_inc(a_qkeep, 1)

            def a_keep_max(b, z):
                pool.wait_ge(a_neg, b * 2 + 2)
                nc.gpsimd.tensor_copy(rowneg[:, bass.ds(b * H0, H0)], negmax[:, z, :]).then_inc(a_nkeep, 1)

            def a_expand(b, z):
                pool.wait_ge(a_k, b + 1)
                reused(pool, a_s, b, 2)
                nc.gpsimd.tensor_tensor(kexp[:, z], kT[:, b, :].unsqueeze(1).to_broadcast([P, H0, LK]),
                                        headscale.unsqueeze(2).to_broadcast([P, H0, LK]), ALU.mult
                                        ).then_inc(a_kexp, 1)

            software_pipeline(pool, [(1, a_keep_context), (1, a_expand), (1, a_keep), (3, a_keep_max)], peel=6)

            def tail_rstd(ph):
                s, per = tails[ph], 6 if ph == "b" else 2

                def run(b, z):
                    pool.wait_ge(s["ag"], b + 1)
                    reused(pool, s["xr" if ph == "b" else "xn"], b)
                    r = [rstd[:, z, i:i + 1] for i in range(4)]
                    var = mv[:, z, 1:2]
                    nc.gpsimd.tensor_tensor(r[0], var, eps[:, 1:2], ALU.add).then_inc(s["pool"], 1)
                    pool.wait_ge(s["pool"], b * per + 1)
                    nc.gpsimd.tensor_tensor(r[1], r[0], half_power, ALU.pow).then_inc(s["pool"], 1)
                    if ph == "b":
                        pool.wait_ge(s["pool"], b * per + 2)
                        nc.gpsimd.tensor_tensor(r[2], r[1], r[1], ALU.mult).then_inc(s["pool"], 1)
                        pool.wait_ge(s["pool"], b * per + 3)
                        nc.gpsimd.tensor_tensor(r[0], r[2], var, ALU.mult).then_inc(s["pool"], 1)
                        pool.wait_ge(s["pool"], b * per + 4)
                        nc.gpsimd.tensor_tensor(r[2], r[0], eps[:, 2:3], ALU.add).then_inc(s["pool"], 1)
                        pool.wait_ge(s["pool"], b * per + 5)
                        nc.gpsimd.tensor_tensor(r[3], r[2], half_power, ALU.pow).then_inc(s["pool"], 1)
                return run

            def tail_keep(ph):
                s = tails[ph]

                def run(b, z):
                    pool.wait_ge(s["ev"], b + 1)
                    nc.gpsimd.tensor_copy(xT[:, b, :], xnT[:, z, :]).then_inc(s["keep"], 1)
                return run

            def b_stage(b, z):
                reused(pool, b_s, b, 2)
                nc.gpsimd.tensor_copy(ktS[:, z, :], kT[:, b, :]).then_inc(b_kt, 1)
                reused(pool, b_od, b)
                nc.gpsimd.tensor_copy(
                    vpad[:, z].rearrange("p g (i c) -> p g i c", c=40)[:, :, :, 0:DK0],
                    v0[:, b, :].rearrange("p (g i j) -> p g i j", g=4, j=DK0)).then_inc(b_v, 1)

            pool.wait_ge(m_pe, 2)
            pool.wait_ge(a_s, 2 * NB)
            pool.wait_ge(a_bn, 2 * NB)
            pool.wait_ge(a_xc, NB)
            nc.gpsimd.memset(wa[:, 0:H0 * LQ], 0.0).then_inc(mrow_zero, 1)
            nc.gpsimd.memset(vpad[:, :, :, :], 0.0).then_inc(consts_set, 1)
            pool.wait_ge(consts_set, 6)
            software_pipeline(pool, [(0, b_stage), (3, tail_rstd("b")), (5, tail_keep("b"))], peel=8)
            software_pipeline(pool, [(2, tail_rstd("c")), (3, tail_keep("c"))], peel=6)

            def d_stage(b, z):
                reused(pool, d_vwp, b)
                nc.gpsimd.tensor_copy(cS[:, z, :], ctxT[:, b, :]).then_inc(d_cs, 1)

            software_pipeline(pool, [(2, d_stage), (4, tail_rstd("d")), (6, tail_keep("d"))], peel=8)

        @block.vector
        def _(dve):
            nc.vector.memset(ones[:, :], 1.0).then_inc(consts_set, 1)
            dve.wait_ge(w0_ps, 1)
            nc.vector.tensor_copy(w4T[:, :, :], psum[:, 0, :].rearrange("p (i d) -> p i d", i=4)).then_inc(w0_sb, 1)
            dve.wait_ge(ld_x, 64)
            bn0 = wa[:, 0:NB * 6].rearrange("p (b s) -> p b s", b=NB)
            for b in range(NB):
                i = nc.vector.bn_stats(bn0[:, b, :], x[:, b, :])
            i.then_inc(ln0_st, 1)
            dve.wait_ge(ln0_st, 1)
            for b in range(NB):
                i = nc.vector.bn_aggr(mean0[:, b, :], bn0[:, b, :])
            i.then_inc(ln0_ag, 1)
            dve.wait_ge(ln0_r, 1)

            carriers = []

            def carrier():
                n = len(carriers)
                carriers.append(sem(f"carried{n}"))

                def stats_wait(b, *waits):
                    for s, v in waits + ((carriers[n], b),):
                        if not isinstance(v, int) or v > 0:
                            dve.wait_ge(s, v)
                    nc.vector.memset(carried[:, n:n + 1], 0.0).then_inc(carriers[n], 1)
                return stats_wait

            def a_norm(b, z):
                reused(dve, a_tps, b)
                nc.vector.tensor_scalar(xn[:, z, :], x[:, b, :], mean0[:, b, 0:1], rstd0[:, bass.ds(b, 1)],
                                        ALU.subtract, ALU.mult).then_inc(a_xn, 1)

            def a_turned(b, z):
                dve.wait_ge(a_tps, b + 1)
                reused(dve, a_qkv, b)
                reused(dve, a_ctx, b)
                nc.vector.tensor_copy(xc[:, z, :], psum[:, 0, 0:LQ + LK]).then_inc(a_xc, 1)

            def a_values(b, z):
                dve.wait_ge(a_qkv, b + 1)
                nc.vector.tensor_tensor(v0[:, b, :], psum[0:LK, 2, 0:D], bv0[:, :], ALU.add).then_inc(a_v, 1)

            def a_rowmax(half):
                def run(b, z):
                    dve.wait_ge(a_s, b * 2 + half + 1)
                    if half == 0:
                        reused(dve, a_exp, b, 2)
                        reused(dve, a_nkeep, b)
                    nc.vector.tensor_reduce(
                        negmax[:, z, half * HALF0:(half + 1) * HALF0].rearrange("p (a h) -> p a h", a=2),
                        psum[:, 3 + 2 * half:5 + 2 * half, 0:4 * LK].rearrange("p a (h k) -> p a h k", k=LK),
                        AX_X, ALU.max, negate=True).then_inc(a_neg, 1)
                return run

            def a_stats(half):
                stats_wait = carrier()

                def run(b, z):
                    stats_wait(b, (a_exp, b * 2 + half + 1))
                    for h in range(half * HALF0, (half + 1) * HALF0):
                        s = nc.vector.bn_stats(bnout[:, bass.ds(b * H0 + h, 1), :].rearrange("p a s -> p (a s)"),
                                               prob[:, z, h, :])
                    s.then_inc(a_bn, 1)
                return run

            software_pipeline(dve, [(0, a_norm), (4, a_stats(0)), (3, a_rowmax(0)), (1, a_turned), (4, a_stats(1)),
                                    (1, a_values), (3, a_rowmax(1))], peel=6)

            weight_copies(nc.vector, dve, 0)

            dve.wait_ge(m_pe, 1)
            nc.vector.tensor_copy(w1T[:, :], psum[0:3, 4, 8:8 + DH0]).then_inc(m_dve, 1)
            nc.vector.tensor_copy(w2T[:, :], psum[0:DH0, 4, 128:128 + DH0]).then_inc(m_dve, 1)
            nc.vector.tensor_copy(w3c[:, :], psum[0:DH0, 4, 256:256 + P]).then_inc(m_dve, 1)
            nc.vector.tensor_copy(routerT[:, :], psum[:, 4, 0:NE]).then_inc(m_dve, 1)
            nc.vector.tensor_copy(cvec[:, :], psum[:, 4, 400:408]).then_inc(m_dve, 1)
            nc.vector.tensor_copy(uvec[:, :], psum[:, 4, 408:416]).then_inc(m_dve, 1)
            nc.vector.tensor_tensor(small[:, 7, 0:H1], bqk1[:, 0], bqk1[:, 1], ALU.mult).then_inc(m_dve, 1)
            dve.wait_ge(m_pe, 2)
            nc.vector.tensor_copy(w1f.rearrange("p c h -> p (c h)"), psum[:, 5, 0:3 * DH0]).then_inc(m_dve, 1)
            nc.vector.tensor_copy(ubias[:, :], psum[:, 5, 200:208]).then_inc(m_dve, 1)
            nc.vector.tensor_copy(bout1[:, :], psum[0:1, 5, 256:256 + D]).then_inc(m_dve, 1)
            dve.wait_ge(a_nkeep, NB)
            dve.wait_ge(a_k, NB)
            dve.wait_ge(a_bn, 2 * NB)
            mean_e, m2_e, mean_o, m2_o = (bnout[:, :, i] for i in (1, 2, 4, 5))
            HALF_KEYS = LK // 2
            nc.vector.tensor_tensor(small[:, 0, :], mean_e, mean_o, ALU.add)
            nc.vector.tensor_tensor(small[:, 1, :], mean_e, mean_o, ALU.subtract)
            nc.vector.tensor_tensor(small[:, 5, 0:NB], qsum[:, :], ksum[:, :], ALU.mult).then_inc(m_dve, 1)
            dve.wait_ge(m_dve, 11)
            nc.vector.tensor_tensor(small[:, 2, :], small[:, 0, :], small[:, 0, :], ALU.mult)
            nc.vector.tensor_tensor(small[:, 3, :], small[:, 1, :], small[:, 1, :], ALU.mult)
            nc.vector.tensor_tensor(small[:, 4, :].rearrange("p (b h) -> p b h", b=NB),
                                    small[:, 5, 0:NB].unsqueeze(2).to_broadcast([P, NB, H0]),
                                    headmask.unsqueeze(1).to_broadcast([P, NB, H0]), ALU.mult).then_inc(m_dve, 1)
            dve.wait_ge(m_dve, 12)
            nc.vector.scalar_tensor_tensor(out=small[:, 1, :], in0=small[:, 3, :], scalar=HALF_KEYS / 2.0, in1=m2_e,
                                           op0=ALU.mult, op1=ALU.add)
            nc.vector.reciprocal(small[:, 0, :], small[:, 2, :]).then_inc(m_dve, 1)
            dve.wait_ge(m_dve, 13)
            nc.vector.tensor_tensor(small[:, 3, :], small[:, 1, :], m2_o, ALU.add).then_inc(m_dve, 1)
            dve.wait_ge(m_dve, 14)
            nc.vector.scalar_tensor_tensor(out=small[:, 2, :], in0=small[:, 3, :],
                                           scalar=1.0 / ((LK - 1) * HALF_KEYS ** 2), in1=small[:, 0, :],
                                           op0=ALU.mult, op1=ALU.mult).then_inc(m_dve, 1)
            dve.wait_ge(m_pe, 7)
            nc.vector.tensor_scalar(small[:, 0, :], psum[:, 4, 256:512], b3c, LOG_T_MIN, ALU.add, ALU.max
                                    ).then_inc(m_dve, 1)
            dve.wait_ge(m_dve, 16)
            nc.vector.tensor_scalar(small[:, 1, :], small[:, 0, :], LOG_T_MAX, math.log(2.0), ALU.min, ALU.add
                                    ).then_inc(m_dve, 1)
            dve.wait_ge(m_act, 3)
            nc.vector.scalar_tensor_tensor(out=small[:, 2, :], in0=rowneg[:, :], scalar=math.sqrt(DK0),
                                           in1=invt[:, :], op0=ALU.mult, op1=ALU.mult).then_inc(m_dve, 1)
            nc.vector.tensor_tensor(small[:, 3, :].rearrange("p (b h) -> p b h", b=NB),
                                    invt.rearrange("p (b h) -> p b h", b=NB),
                                    headmask.unsqueeze(1).to_broadcast([P, NB, H0]), ALU.mult).then_inc(m_dve, 1)
            dve.wait_ge(m_dve, 19)
            nc.vector.tensor_reduce(invtT[:, :], small[:, 3, :].rearrange("p (b h) -> p b h", b=NB), AX_X, ALU.add
                                    ).then_inc(m_dve, 1)
            dve.wait_ge(m_pe, 8)
            turned = psum[:, 5, 0:BH].rearrange("p (a q) -> p a q", a=2)
            nc.vector.tensor_copy(mparts[:, :, 0, :], turned).then_inc(m_dve, 1)
            dve.wait_ge(m_dve, 21)
            nc.vector.tensor_tensor(mparts[:, :, 1, :], turned, mparts[:, :, 0, :], ALU.subtract
                                    ).then_inc(m_dve, 1)

            def b_scale(b, z):
                reused(dve, b_qexp, b, 2)
                nc.vector.tensor_scalar(qsc[:, z, :], qT[:, b, :], invtT[:, bass.ds(b, 1)], None, ALU.mult
                                        ).then_inc(b_qsc, 1)

            def b_expand(half):
                def run(b, z):
                    dve.wait_ge(b_qsc, b + 1)
                    reused(dve, b_s, b, 2)
                    heads = slice(half * HALF0, (half + 1) * HALF0)
                    nc.vector.tensor_tensor(qexp[:, z, heads, :],
                                            qsc[:, z, :].unsqueeze(1).to_broadcast([P, HALF0, LQ]),
                                            headmask[:, heads].unsqueeze(2).to_broadcast([P, HALF0, LQ]), ALU.mult
                                            ).then_inc(b_qexp, 1)
                return run

            def b_recip(b, z):
                dve.wait_ge(b_od, b + 1)
                reused(dve, b_oT, b)
                nc.vector.reciprocal(rden[:, z, :], psum[:, 4, LQ:2 * LQ]).then_inc(b_rden, 1)

            def b_norm(b, z):
                dve.wait_ge(b_rden, b + 1)
                reused(dve, b_y, b)
                nc.vector.tensor_tensor(oT[:, z, :], psum[:, 4, 0:LQ], rden[:, z, :], ALU.mult).then_inc(b_oT, 1)

            def b_residual(b, z):
                dve.wait_ge(b_y, b + 1)
                nc.vector.tensor_tensor(x[:, b, :], psum[:, 5, 0:D], x[:, b, :], ALU.add).then_inc(b_x1, 1)

            def tail_stats(ph, ready, per):
                s, stats_wait = tails[ph], carrier()

                def run(b, z):
                    stats_wait(b, (ready, (b + 1) * per), (s["ag"], b - 1))
                    nc.vector.bn_stats(bn6[:, z, :], x[:, b, :]).then_inc(s["bn"], 1)
                return run

            def tail_aggr(ph):
                s, stats_wait, pool_per = tails[ph], carrier(), 6 if ph == "b" else 2

                def run(b, z):
                    stats_wait(b, (s["bn"], b + 1), (s["pool"], (b - 1) * pool_per), (s["xn"], b - 1))
                    nc.vector.bn_aggr(mv[:, z, :], bn6[:, z, :]).then_inc(s["ag"], 1)
                return run

            def tail_norm(ph):
                s, pool_per = tails[ph], 6 if ph == "b" else 2

                def run(b, z):
                    dve.wait_ge(s["pool"], (b + 1) * pool_per)
                    reused(dve, s["tp"], b)
                    if ph == "b":
                        reused(dve, s["xr"], b)
                    i = nc.vector.tensor_scalar(xn[:, z, :], x[:, b, :], mv[:, z, 0:1], rstd[:, z, 1:2],
                                                ALU.subtract, ALU.mult)
                    i.then_inc(s["xn"], 1)
                return run

            def tail_rms(b, z):
                s = tails["b"]
                dve.wait_ge(s["xn"], b + 1)
                nc.vector.tensor_scalar(xr[:, z, :], xn[:, z, :], rstd[:, z, 3:4], None, ALU.mult).then_inc(s["xr"], 1)
                nc.vector.tensor_tensor(x[:, b, :], x[:, b, :], xn[:, z, :], ALU.add).then_inc(b_x, 1)

            software_pipeline(dve, [(0, b_scale), (4, tail_norm("b")), (0, b_expand(0)), (4, tail_rms),
                                    (3, b_residual), (0, b_expand(1)), (3, tail_stats("b", b_x1, 1)), (2, b_recip),
                                    (3, tail_aggr("b")), (2, b_norm)], peel=8)

            def route(n, logits, bias):
                at = n * R_COUNT
                count = [at]

                def done(ins):
                    count[0] += 1
                    ins.then_inc(r_dve, 1)

                def after_all():
                    dve.wait_ge(r_dve, count[0])

                if bias is None:
                    done(nc.vector.tensor_copy(lg[:, :, :], logits))
                else:
                    done(nc.vector.tensor_tensor(lg[:, :, :], logits, bias.unsqueeze(1).to_broadcast([P, NB, NE]),
                                                 ALU.add))
                after_all()
                for b in range(NB):
                    i = nc.vector.max(mx8[:, b, :], lg[:, b, :])
                done(i)
                after_all()
                for b in range(NB):
                    i = nc.vector.max_index(ix8[:, b, :], mx8[:, b, :], lg[:, b, :])
                done(i)
                done(nc.vector.tensor_tensor(rt[:, 0, :], mx8[:, :, 1], mx8[:, :, 0], ALU.subtract))
                after_all()
                done(nc.vector.tensor_copy(rt[:, 4:6, :].rearrange("p j b -> p b j"), ix8[:, :, 0:2]))
                dve.wait_ge(r_act, n + 1)
                done(nc.vector.tensor_scalar(rt[:, 2, :], rt[:, 1, :], 1.0, None, ALU.add))
                after_all()
                done(nc.vector.reciprocal(rt[:, 3, :], rt[:, 2, :]))
                after_all()
                done(nc.vector.tensor_tensor(rt[:, 2, :], rt[:, 1, :], rt[:, 3, :], ALU.mult))
                experts = iota.unsqueeze(1).to_broadcast([P, NB, NE])
                for j in range(2):
                    done(nc.vector.tensor_tensor(oh[:, j], experts, rt[:, 4 + j, :].unsqueeze(2).to_broadcast([P, NB, NE]),
                                                 ALU.is_equal))
                after_all()
                for j in range(2):
                    done(nc.vector.tensor_tensor(oh[:, j], oh[:, j], rt[:, 3 - j, :].unsqueeze(2).to_broadcast([P, NB, NE]),
                                                 ALU.mult))
                after_all()
                done(nc.vector.tensor_tensor(gate[:, :, :], oh[:, 0], oh[:, 1], ALU.add))
                after_all()
                assert count[0] == at + R_COUNT

            dve.wait_ge(tails["b"]["lg"], NB)
            dve.wait_ge(b_x, NB)
            route(0, logits0, None)

            def c_hidden(b, e):
                u = b * NE + e
                dve.wait_ge(c_silu, u + 1)
                if not isinstance(u, int) or u >= 2:
                    dve.wait_ge(c_dn, u - 1)
                nc.vector.tensor_tensor(hT[:, e % 2, :], psum[:, e % 2, 0:HID0], silu[:, e % 2, :], ALU.mult
                                        ).then_inc(c_h, 1)

            def c_accumulate(b, e):
                u = b * NE + e
                dve.wait_ge(c_dn, u + 1)
                if e:
                    dve.wait_ge(c_acc, u)
                nc.vector.scalar_tensor_tensor(out=x[:, b, :], in0=psum[:, 2 + e % 2, 0:D],
                                               scalar=gate[:, b, e:e + 1], in1=x[:, b, :],
                                               op0=ALU.mult, op1=ALU.add).then_inc(c_acc, 1)

            def c_rest(b, z):
                for e in range(1, NE):
                    c_hidden(b, e)
                    c_accumulate(b, e - 1)

            software_pipeline(dve, [(0, lambda b, z: c_hidden(b, 0)), (1, lambda b, z: c_accumulate(b, NE - 1)),
                                    (2, tail_norm("c")), (1, tail_stats("c", c_acc, NE)), (0, c_rest),
                                    (1, tail_aggr("c"))], peel=6)

            def d_queries(b, z):
                dve.wait_ge(d_q, b + 1)
                reused(dve, d_s, b)
                nc.vector.tensor_tensor(q2[:, z].rearrange("p (a h) q -> p a h q", a=2),
                                        psum[:, 0:2, :].rearrange("p a (h q) -> p a h q", q=LQ),
                                        cvec.rearrange("p (a h) -> p a h", a=2).unsqueeze(3).to_broadcast([P, 2, 4, LQ]),
                                        ALU.add).then_inc(d_q2, 1)

            def d_scores(b, z):
                dve.wait_ge(d_s, b + 1)
                reused(dve, d_exp, b)
                for a in range(2):
                    i = nc.vector.tensor_tensor(
                        s1[:, z, 4 * a:4 * a + 4, :].rearrange("p (n i) k -> p n i k", n=2),
                        psum[:, 2 + a, 0:4 * LK].rearrange("p (n i k) -> p n i k", n=2, i=2),
                        window[:, 2 * a:2 * a + 2, :].unsqueeze(2).to_broadcast([P, 2, 2, LK]), ALU.add)
                i.then_inc(d_sm, 1)
                dve.wait_ge(d_sm, b + 1)
                reused(dve, d_mu, b)
                nc.vector.tensor_reduce(d8[:, z, 0, :], s1[:, z], AX_X, ALU.max, negate=True).then_inc(d_max, 1)
                dve.wait_ge(d_max, b + 1)
                reused(dve, d_sh, b)
                nc.vector.tensor_tensor(d8[:, z, 2, :], u1s[:, b, :], d8[:, z, 0, :], ALU.subtract).then_inc(d_mu, 1)
                dve.wait_ge(d_mu, b + 1)
                nc.vector.tensor_tensor(d8[:, z, 3, :], u1s[:, b, :], d8[:, z, 2, :], ALU.subtract).then_inc(d_sh, 1)

            def d_weights(b, z):
                dve.wait_ge(d_exp, b + 1)
                reused(dve, d_a, b)
                nc.vector.reciprocal(d8[:, z, 1, :], d8[:, z, 4, :]).then_inc(d_rs, 1)
                dve.wait_ge(d_rs, b + 1)
                reused(dve, d_tp, b)
                nc.vector.tensor_tensor(a1[:, z], e1[:, z], d8[:, z, 1, :].unsqueeze(2).to_broadcast([P, H1, LK]),
                                        ALU.mult).then_inc(d_a, 1)

            def d_residual(b, z):
                dve.wait_ge(d_y, b + 1)
                nc.vector.tensor_tensor(x[:, b, :], psum[:, BANK_TAIL, 128:128 + D], x[:, b, :], ALU.add
                                        ).then_inc(d_x, 1)

            dve.wait_ge(tails["c"]["lg"], NB)
            nc.vector.tensor_tensor(u1s[:, :, :], u1, ubias.unsqueeze(1).to_broadcast([P, NB, H1]), ALU.add
                                    ).then_inc(d_u, 1)
            dve.wait_ge(d_u, 1)
            software_pipeline(dve, [(5, tail_norm("d")), (1, d_scores), (0, d_queries), (2, d_weights),
                                    (4, d_residual), (4, tail_stats("d", d_x, 1)), (4, tail_aggr("d"))], peel=8)

            dve.wait_ge(tails["d"]["lg"], NB)
            route(1, logits1, rb1)
            dve.wait_ge(e_gt, 1)
            nc.vector.tensor_copy(gateT[:, :], psum[:, BANK_TAIL, 0:P]).then_inc(e_gts, 1)

            dve.wait_ge(tails["d"]["lg"], NB)

            def e_bias(b, z):
                reused(dve, e_y, b)
                nc.vector.tensor_scalar(b2blk[:, z, :], b2rows[:, :], headmask[:, bass.ds(b, 1)], None, ALU.mult
                                        ).then_inc(e_b2, 1)

            def e_accumulate(b, z):
                per = NE + 1
                dve.wait_ge(e_y, b + 1)
                if not isinstance(b, int) or b >= 2:
                    dve.wait_ge(e_out[z], (b - z) * 8)
                nc.vector.tensor_tensor(yacc[:, z, :], psum[:, BANK_TAIL + z, 0:D], x[:, b, :],
                                        ALU.add).then_inc(e_acc, 1)
                for e in range(NE):
                    dve.wait_ge(e_acc, b * per + e + 1)
                    nc.vector.scalar_tensor_tensor(
                        out=yacc[:, z, :], in0=psum[:, 2 + 2 * z + e % 2, (e // 2) * D:(e // 2 + 1) * D],
                        scalar=gate[:, b, e:e + 1], in1=yacc[:, z, :], op0=ALU.mult, op1=ALU.add).then_inc(e_acc, 1)

            software_pipeline(dve, [(0, e_bias), (1, e_accumulate)])

        @block.tensor
        def _(pe):
            def turn(dst, src, k):
                return nc.tensor.transpose(dst, src, ident[0:k, 0:k])

            pe.wait_ge(ld_first, 16 * N_FIRST)
            for i in range(4):
                m = turn(psum[:, 0, i * D:(i + 1) * D], nat0[:, i, :], P)
            m.then_inc(w0_ps, 1)
            pe.wait_ge(w0_sb, 1)

            def a_turn(b, z):
                pe.wait_ge(a_xn, b + 1)
                pe.wait_ge(ld_ctx[z], (b - z + 2) * 8)
                if not isinstance(b, int) or b >= 1:
                    pe.wait_ge(a_xc, b)
                turn(psum[:, 0, 0:LQ], xn[:, z, :], P)
                turn(psum[:, 0, LQ:LQ + LK], craw[:, z, :], LK).then_inc(a_tps, 1)

            def a_project(b, z):
                pe.wait_ge(a_xc, b + 1)
                if not isinstance(b, int) or b >= 1:
                    pe.wait_ge(a_k, b)
                    pe.wait_ge(a_v, b)
                nc.tensor.matmul(psum[:, 1, 0:LQ], w4T[:, 0, :], xc[:, z, 0:LQ], start=True, stop=True)
                nc.tensor.matmul(psum[:, 1, LQ:LQ + LK], w4T[:, 1, :], xc[:, z, LQ:LQ + LK], start=True, stop=True)
                nc.tensor.matmul(psum[0:LK, 2, 0:D], xc[:, z, LQ:LQ + LK], w4T[:, 2, :], start=True, stop=True
                                 ).then_inc(a_qkv, 1)

            def a_scores(half):
                def run(b, z):
                    pe.wait_ge(a_q, b + 1)
                    pe.wait_ge(a_kexp, b + 1)
                    if not isinstance(b, int) or b >= 1:
                        pe.wait_ge(a_exp, b * 2 + half - 1)
                    for j in range(2):
                        h = half * HALF0 + 4 * j
                        m = nc.tensor.matmul(psum[:, 3 + 2 * half + j, 0:4 * LK], qs[:, z, :],
                                             kexp[:, z, h:h + 4, :].rearrange("p h k -> p (h k)"), start=True, stop=True)
                    m.then_inc(a_s, 1)
                return run

            software_pipeline(pe, [(3, a_scores(0)), (1, a_turn), (3, a_scores(1)), (1, a_project)], peel=6)

            pe.wait_ge(ld_w, 16 * N_W)
            pe.wait_ge(a_exp, 2 * NB)
            pe.wait_ge(a_xc, NB)
            pe.wait_ge(a_k, NB)
            pe.wait_ge(a_v, NB)
            for g, (_, tiles) in enumerate(weight_groups()):
                if g >= RING_W:
                    pe.wait_ge(wt_sb[g % 2], (g - RING_W) // 2 + 1)
                if g == WC_GROUPS[-1] + 3:
                    for which in range(2):
                        pe.wait_ge(wt_sb[which], WC_GROUPS[-1] // 2 + 1)
                for i, ops in enumerate(tiles):
                    dst = psum[:, g % RING_W, i * D:(i + 1) * D]
                    m = turn(dst, ops[1], P) if ops[0] == "turn" else \
                        nc.tensor.matmul(dst, ops[1], ops[2], start=True, stop=True)
                m.then_inc(wt_ps, 1)
            pe.wait_ge(consts_set, 5)
            turn(psum[:, 4, 0:NE], nat0[0:NE, 4, :], NE)
            turn(psum[0:3, 4, 8:8 + DH0], wsm[0:DH0, 0:3], DH0)
            turn(psum[0:DH0, 4, 128:128 + DH0], wsm[0:DH0, 3:3 + DH0], DH0)
            nc.tensor.matmul(psum[0:DH0, 4, 256:256 + P], wsm[0:1, 3 + DH0:3 + 2 * DH0], ones[0:1, :],
                             start=True, stop=True)
            for h in range(H1):
                nc.tensor.matmul(psum[:, 4, 400 + h:401 + h], l1N[:, 1, h, :], bqk1[:, 0, h:h + 1], start=True, stop=True)
                m = nc.tensor.matmul(psum[:, 4, 408 + h:409 + h], l1N[:, 0, h, :], bqk1[:, 1, h:h + 1],
                                     start=True, stop=True)
            m.then_inc(m_pe, 1)
            pe.wait_ge(m_dve, 7)
            for c in range(3):
                nc.tensor.matmul(psum[:, 5, c * DH0:(c + 1) * DH0], sel[0:3, c, :], w1T[:, :], start=True, stop=True)
            nc.tensor.matmul(psum[:, 5, 200:208], ones[:, :], small[:, 7, 0:H1], start=True, stop=True)
            nc.tensor.matmul(psum[0:1, 5, 256:256 + D], ones[0:1, 0:1], bc1[:, :], start=True, stop=False)
            for h in range(H1):
                m = nc.tensor.matmul(psum[0:1, 5, 256:256 + D], bqk1[:, 2, h:h + 1], wcT[:, h, :],
                                     start=False, stop=(h == H1 - 1))
            m.then_inc(m_pe, 1)

            pe.wait_ge(m_dve, 15)
            for c, feature in enumerate((small[:, 4, :], rowneg[:, :], small[:, 2, :])):
                m = nc.tensor.matmul(psum[0:DH0, 4, 0:BH], w1f[:, c, :], feature, start=(c == 0), stop=(c == 2))
            m.then_inc(m_pe, 3)
            pe.wait_ge(m_act, 1)
            nc.tensor.matmul(psum[0:DH0, 5, 0:BH], w2T[:, :], small[0:DH0, 6, :], start=True, stop=True).then_inc(m_pe, 1)
            pe.wait_ge(m_act, 2)
            nc.tensor.matmul(psum[:, 4, 256:512], w3c[:, :], small[0:DH0, 7, :], start=True, stop=True).then_inc(m_pe, 1)
            pe.wait_ge(m_dve, 18)
            for half in range(2):
                m = turn(psum[:, 5, half * P:(half + 1) * P], small[:, 2, half * P:(half + 1) * P], P)
            m.then_inc(m_pe, 1)

            def tail_turn(ph):
                s = tails[ph]

                def run(b, z):
                    pe.wait_ge(s["xr" if ph == "b" else "xn"], b + 1)
                    if not isinstance(b, int) or b >= 1:
                        pe.wait_ge(s["ev"], b)
                    if ph == "d":
                        pe.wait_ge(d_x, min(b + 2, NB) if isinstance(b, int) else b + 2)
                    turn(tail_ps, (xr if ph == "b" else xn)[:, z, :], P).then_inc(s["tp"], 1)
                return run

            def tail_logits(ph, dst, weights):
                s = tails[ph]

                def run(b, z):
                    pe.wait_ge(s["ev"], b + 1)
                    nc.tensor.matmul(dst[:, b, :], xnT[:, z, :], weights, start=True, stop=True).then_inc(s["lg"], 1)
                return run

            def b_scores(half):
                def run(b, z):
                    pe.wait_ge(b_qexp, b * 2 + half + 1)
                    pe.wait_ge(b_kt, b + 1)
                    pe.wait_ge(ld_m[z], (b - z + 2) * 8)
                    if not isinstance(b, int) or b >= 1:
                        pe.wait_ge(b_exp, b * 2 + half - 1)
                    for j in range(2):
                        h = half * HALF0 + 4 * j
                        dst = psum[0:LK, 2 * half + j, :]
                        nc.tensor.matmul(dst, ktS[:, z, :], qexp[:, z, h:h + 4, :].rearrange("p h q -> p (h q)"),
                                         start=True, stop=False)
                        m = nc.tensor.matmul(dst, onesb[:, :], mrow[:, z, h * LQ:(h + 4) * LQ], start=False, stop=True)
                    m.then_inc(b_s, 1)
                return run

            def b_output(b, z):
                pe.wait_ge(b_exp, b * 2 + 2)
                pe.wait_ge(b_v, b + 1)
                if not isinstance(b, int) or b >= 1:
                    pe.wait_ge(b_oT, b)
                for c, pad in ((0, None), (1, opad)):
                    for g in range(4):
                        for i in range(4):
                            w = vpad[:, z, g, 32 * i:32 * i + 32] if pad is None else pad[:, 32 * i:32 * i + 32]
                            m = nc.tensor.matmul(psum[32 * g:32 * g + 32, 4, c * LQ:(c + 1) * LQ], w,
                                                 probT[:, z, 4 * g + i, :], start=(i == 0), stop=(i == 3))
                m.then_inc(b_od, 1)

            def b_project(b, z):
                pe.wait_ge(b_oT, b + 1)
                if not isinstance(b, int) or b >= 1:
                    pe.wait_ge(b_x1, b)
                nc.tensor.matmul(psum[:, 5, 0:D], oT[:, z, :], w4T[:, 3, :], start=True, stop=False)
                nc.tensor.matmul(psum[:, 5, 0:D], ones[0:1, :], bo0[:, :], start=False, stop=True).then_inc(b_y, 1)

            pe.wait_ge(m_dve, 22)
            software_pipeline(pe, [(5, tail_turn("b")), (1, b_scores(0)), (3, b_project), (2, b_output),
                                   (5, tail_logits("b", logits0, routerT)), (1, b_scores(1))], peel=8)

            def c_up_project(b, e):
                u = b * NE + e
                if not isinstance(u, int) or u >= 2:
                    pe.wait_ge(c_h, u - 1)
                for i in range(UP_TILES):
                    m = nc.tensor.matmul(psum[:, e % 2, i * LQ:(i + 1) * LQ], upT[:, e * UP_TILES + i, :], xT[:, b, :],
                                         start=True, stop=True)
                m.then_inc(c_up, 1)

            def c_down_project(b, e):
                u = b * NE + e
                pe.wait_ge(c_h, u + 1)
                if not isinstance(u, int) or u >= 2:
                    pe.wait_ge(c_acc, u - 1)
                for i in range(DN_TILES):
                    m = nc.tensor.matmul(psum[:, 2 + e % 2, 0:D], hT[:, e % 2, i * LQ:(i + 1) * LQ],
                                         dnT[:, e * DN_TILES + i, :], start=(i == 0), stop=(i == DN_TILES - 1))
                m.then_inc(c_dn, 1)

            def c_rest(b, z):
                for e in range(1, NE):
                    c_up_project(b, e)
                    c_down_project(b, e - 1)

            pe.wait_ge(tails["b"]["keep"], NB)
            software_pipeline(pe, [(0, lambda b, z: c_up_project(b, 0)), (1, lambda b, z: c_down_project(b, NE - 1)),
                                   (3, tail_turn("c")), (0, c_rest), (3, tail_logits("c", u1, uvec))], peel=6)

            def d_queries(b, z):
                if not isinstance(b, int) or b >= 1:
                    pe.wait_ge(d_q2, b)
                for h in range(H1):
                    m = nc.tensor.matmul(psum[:, h // 4, (h % 4) * LQ:(h % 4 + 1) * LQ], qk1[:, h, :], xT[:, b, :],
                                         start=True, stop=True)
                m.then_inc(d_q, 1)

            def d_scores(b, z):
                pe.wait_ge(d_q2, b + 1)
                if not isinstance(b, int) or b >= 1:
                    pe.wait_ge(d_sm, b)
                for h in range(H1):
                    m = nc.tensor.matmul(psum[:, 2 + h // 4, (h % 4) * LK:(h % 4 + 1) * LK], q2[:, z, h, :],
                                         ctxT[:, b, :], start=True, stop=True)
                m.then_inc(d_s, 1)

            def d_values(b, z):
                pe.wait_ge(d_cs, b + 1)
                if not isinstance(b, int) or b >= 1:
                    pe.wait_ge(d_aT, b)
                for a in range(2):
                    m = nc.tensor.matmul(psum[0:LK, 4 + a, :], cS[:, z, :],
                                         vo1[:, 4 * a:4 * a + 4, :].rearrange("p h d -> p (h d)"), start=True, stop=True)
                m.then_inc(d_vwp, 1)

            def d_turn(b, z):
                pe.wait_ge(d_a, b + 1)
                pe.wait_ge(d_vw, b + 1)
                for h in range(H1):
                    m = turn(psum[0:LK, 4 + h // 4, (h % 4) * LQ:(h % 4 + 1) * LQ], a1[:, z, h, :], P)
                m.then_inc(d_tp, 1)

            def d_output(b, z):
                pe.wait_ge(d_aT, b + 1)
                pe.wait_ge(d_vw, b + 1)
                if not isinstance(b, int) or b >= 1:
                    pe.wait_ge(d_x, b)
                reused(pe, tails["d"]["ev"], b)
                dst = psum[:, BANK_TAIL, 128:128 + D]
                nc.tensor.matmul(dst, ones[0:1, :], bout1[:, :], start=True, stop=False)
                for h in range(H1):
                    m = nc.tensor.matmul(dst, a1T[:, z, h, :], vw[:, z, h, :], start=False, stop=(h == H1 - 1))
                m.then_inc(d_y, 1)

            pe.wait_ge(tails["c"]["keep"], NB)
            software_pipeline(pe, [(1, d_scores), (6, tail_turn("d")), (3, d_values), (0, d_queries), (3, d_turn),
                                   (4, d_output), (6, tail_logits("d", logits1, router1))], peel=8)

            pe.wait_ge(r_dve, 2 * R_COUNT)
            turn(psum[:, BANK_TAIL, 0:P], gate.rearrange("p b e -> p (b e)"), P).then_inc(e_gt, 1)
            pe.wait_ge(e_gts, 1)
            pe.wait_ge(tails["d"]["keep"], NB)

            def e_hidden(b, z):
                reused(pe, e_g, b)
                for m_ in range(H1_TILES):
                    m = nc.tensor.matmul(psum[:, z, m_ * LQ:(m_ + 1) * LQ],
                                         ew1[:, 2 * m_:2 * m_ + 2, :].rearrange("p n f -> p (n f)"), xT[:, b, :],
                                         start=True, stop=True)
                m.then_inc(e_h, 1)

            def e_output(b, z):
                pe.wait_ge(e_g, b + 1)
                pe.wait_ge(e_b2, b + 1)
                reused(pe, e_acc, b, NE + 1)
                nc.tensor.matmul(psum[:, BANK_TAIL + z, 0:D], gateT[:, :], b2blk[:, z, :],
                                 start=True, stop=True)
                for e in range(NE):
                    rows = slice(F1 * (e % 2), F1 * (e % 2 + 1))
                    m = nc.tensor.matmul(psum[:, 2 + 2 * z + e % 2, (e // 2) * D:(e // 2 + 1) * D],
                                         h1[rows, z, e // 2, :], ew2[rows, e // 2, :], start=True, stop=True)
                m.then_inc(e_y, 1)

            software_pipeline(pe, [(0, e_hidden), (1, e_output)])


_INS = ['x', 'ctx_1024', 'L0_xattn_Wq', 'L0_xattn_bq', 'L0_xattn_Wk', 'L0_xattn_bk', 'L0_xattn_Wv', 'L0_xattn_bv',
        'L0_xattn_Wo', 'L0_xattn_bo', 'L0_xattn_w1', 'L0_xattn_b1', 'L0_xattn_w2', 'L0_xattn_b2', 'L0_xattn_w3',
        'L0_xattn_b3', 'L0_ffn_norm_scale', 'L0_ffn_w_router', 'L0_ffn_w_up', 'L0_ffn_w_down', 'L1_xattn_Wq',
        'L1_xattn_bq', 'L1_xattn_Wk', 'L1_xattn_bk', 'L1_xattn_Wv', 'L1_xattn_bv', 'L1_xattn_Wc', 'L1_xattn_bc',
        'L1_ffn_router_w', 'L1_ffn_router_b', 'L1_ffn_W1', 'L1_ffn_b1', 'L1_ffn_W2', 'L1_ffn_b2']


def kernel(**inputs):
    import numpy as _np
    import concourse.bacc as _bacc
    from concourse import mybir as _mybir
    from concourse.bass_utils import run_bass_kernel_spmd as _run

    nc = _bacc.Bacc("TRN2", target_bir_lowering=False, num_devices=1)
    cols, consts = shape_constants()
    arrays, t = {}, {}
    for name, value in [(n, inputs[n]) for n in _INS] + [("consts", consts)]:
        a = _np.ascontiguousarray(value)
        arrays[f"in_{name}_dram"] = a
        t[name] = nc.dram_tensor(f"in_{name}_dram", a.shape, _mybir.dt.from_np(a.dtype), kind="ExternalInput").ap()
    out = nc.dram_tensor("out_0_dram", (NB, LQ, D), F32, kind="ExternalOutput").ap()
    build(nc, cols, t, out)
    r = _run(nc, [arrays], core_ids=[0])
    return r.results[0]["out_0_dram"]
```

```python
import math
from contextlib import ExitStack

import numpy as np

import concourse.bass as bass
from concourse import mybir

F32 = mybir.dt.float32
F32R = mybir.dt.float32r
BF16 = mybir.dt.bfloat16
U32 = mybir.dt.uint32
ALU = mybir.AluOpType
ACT = mybir.ActivationFunctionType
AX_X = mybir.AxisListType.X

P = 128

NB, LQ, LK, D = 16, 128, 120, 128
H0, DK0 = 16, 8
DH0 = 64
NE = 8
HID0 = 256
H1, E1 = 8, 128
K1, DILATIONS = 64, (1, 2, 4, 8)
F1 = 64
LOG_T_MIN, LOG_T_MAX = math.log(0.1), math.log(10.0)
LN_EPS, RMS_EPS = 1e-5, 1e-6
NEG = -1.0e9
BH = NB * H0
X_GROUPS = 4
HALF0 = H0 // 2
UP_TILES = 2 * HID0 // P
DN_TILES = HID0 // P
H1_TILES = NE * F1 // P
SEQS = 4
GROUPS = NB // SEQS


def shape_constants():
    ident = np.eye(P, dtype=np.float32)
    part = np.arange(P)[:, None]
    headmask = (part // DK0 == np.arange(H0)[None, :]).astype(np.float32)
    mask = np.full((LQ, len(DILATIONS), LK), NEG, np.float64)
    for n, dil in enumerate(DILATIONS):
        count = np.zeros((LQ, LK))
        for l in range(LQ):
            for o in range(K1):
                at = l + (o - (K1 - 1) // 2) * dil
                if 0 <= at < LQ:
                    count[l, min(at, LK - 1)] += 1
        mask[:, n][count > 0] = np.log(count[count > 0])
    iota = np.tile(np.arange(NE, dtype=np.float32), (P, 1))
    sel = np.zeros((P, 3, P), np.float32)
    for c, w in enumerate((1.0 / (LQ * LK * math.sqrt(DK0)), -1.0 / LQ, 1.0 / LQ)):
        sel[c, c, :] = w
    expert_rows = ((part % NE)[:, :, None] == (2 * np.arange(H1_TILES)[:, None] + np.arange(P)[None, :] // F1)[None]
                   ).astype(np.float32)
    cols, at, parts = {}, 0, []
    for name, a in (("ident", ident), ("headmask", headmask), ("headscale", headmask / math.sqrt(DK0)),
                    ("iota", iota), ("sel", sel.reshape(P, -1)), ("window", mask.reshape(LQ, -1)),
                    ("expert_rows", expert_rows.reshape(P, -1))):
        cols[name] = (at, at + a.shape[1])
        at += a.shape[1]
        parts.append(a.astype(np.float32))
    return cols, np.ascontiguousarray(np.concatenate(parts, axis=1))


def software_pipeline(eng, stages, n=NB, peel=4):
    assert all(lag <= peel - 2 for lag, _ in stages) and (n - peel) % 2 == 0

    def step(b, parity):
        for lag, stage in stages:
            if not isinstance(b, int) or 0 <= b - lag < n:
                stage(b - lag, (parity - lag) % 2)

    for b in range(peel):
        step(b, b % 2)
    with eng.Fori(0, (n - peel) // 2) as i:
        for parity in range(2):
            step(i * 2 + (peel + parity), parity)
    for b in range(n, n + peel):
        step(b, b % 2)


def expert_slots(eng, slot, n=GROUPS):
    for g in range(2):
        for e in range(NE):
            slot(g, e)
    with eng.Fori(2, n) as g:
        for e in range(NE):
            slot(g, e)


def reused(eng, sem, b, per=1):
    if not isinstance(b, int) or b >= 2:
        eng.wait_ge(sem, (b - 1) * per)


def build(nc, cols, t, out):
    with ExitStack() as ctx:
        def sb(name, shape, dt=F32):
            return ctx.enter_context(nc.sbuf_tensor(name, shape, dt))[:]

        def shared(name, shape, parts):
            with nc.sbuf_tensor(name, shape, F32) as a:
                whole = a[:]
            return whole, [sb(*part) for part in parts]

        def sem(name):
            return ctx.enter_context(nc.semaphore(name))

        psum = ctx.enter_context(nc.psum_tensor("psum", [P, 8, 512], F32))
        BANK_KEEP, BANK_TAIL = 7, 6

        cst = sb("cst", [P, cols["window"][1]])
        ident = cst[:, slice(*cols["ident"])]
        headmask = cst[:, slice(*cols["headmask"])]
        headscale = cst[:, slice(*cols["headscale"])]
        window = cst[:, slice(*cols["window"])].rearrange("p (n k) -> p n k", n=len(DILATIONS))
        iota = cst[:, slice(*cols["iota"])]
        sel = cst[:, slice(*cols["sel"])].rearrange("p (c q) -> p c q", c=3)
        x = sb("x", [P, NB, D])
        ctxT = sb("ctxT", [P, NB, LK])
        qT = sb("qT", [P, NB, LQ])
        kT = sb("kT", [P, NB, LK])
        v0 = sb("v0", [LK, NB, D])
        xT, (x_hi,) = shared("xT", [P, NB, LQ], [("x_hi", [P, NB, LQ], F32R)])
        scored, (x_lo,) = shared("scored", [P, 8 * BH], [("x_lo", [P, NB, LQ], F32R)])
        gate = sb("gate", [P, NB, NE])
        bnout = scored[:, 0:6 * BH].rearrange("p (r s) -> p r s", s=6)
        rowneg = scored[:, 6 * BH:7 * BH]
        negmax = sb("negmax", [P, 2, H0])
        qsum = sb("qsum", [P, NB])
        ksum = sb("ksum", [P, NB])
        invt = scored[:, 7 * BH:8 * BH]
        invtT = sb("invtT", [P, NB])
        small = sb("small", [P, 8, BH])
        ones = sb("ones", [P, P])
        onesb = sb("onesb", [P, LK], BF16)
        w4T = sb("w4T", [P, 4, D])
        upT = sb("upT", [P, NE * UP_TILES, P])
        dnT = sb("dnT", [P, NE * DN_TILES, D])
        routerT = sb("routerT", [P, NE])
        w1f = sb("w1f", [P, 3, DH0])
        w1T = sb("w1T", [3, DH0])
        w2T = sb("w2T", [DH0, DH0])
        w3c = sb("w3c", [DH0, P])
        qk1 = sb("qk1", [P, H1, D])
        vo1 = sb("vo1", [P, H1, D])
        cvec = sb("cvec", [P, H1])
        uvec = sb("uvec", [P, H1])
        ubias = sb("ubias", [P, H1])
        bout1 = sb("bout1", [1, D])
        router1 = sb("router1", [P, NE])
        ew1 = sb("ew1", [P, NE, F1])
        ew2 = sb("ew2", [P, H1_TILES, D])
        b2rows = sb("b2rows", [P, D])
        gateT = sb("gateT", [P, P])
        vecs = sb("vecs", [P, 16])
        bq0, bk0, b1c, b2c, b3c, nscale, bv0 = (vecs[:, i:i + 1] for i in range(7))
        b1e = vecs[:, 7:7 + H1_TILES]
        bo0 = sb("bo0", [1, D])
        bout0 = sb("bout0", [1, D])
        bc1 = sb("bc1", [1, D])
        rb1 = sb("rb1", [P, NE])
        bqk1 = sb("bqk1", [P, 3, H1])
        bqk = sb("bqk", [P, H1])
        nat0 = sb("nat0", [P, 5, D])
        wsm = sb("wsm", [P, 3 + DH0 + DH0])
        eps = sb("eps", [P, 4])
        carried = sb("carried", [P, 8])
        bn6 = sb("bn6", [P, 2, 6])
        mv = sb("mv", [P, 2, 2])
        rstd = sb("rstd", [P, 2, 4])
        mean0 = sb("mean0", [P, NB, 2])
        rstd0 = sb("rstd0", [P, NB])
        xn = sb("xn", [P, 2, D])
        xnT = sb("xnT", [P, 2, LQ])
        work, (_, up_lo) = shared("work", [P, 13552], [("work_head", [P, 9456], F32),
                                                       ("up_lo", [P, NE * UP_TILES, P], F32R)])

        def area(at, n):
            return work[:, at:at + n]

        W_UP, W_DN, W_L1, W_C = 2048, 6144, 8192, 11264
        upN = area(W_UP, 4096).rearrange("p (t d) -> p t d", d=D)
        dnN = area(W_DN, 2048).rearrange("p (e h) -> p e h", e=NE)
        l1N = area(W_L1, 3072).rearrange("p (w h d) -> p w h d", w=3, h=H1)
        wcN = area(W_C, 1024).rearrange("p (h e) -> p h e", h=H1)
        wcT = area(W_C + 1024, 1024).rearrange("p (h o) -> p h o", h=H1)
        wa, (_, up_hi) = shared("wa", [P, 8688], [("wa_head", [P, 3328], F32),
                                                  ("up_hi", [P, NE * UP_TILES, P], F32R)])
        sb("wa_rest", [P, 8688 - 3328 - 4096])
        kexp = wa[:, 0:3840].rearrange("p (z h k) -> p z h k", z=2, h=H0)
        prob = wa[:, 3840:7680].rearrange("p (z h k) -> p z h k", z=2, h=H0)
        craw = wa[0:LK, 7680:7936].rearrange("p (z d) -> p z d", z=2)
        xc = wa[:, 7936:8432].rearrange("p (z c) -> p z c", z=2)
        qs = wa[:, 8432:8688].rearrange("p (z q) -> p z q", z=2)
        mrow = wa[:, 0:H0 * LQ].bitcast(BF16).rearrange("p (z c) -> p z c", z=2)
        vpad = wa[0:LK, 2048:3328].rearrange("p (z g c) -> p z g c", z=2, g=4)
        opad = sb("opad", [LK, 160])
        qexp = area(0, 4096).rearrange("p (z h q) -> p z h q", z=2, h=H0)
        probT = area(4096, 4096)[0:LK].rearrange("p (z h q) -> p z h q", z=2, h=H0)
        ktS = area(8192, 240).rearrange("p (z k) -> p z k", z=2)
        qsc = area(8432, 256).rearrange("p (z q) -> p z q", z=2)
        rden = area(8688, 256).rearrange("p (z q) -> p z q", z=2)
        oT = area(8944, 256).rearrange("p (z q) -> p z q", z=2)
        xr = area(9200, 256).rearrange("p (z d) -> p z d", z=2)
        mparts = sb("mparts", [P, 2, 2, LQ], BF16)
        silu = area(0, 1024).rearrange("p (j c) -> p j c", j=DN_TILES)
        hT = area(1024, 2048).rearrange("p (z j c) -> p z j c", z=2, j=DN_TILES)
        q2 = area(1024, 2048).rearrange("p (z h q) -> p z h q", z=2, h=H1)
        s1 = area(3072, 1920).rearrange("p (z h k) -> p z h k", z=2, h=H1)
        e1 = area(4992, 1920).rearrange("p (z h k) -> p z h k", z=2, h=H1)
        a1 = area(6912, 1920).rearrange("p (z h k) -> p z h k", z=2, h=H1)
        a1T = area(8832, 2048)[0:LK].rearrange("p (z h q) -> p z h q", z=2, h=H1)
        vw = area(10880, 2048)[0:LK].rearrange("p (z h d) -> p z h d", z=2, h=H1)
        cS = area(12928, 240).rearrange("p (z k) -> p z k", z=2)
        d8 = sb("d8", [P, 2, 6, H1])
        h1 = wa[:, 0:1024].rearrange("p (z m q) -> p z m q", z=2, m=H1_TILES)
        gm = wa[:, 1024:1280].rearrange("p (z d) -> p z d", z=2)
        yacc = wa[:, 1280:1536].rearrange("p (z d) -> p z d", z=2)
        hg = wa[:, 1536:2560].rearrange("p (z m q) -> p z m q", z=2, m=H1_TILES)
        expert_rows = wa[:, 7424:7936].rearrange("p (m c) -> p m c", m=H1_TILES)
        lg = small[:, 1, 0:P].rearrange("p (b e) -> p b e", b=NB)
        mx8 = small[:, 1, P:2 * P].rearrange("p (b e) -> p b e", b=NB)
        ix8 = sb("ix8", [P, NB, 8], U32)
        rt = sb("rt", [P, 6, NB])
        u1s = small[:, 2, 0:P].rearrange("p (b h) -> p b h", b=NB)
        oh = small[:, 0, :].rearrange("p (j b e) -> p j b e", j=2, b=NB)
        mscratch = nc.dram_tensor("mscratch", (2, NB, H0, LQ), BF16, kind="Internal").ap()

        def banks(a, n, parts=P):
            return psum[0:parts, a:a + n, :]

        keep = psum[:, BANK_KEEP, :]
        logits0 = keep[:, 0:128].rearrange("p (b e) -> p b e", b=NB)
        u1 = keep[:, 128:256].rearrange("p (b e) -> p b e", b=NB)
        logits1 = keep[:, 256:384].rearrange("p (b e) -> p b e", b=NB)
        tail_ps = psum[:, BANK_TAIL, 0:LQ]

        ld_first, ld_w, ld_late, ld_ctx = sem("ld_first"), sem("ld_w"), sem("ld_late"), [sem("ld_ctx0"), sem("ld_ctx1")]
        ld_m = [sem("ld_m0"), sem("ld_m1")]
        ld_x = [sem(f"ld_x{g}") for g in range(X_GROUPS)]
        consts_set = sem("consts_set")
        w0_ps, w0_sb = sem("w0_ps"), sem("w0_sb")
        wt_ps, wt_act, wt_dve = sem("wt_ps"), sem("wt_act"), sem("wt_dve")
        f_dve, f_pe, mlp_pe, mlp_act, temp_dve, l1_pe, l1_dve = (
            sem(n) for n in ("f_dve", "f_pe", "mlp_pe", "mlp_act", "temp_dve", "l1_pe", "l1_dve"))
        ln0_st, ln0_ag, ln0_eps, ln0_r = sem("ln0_st"), sem("ln0_ag"), sem("ln0_eps"), sem("ln0_r")
        a_xn, a_tps, a_xc, a_ctx, a_qkv, a_q, a_k, a_v, a_kexp, a_qkeep = (
            sem("a_" + n) for n in ("xn", "tps", "xc", "ctx", "qkv", "q", "k", "v", "kexp", "qkeep"))
        a_nkeep = sem("a_nkeep")
        a_s, a_max, a_neg, a_exp, a_bn = (sem("a_" + n) for n in ("s", "max", "neg", "exp", "bn"))
        m_store = sem("m_store")
        b_kt, b_v, b_qsc, b_qexp, b_s, b_exp, b_od, b_rden, b_oT, b_y, b_x1, b_x = (
            sem("b_" + n) for n in ("kt", "v", "qsc", "qexp", "s", "exp", "od", "rden", "oT", "y", "x1", "x"))
        tails = {ph: {n: sem(f"{ph}t_{n}") for n in ("bn", "ag", "pool", "r", "xn", "xr", "tp", "ev", "lg", "keep")}
                 for ph in "bcd"}
        mrow_zero = sem("mrow_zero")
        r_dve, r_act, gates_set = sem("r_dve"), sem("r_act"), sem("gates_set")
        b_hi, b_lo, b_xhi, c_gate = sem("b_hi"), sem("b_lo"), sem("b_xhi"), sem("c_gate")
        c_up, c_silu, c_h, c_dn, c_acc = (sem("c_" + n) for n in ("up", "silu", "h", "dn", "acc"))
        d_cs, d_q, d_q2, d_s, d_sm, d_max, d_mu, d_sh, d_exp, d_rs, d_a, d_tp, d_aT, d_vwp, d_vw, d_y, d_x = (
            sem("d_" + n) for n in ("cs", "q", "q2", "s", "sm", "max", "mu", "sh", "exp", "rs", "a", "tp",
                                    "aT", "vwp", "vw", "y", "x"))
        d_u = sem("d_u")
        e_gt, e_gts, e_h, e_g, e_gm, e_gps, e_hg, e_y, e_acc = (
            sem("e_" + n) for n in ("gt", "gts", "h", "g", "gm", "gps", "hg", "y", "acc"))
        e_out = [sem("e_out0"), sem("e_out1")]

        N_FIRST, N_W, N_LATE = 13, 15, 8 + NB
        block = ctx.enter_context(nc.Block())

        @block.sync
        def _(sp):
            first = [
                (cst[:, 0:cols["sel"][1]], t["consts"][:, 0:cols["sel"][1]]),
                (nat0[:, 0, :], t["L0_xattn_Wq"]),
                (nat0[:, 1, :], t["L0_xattn_Wk"]),
                (nat0[:, 2, :], t["L0_xattn_Wv"]),
                (nat0[:, 3, :], t["L0_xattn_Wo"]),
                (bq0, t["L0_xattn_bq"].rearrange("(p c) -> p c", c=1)),
                (bk0, t["L0_xattn_bk"].rearrange("(p c) -> p c", c=1)),
                (bv0, t["L0_xattn_bv"].rearrange("(p c) -> p c", c=1)),
                (bo0[:, :], t["L0_xattn_bo"].rearrange("(a d) -> a d", a=1)),
                (wsm[0:DH0, 0:3], t["L0_xattn_w1"]),
                (wsm[0:DH0, 3:3 + DH0], t["L0_xattn_w2"]),
                (wsm[0:1, 3 + DH0:3 + 2 * DH0], t["L0_xattn_w3"]),
                (nat0[0:NE, 4, :], t["L0_ffn_w_router"]),
            ]
            assert len(first) == N_FIRST
            for dst, src in first:
                sp.dma_start(dst, src, allow_slow_non_contiguous=True).then_inc(ld_first, 16)

            def load_ctx(b, z):
                reused(sp, a_tps, b)
                sp.dma_start(craw[:, z, :], t["ctx_1024"][b]).then_inc(ld_ctx[z], 16)

            for b in range(2):
                load_ctx(b, b)
            small_loads = [
                (b1c[0:DH0], t["L0_xattn_b1"].rearrange("(p c) -> p c", c=1)),
                (b2c[0:DH0], t["L0_xattn_b2"].rearrange("(p c) -> p c", c=1)),
                (b3c, t["L0_xattn_b3"].rearrange("(a c) -> a c", a=1).to_broadcast([P, 1])),
                (nscale, t["L0_ffn_norm_scale"].rearrange("(p c) -> p c", c=1)),
                (bqk1[:, 0], t["L1_xattn_bq"].rearrange("h e -> e h")),
                (bqk1[:, 1], t["L1_xattn_bk"].rearrange("h e -> e h")),
                (bqk1[:, 2], t["L1_xattn_bv"].rearrange("h e -> e h")),
                (bc1[:, :], t["L1_xattn_bc"].rearrange("(a d) -> a d", a=1)),
            ]
            up_rows = t["L0_ffn_w_up"].rearrange("e (t p) d -> p (e t) d", p=P)
            large_loads = [
                (upN[:, 0:16], up_rows[:, 0:16]),
                (upN[:, 16:32], up_rows[:, 16:32]),
                (dnN, t["L0_ffn_w_down"].rearrange("e p h -> p e h")),
                (l1N[:, 0], t["L1_xattn_Wq"].rearrange("h e d -> e h d")),
                (l1N[:, 1], t["L1_xattn_Wk"].rearrange("h e d -> e h d")),
                (l1N[:, 2], t["L1_xattn_Wv"].rearrange("h e d -> e h d")),
                (wcN, t["L1_xattn_Wc"].rearrange("o (h e) -> o h e", h=H1)),
            ]
            assert len(small_loads) + len(large_loads) == N_W
            for dst, src in small_loads:
                sp.dma_start(dst, src, allow_slow_non_contiguous=True).then_inc(ld_w, 16)
            for b in range(2, 4):
                for dst, src in large_loads[2 * (b - 2):2 * (b - 1)]:
                    sp.dma_start(dst, src).then_inc(ld_w, 16)
                load_ctx(b, b % 2)
            for dst, src in large_loads[4:]:
                sp.dma_start(dst, src).then_inc(ld_w, 16)
            with sp.Fori(2, NB // 2) as i:
                for z in range(2):
                    load_ctx(i * 2 + z, z)

            late = [
                (cst[:, slice(*cols["window"])], t["consts"][:, slice(*cols["window"])]),
                (router1[:, :], t["L1_ffn_router_w"]),
                (rb1[:, :], t["L1_ffn_router_b"].rearrange("(a d) -> a d", a=1).to_broadcast([P, NE])),
                (ew1[:, :, :], t["L1_ffn_W1"].rearrange("n d e -> d n e")),
                (ew2[0:F1], t["L1_ffn_W2"].rearrange("(m j) f d -> j f m d", j=2)[0]),
                (ew2[F1:P], t["L1_ffn_W2"].rearrange("(m j) f d -> j f m d", j=2)[1]),
                (b1e[0:F1], t["L1_ffn_b1"].rearrange("(m j) f -> j f m", j=2)[0]),
                (b1e[F1:P], t["L1_ffn_b1"].rearrange("(m j) f -> j f m", j=2)[1]),
            ] + [(b2rows[NE * b:NE * (b + 1), :], t["L1_ffn_b2"]) for b in range(NB)]
            assert len(late) == N_LATE
            for dst, src in late:
                sp.dma_start(dst, src, allow_slow_non_contiguous=True).then_inc(ld_late, 16)

            sp.wait_ge(m_store, 32)
            sp.dma_start(expert_rows.rearrange("p m c -> p (m c)"), t["consts"][:, slice(*cols["expert_rows"])]
                         ).then_inc(ld_late, 16)
            sp.wait_ge(mrow_zero, 1)

            def load_m(b, z):
                reused(sp, b_s, b, 2)
                sp.dma_start(mrow[0:2, z, :], mscratch[:, b].rearrange("c h q -> c (h q)")).then_inc(ld_m[z], 16)

            software_pipeline(sp, [(0, load_m)])

            def store(b, z):
                sp.wait_ge(e_acc, b + 1)
                sp.dma_start(out[b], yacc[:, z, :]).then_inc(e_out[z], 16)

            software_pipeline(sp, [(0, store)])
            for z in range(2):
                sp.wait_ge(e_out[z], 16 * NB // 2)

        def weight_groups():
            groups = []
            for g in range(NE * UP_TILES // 4):
                groups.append((upT[:, 4 * g:4 * g + 4, :], [("turn", upN[:, 4 * g + i, :]) for i in range(4)]))
            for g in range(NE * DN_TILES // 4):
                groups.append((dnT[:, 4 * g:4 * g + 4, :],
                               [("turn", dnN[:, 2 * g + i // 2, (i % 2) * P:(i % 2 + 1) * P]) for i in range(4)]))
            for g in range(H1 // 4):
                groups.append((wcT[:, 4 * g:4 * g + 4, :], [("turn", wcN[:, 4 * g + i, :]) for i in range(4)]))
            for g in range(H1 // 4):
                groups.append((qk1[:, 4 * g:4 * g + 4, :],
                               [("prod", l1N[:, 0, 4 * g + i, :], l1N[:, 1, 4 * g + i, :]) for i in range(4)]))
            for g in range(H1 // 4):
                groups.append((vo1[:, 4 * g:4 * g + 4, :],
                               [("prod", l1N[:, 2, 4 * g + i, :], wcT[:, 4 * g + i, :]) for i in range(4)]))
            return groups

        WC_GROUPS = range(12, 14)
        N_GROUPS = 18
        RING_W = 4
        ACT_GROUPS = 9

        def weight_copies(ns, eng, groups):
            for g in groups:
                eng.wait_ge(wt_ps, g + 1)
                src = psum[:, g % RING_W, :].rearrange("p (i d) -> p i d", d=D)
                if g < ACT_GROUPS:
                    ns.copy(weight_groups()[g][0], src).then_inc(wt_act, 1)
                else:
                    ns.tensor_copy(weight_groups()[g][0], src).then_inc(wt_dve, 1)

        def group_copied(eng, g):
            if g < ACT_GROUPS:
                eng.wait_ge(wt_act, g + 1)
            else:
                eng.wait_ge(wt_dve, g - ACT_GROUPS + 1)

        T_CLIPPED, T_SCALED, T_PARTS = 2, 3, 7
        ROUTE_SLOT = 1
        STATS_SLOTS, NORM_SLOTS, TURN_SLOTS, LOGITS_SLOTS = (range(a, a + SEQS) for a in (1, 2, 3, 4))
        R_DIFF, R_COUNT = 4, 13

        @block.scalar
        def _(act):
            for g in range(X_GROUPS):
                act.dma_start(x[:, 4 * g:4 * g + 4, :], t["x"][4 * g:4 * g + 4].rearrange("b t d -> t b d")
                              ).then_inc(ld_x[g], 16)

            act.wait_ge(ld_first, 16 * N_FIRST)

            def a_project(b, z):
                act.wait_ge(a_qkv, b + 1)
                reused(act, a_s, b, 2)
                reused(act, a_qkeep, b)
                nc.scalar.activation(qs[:, z, :], psum[:, 1, 0:LQ], ACT.Identity, bias=bq0,
                                     accum_out=qsum[:, bass.ds(b, 1)]).then_inc(a_q, 1)
                nc.scalar.activation(kT[:, b, :], psum[:, 1, LQ:LQ + LK], ACT.Identity, bias=bk0,
                                     accum_out=ksum[:, bass.ds(b, 1)]).then_inc(a_k, 1)

            def a_turned(b, z):
                act.wait_ge(a_tps, b + 1)
                reused(act, a_qkv, b)
                reused(act, a_ctx, b)
                nc.scalar.copy(xc[:, z, :], psum[:, 0, 0:LQ + LK]).then_inc(a_xc, 1)

            def a_values(b, z):
                act.wait_ge(a_qkv, b + 1)
                nc.scalar.copy(v0[:, b, :], psum[0:LK, 2, 0:D]).then_inc(a_v, 1)

            def a_softmax(half):
                def run(b, z):
                    act.wait_ge(a_neg, b * 2 + half + 1)
                    if half == 0:
                        reused(act, a_bn, b, 2)
                    for h in range(HALF0):
                        hh = half * HALF0 + h
                        e = nc.scalar.activation(
                            prob[:, z, hh, :], psum[:, 3 + 2 * half + h // 4, (h % 4) * LK:(h % 4 + 1) * LK],
                            ACT.Exp, bias=negmax[:, z, hh:hh + 1])
                    e.then_inc(a_exp, 1)
                return run

            software_pipeline(act, [(3, a_softmax(0)), (1, a_turned), (3, a_softmax(1)), (1, a_project), (1, a_values)],
                              peel=6)

            weight_copies(nc.scalar, act, range(ACT_GROUPS))

            act.wait_ge(ld_w, 16 * N_W)
            act.wait_ge(mlp_pe, 1)
            nc.scalar.activation(small[0:DH0, 6, :], psum[0:DH0, 4, 0:BH], ACT.Gelu, bias=b1c[0:DH0]
                                 ).then_inc(mlp_act, 1)
            act.wait_ge(mlp_pe, 2)
            nc.scalar.activation(small[0:DH0, 7, :], psum[0:DH0, 5, 0:BH], ACT.Gelu, bias=b2c[0:DH0]
                                 ).then_inc(mlp_act, 1)
            act.wait_ge(temp_dve, T_CLIPPED)
            nc.scalar.activation(invt[:, :], small[:, 1, :], ACT.Exp, scale=-1.0).then_inc(mlp_act, 1)
            act.wait_ge(temp_dve, T_PARTS)
            for half in range(2):
                act.dma_start(mscratch[:, 8 * half:8 * half + 8].rearrange("c b h q -> (b h) c q"),
                              mparts[:, half, :, :]).then_inc(m_store, 16)

            def b_softmax(half):
                def run(b, z):
                    act.wait_ge(b_s, b * 2 + half + 1)
                    if half == 0:
                        reused(act, b_od, b)
                    nc.scalar.activation(
                        probT[:, z, half * HALF0:(half + 1) * HALF0, :].rearrange("p h q -> p (h q)"),
                        psum[0:LK, 2 * half:2 * half + 2, :].rearrange("p a c -> p (a c)"), ACT.Exp
                    ).then_inc(b_exp, 1)
                return run

            def tail_evict(ph):
                s = tails[ph]

                def run(b, z):
                    act.wait_ge(s["tp"], b + 1)
                    reused(act, s["keep"], b)
                    reused(act, s["lg"], b)
                    if ph == "b":
                        nc.scalar.mul(xnT[:, z, :], tail_ps, nscale).then_inc(s["ev"], 1)
                    else:
                        nc.scalar.copy(xnT[:, z, :], tail_ps).then_inc(s["ev"], 1)
                return run

            def b_split(b, z):
                tiles = bass.ds(b * 2, 2)
                nc.scalar.copy(up_hi[:, tiles, :], upT[:, tiles, :]).then_inc(b_hi, 1)

            act.wait_ge(l1_pe, 2)
            act.wait_ge(wt_dve, N_GROUPS - ACT_GROUPS)
            software_pipeline(act, [(5, tail_evict("b")), (1, b_softmax(0)), (1, b_softmax(1)), (1, b_split)], peel=8)

            def route_exp(n):
                act.wait_ge(r_dve, R_DIFF + n * R_COUNT)
                nc.scalar.activation(rt[:, 1, :], rt[:, 0, :], ACT.Exp).then_inc(r_act, 1)

            def c_slot(g, e):
                for j in range(DN_TILES):
                    v = (g * NE + e) * DN_TILES + j
                    act.wait_ge(c_gate, v + 1)
                    nc.scalar.activation(silu[:, j, :], psum[:, 2 * j + 1, :], ACT.Silu).then_inc(c_silu, 1)
                if isinstance(g, int) and g == 0:
                    if e == ROUTE_SLOT:
                        route_exp(0)
                elif e in TURN_SLOTS:
                    sq = e - TURN_SLOTS[0]
                    tail_evict("c")((g - 1) * SEQS + sq, sq % 2)

            expert_slots(act, c_slot)
            for sq in range(SEQS):
                tail_evict("c")((GROUPS - 1) * SEQS + sq, sq % 2)

            def d_vw_copy(b, z):
                act.wait_ge(d_vwp, b + 1)
                reused(act, d_y, b)
                nc.scalar.copy(vw[:, z].rearrange("p h d -> p (h d)"),
                               psum[0:LK, 4:6, :].rearrange("p a c -> p (a c)")).then_inc(d_vw, 1)

            def d_softmax(b, z):
                act.wait_ge(d_sh, b + 1)
                reused(act, d_a, b)
                for h in range(H1):
                    e = nc.scalar.activation(e1[:, z, h, :], s1[:, z, h, :], ACT.Exp, bias=d8[:, z, 3, h:h + 1],
                                             accum_out=d8[:, z, 4, h:h + 1])
                e.then_inc(d_exp, 1)

            def d_aT_copy(b, z):
                act.wait_ge(d_tp, b + 1)
                nc.scalar.copy(a1T[:, z].rearrange("p h q -> p (h q)"),
                               psum[0:LK, 4:6, :].rearrange("p a c -> p (a c)")).then_inc(d_aT, 1)

            software_pipeline(act, [(6, tail_evict("d")), (3, d_vw_copy), (1, d_softmax), (3, d_aT_copy)], peel=8)
            route_exp(1)

            def e_gelu(b, z):
                act.wait_ge(e_h, b + 1)
                reused(act, e_hg, b)
                for m in range(H1_TILES):
                    g = nc.scalar.activation(h1[:, z, m, :], psum[:, z, m * LQ:(m + 1) * LQ], ACT.Gelu,
                                             bias=b1e[:, m:m + 1])
                g.then_inc(e_g, 1)

            software_pipeline(act, [(0, e_gelu)])

        @block.gpsimd
        def _(pool):
            nc.gpsimd.memset(eps[:, 0:1], -0.5)
            nc.gpsimd.memset(eps[:, 1:2], LN_EPS)
            nc.gpsimd.memset(eps[:, 2:3], RMS_EPS).then_inc(consts_set, 1)
            nc.gpsimd.memset(onesb[:, :], 0.0).then_inc(consts_set, 1)
            nc.gpsimd.memset(opad[:, :], 0.0).then_inc(consts_set, 1)
            pool.wait_ge(consts_set, 4)
            nc.gpsimd.memset(onesb[0:2, :], 1.0)
            nc.gpsimd.memset(opad.rearrange("p (i c) -> p i c", c=40)[:, :, 0:DK0], 1.0).then_inc(consts_set, 1)
            half_power = eps[:, 0:1]

            for g in range(X_GROUPS):
                of = slice(4 * g, 4 * g + 4)
                pool.wait_ge(ln0_ag, g + 1)
                nc.gpsimd.tensor_scalar(rstd0[:, of], mean0[:, of, 1], LN_EPS, None, ALU.add).then_inc(ln0_eps, 1)
                pool.wait_ge(ln0_eps, g + 1)
                nc.gpsimd.tensor_tensor(rstd0[:, of], rstd0[:, of], half_power.to_broadcast([P, 4]), ALU.pow
                                        ).then_inc(ln0_r, 1)

            pool.wait_ge(ld_first, 16 * N_FIRST)

            def a_keep_context(b, z):
                pool.wait_ge(a_xc, b + 1)
                nc.gpsimd.tensor_copy(ctxT[:, b, :], xc[:, z, LQ:LQ + LK]).then_inc(a_ctx, 1)

            def a_keep(b, z):
                pool.wait_ge(a_q, b + 1)
                nc.gpsimd.tensor_copy(qT[:, b, :], qs[:, z, :]).then_inc(a_qkeep, 1)

            def a_keep_max(b, z):
                pool.wait_ge(a_neg, b * 2 + 2)
                nc.gpsimd.tensor_copy(rowneg[:, bass.ds(b * H0, H0)], negmax[:, z, :]).then_inc(a_nkeep, 1)

            def a_expand(b, z):
                pool.wait_ge(a_k, b + 1)
                reused(pool, a_s, b, 2)
                nc.gpsimd.tensor_tensor(kexp[:, z], kT[:, b, :].unsqueeze(1).to_broadcast([P, H0, LK]),
                                        headscale.unsqueeze(2).to_broadcast([P, H0, LK]), ALU.mult
                                        ).then_inc(a_kexp, 1)

            software_pipeline(pool, [(1, a_keep_context), (1, a_expand), (1, a_keep), (3, a_keep_max)], peel=6)

            def tail_rstd(ph):
                s, per = tails[ph], 6 if ph == "b" else 2

                def run(b, z):
                    pool.wait_ge(s["ag"], b + 1)
                    reused(pool, s["xr" if ph == "b" else "xn"], b)
                    r = [rstd[:, z, i:i + 1] for i in range(4)]
                    var = mv[:, z, 1:2]
                    nc.gpsimd.tensor_tensor(r[0], var, eps[:, 1:2], ALU.add).then_inc(s["pool"], 1)
                    pool.wait_ge(s["pool"], b * per + 1)
                    nc.gpsimd.tensor_tensor(r[1], r[0], half_power, ALU.pow).then_inc(s["pool"], 1)
                    if ph == "b":
                        pool.wait_ge(s["pool"], b * per + 2)
                        nc.gpsimd.tensor_tensor(r[2], r[1], r[1], ALU.mult).then_inc(s["pool"], 1)
                        pool.wait_ge(s["pool"], b * per + 3)
                        nc.gpsimd.tensor_tensor(r[0], r[2], var, ALU.mult).then_inc(s["pool"], 1)
                        pool.wait_ge(s["pool"], b * per + 4)
                        nc.gpsimd.tensor_tensor(r[2], r[0], eps[:, 2:3], ALU.add).then_inc(s["pool"], 1)
                        pool.wait_ge(s["pool"], b * per + 5)
                        nc.gpsimd.tensor_tensor(r[3], r[2], half_power, ALU.pow).then_inc(s["pool"], 1)
                return run

            def tail_keep(ph):
                s = tails[ph]

                def run(b, z):
                    pool.wait_ge(s["ev"], b + 1)
                    if ph == "b":
                        nc.gpsimd.tensor_copy(x_hi[:, b, :], xnT[:, z, :]).then_inc(b_xhi, 1)
                        pool.wait_ge(b_xhi, b + 1)
                        nc.gpsimd.tensor_tensor(x_lo[:, b, :], xnT[:, z, :], x_hi[:, b, :].bitcast(F32), ALU.subtract
                                                ).then_inc(s["keep"], 1)
                    else:
                        nc.gpsimd.tensor_copy(xT[:, b, :], xnT[:, z, :]).then_inc(s["keep"], 1)
                return run

            def b_stage(b, z):
                reused(pool, b_s, b, 2)
                nc.gpsimd.tensor_copy(ktS[:, z, :], kT[:, b, :]).then_inc(b_kt, 1)
                reused(pool, b_od, b)
                nc.gpsimd.tensor_copy(
                    vpad[:, z].rearrange("p g (i c) -> p g i c", c=40)[:, :, :, 0:DK0],
                    v0[:, b, :].rearrange("p (g i j) -> p g i j", g=4, j=DK0)).then_inc(b_v, 1)

            pool.wait_ge(a_s, 2 * NB)
            pool.wait_ge(a_bn, 2 * NB)
            pool.wait_ge(a_xc, NB)
            nc.gpsimd.memset(wa[:, 0:H0 * LQ], 0.0).then_inc(mrow_zero, 1)
            nc.gpsimd.memset(vpad[:, :, :, :], 0.0).then_inc(consts_set, 1)
            pool.wait_ge(consts_set, 6)
            pool.wait_ge(l1_pe, 2)
            def b_split(b, z):
                tiles = bass.ds(b * 2, 2)
                pool.wait_ge(b_hi, b + 1)
                nc.gpsimd.tensor_tensor(up_lo[:, tiles, :], upT[:, tiles, :], up_hi[:, tiles, :].bitcast(F32), ALU.subtract
                                        ).then_inc(b_lo, 1)

            software_pipeline(pool, [(0, b_stage), (3, tail_rstd("b")), (2, b_split), (5, tail_keep("b"))], peel=8)

            def c_tails(g):
                for stage, sq in ((tail_rstd, 0), (tail_rstd, 1), (tail_rstd, 2), (tail_keep, 0), (tail_rstd, 3),
                                  (tail_keep, 1), (tail_keep, 2), (tail_keep, 3)):
                    stage("c")(g * SEQS + sq, sq % 2)

            c_tails(0)
            with pool.Fori(1, GROUPS) as g:
                c_tails(g)

            def d_stage(b, z):
                reused(pool, d_vwp, b)
                nc.gpsimd.tensor_copy(cS[:, z, :], ctxT[:, b, :]).then_inc(d_cs, 1)

            software_pipeline(pool, [(2, d_stage), (4, tail_rstd("d")), (6, tail_keep("d"))], peel=8)

        @block.vector
        def _(dve):
            nc.vector.memset(ones[:, :], 1.0).then_inc(consts_set, 1)
            dve.wait_ge(w0_ps, 1)
            nc.vector.tensor_copy(w4T[:, :, :], psum[:, 0, :].rearrange("p (i d) -> p i d", i=4)).then_inc(w0_sb, 1)
            dve.wait_ge(w0_ps, 2)
            nc.vector.tensor_copy(w1T[:, :], psum[0:3, 4, 8:8 + DH0]).then_inc(w0_sb, 1)
            nc.vector.tensor_copy(w2T[:, :], psum[0:DH0, 4, 128:128 + DH0]).then_inc(w0_sb, 1)
            nc.vector.tensor_copy(w3c[:, :], psum[0:DH0, 4, 256:256 + P]).then_inc(w0_sb, 1)
            nc.vector.tensor_copy(routerT[:, :], psum[:, 4, 0:NE]).then_inc(w0_sb, 1)
            bn0 = wa[:, 0:NB * 6].rearrange("p (b s) -> p b s", b=NB)
            for g in range(X_GROUPS):
                dve.wait_ge(ld_x[g], 16)
                for b in range(4 * g, 4 * g + 4):
                    i = nc.vector.bn_stats(bn0[:, b, :], x[:, b, :])
                i.then_inc(ln0_st, 1)
                if g == 1:
                    dve.wait_ge(w0_ps, 3)
                    nc.vector.tensor_copy(w1f.rearrange("p c h -> p (c h)"), psum[:, 5, 0:3 * DH0]).then_inc(w0_sb, 1)
                    nc.vector.tensor_copy(bout0[:, :], psum[0:1, 5, 256:256 + D]).then_inc(w0_sb, 1)
                dve.wait_ge(ln0_st, g + 1)
                for b in range(4 * g, 4 * g + 4):
                    i = nc.vector.bn_aggr(mean0[:, b, :], bn0[:, b, :])
                i.then_inc(ln0_ag, 1)
            dve.wait_ge(ln0_r, 1)

            carriers = []

            def carrier():
                n = len(carriers)
                carriers.append(sem(f"carried{n}"))

                def stats_wait(b, *waits):
                    for s, v in waits + ((carriers[n], b),):
                        if not isinstance(v, int) or v > 0:
                            dve.wait_ge(s, v)
                    nc.vector.memset(carried[:, n:n + 1], 0.0).then_inc(carriers[n], 1)
                return stats_wait

            def a_norm(b, z):
                reused(dve, a_tps, b)
                if isinstance(b, int) and b % 4 == 0 and b < 4 * X_GROUPS:
                    dve.wait_ge(ln0_r, b // 4 + 1 if b == 0 else X_GROUPS)
                nc.vector.tensor_scalar(xn[:, z, :], x[:, b, :], mean0[:, b, 0:1], rstd0[:, bass.ds(b, 1)],
                                        ALU.subtract, ALU.mult).then_inc(a_xn, 1)

            def a_rowmax(half):
                def run(b, z):
                    dve.wait_ge(a_s, b * 2 + half + 1)
                    if half == 0:
                        reused(dve, a_exp, b, 2)
                        reused(dve, a_nkeep, b)
                    nc.vector.tensor_reduce(
                        negmax[:, z, half * HALF0:(half + 1) * HALF0].rearrange("p (a h) -> p a h", a=2),
                        psum[:, 3 + 2 * half:5 + 2 * half, 0:4 * LK].rearrange("p a (h k) -> p a h k", k=LK),
                        AX_X, ALU.max, negate=True).then_inc(a_neg, 1)
                return run

            def a_stats(half):
                stats_wait = carrier()

                def run(b, z):
                    stats_wait(b, (a_exp, b * 2 + half + 1))
                    for h in range(half * HALF0, (half + 1) * HALF0):
                        s = nc.vector.bn_stats(bnout[:, bass.ds(b * H0 + h, 1), :].rearrange("p a s -> p (a s)"),
                                               prob[:, z, h, :])
                    s.then_inc(a_bn, 1)
                return run

            software_pipeline(dve, [(0, a_norm), (4, a_stats(0)), (3, a_rowmax(0)), (4, a_stats(1)), (3, a_rowmax(1))], peel=6)

            dve.wait_ge(a_nkeep, NB)
            dve.wait_ge(a_k, NB)
            dve.wait_ge(a_bn, 2 * NB)
            mean_e, m2_e, mean_o, m2_o = (bnout[:, :, i] for i in (1, 2, 4, 5))
            HALF_KEYS = LK // 2
            nc.vector.tensor_tensor(small[:, 0, :], mean_e, mean_o, ALU.add)
            nc.vector.tensor_tensor(small[:, 1, :], mean_e, mean_o, ALU.subtract)
            nc.vector.tensor_tensor(small[:, 5, 0:NB], qsum[:, :], ksum[:, :], ALU.mult).then_inc(f_dve, 1)
            dve.wait_ge(f_dve, 1)
            nc.vector.tensor_tensor(small[:, 2, :], small[:, 0, :], small[:, 0, :], ALU.mult)
            nc.vector.tensor_tensor(small[:, 3, :], small[:, 1, :], small[:, 1, :], ALU.mult)
            nc.vector.tensor_tensor(small[:, 4, :].rearrange("p (b h) -> p b h", b=NB),
                                    small[:, 5, 0:NB].unsqueeze(2).to_broadcast([P, NB, H0]),
                                    headmask.unsqueeze(1).to_broadcast([P, NB, H0]), ALU.mult).then_inc(f_dve, 1)
            dve.wait_ge(f_dve, 2)
            nc.vector.scalar_tensor_tensor(out=small[:, 1, :], in0=small[:, 3, :], scalar=HALF_KEYS / 2.0, in1=m2_e,
                                           op0=ALU.mult, op1=ALU.add)
            nc.vector.reciprocal(small[:, 0, :], small[:, 2, :]).then_inc(f_dve, 1)
            dve.wait_ge(f_dve, 3)
            nc.vector.tensor_tensor(small[:, 3, :], small[:, 1, :], m2_o, ALU.add).then_inc(f_dve, 1)
            dve.wait_ge(f_dve, 4)
            nc.vector.scalar_tensor_tensor(out=small[:, 2, :], in0=small[:, 3, :],
                                           scalar=1.0 / ((LK - 1) * HALF_KEYS ** 2), in1=small[:, 0, :],
                                           op0=ALU.mult, op1=ALU.mult).then_inc(f_dve, 1)

            dve.wait_ge(ld_w, 16 * N_W)
            nc.vector.tensor_tensor(bqk[:, :], bqk1[:, 0], bqk1[:, 1], ALU.mult).then_inc(l1_dve, 1)
            weight_copies(nc.vector, dve, range(ACT_GROUPS, N_GROUPS - 3))

            dve.wait_ge(mlp_pe, 3)
            nc.vector.tensor_scalar(small[:, 0, :], psum[:, 4, 256:512], b3c, LOG_T_MIN, ALU.add, ALU.max
                                    ).then_inc(temp_dve, 1)
            dve.wait_ge(temp_dve, 1)
            nc.vector.tensor_scalar(small[:, 1, :], small[:, 0, :], LOG_T_MAX, math.log(2.0), ALU.min, ALU.add
                                    ).then_inc(temp_dve, 1)
            weight_copies(nc.vector, dve, range(N_GROUPS - 3, N_GROUPS))
            dve.wait_ge(mlp_act, 3)
            nc.vector.scalar_tensor_tensor(out=small[:, 2, :], in0=rowneg[:, :], scalar=math.sqrt(DK0),
                                           in1=invt[:, :], op0=ALU.mult, op1=ALU.mult).then_inc(temp_dve, 1)
            nc.vector.tensor_tensor(small[:, 3, :].rearrange("p (b h) -> p b h", b=NB),
                                    invt.rearrange("p (b h) -> p b h", b=NB),
                                    headmask.unsqueeze(1).to_broadcast([P, NB, H0]), ALU.mult).then_inc(temp_dve, 1)
            dve.wait_ge(temp_dve, 4)
            nc.vector.tensor_reduce(invtT[:, :], small[:, 3, :].rearrange("p (b h) -> p b h", b=NB), AX_X, ALU.add
                                    ).then_inc(temp_dve, 1)
            dve.wait_ge(mlp_pe, 4)
            turned = psum[:, 5, 0:BH].rearrange("p (a q) -> p a q", a=2)
            nc.vector.tensor_copy(mparts[:, :, 0, :], turned).then_inc(temp_dve, 1)
            dve.wait_ge(temp_dve, 6)
            nc.vector.tensor_tensor(mparts[:, :, 1, :], turned, mparts[:, :, 0, :], ALU.subtract
                                    ).then_inc(temp_dve, 1)
            dve.wait_ge(l1_pe, 2)
            nc.vector.tensor_copy(cvec[:, :], keep[:, 384:384 + H1]).then_inc(l1_dve, 1)
            nc.vector.tensor_copy(uvec[:, :], keep[:, 384 + H1:384 + 2 * H1]).then_inc(l1_dve, 1)
            nc.vector.tensor_copy(ubias[:, :], psum[:, 6, 2 * H1:3 * H1]).then_inc(l1_dve, 1)
            nc.vector.tensor_copy(bout1[:, :], psum[0:1, 6, 256:256 + D]).then_inc(l1_dve, 1)

            def b_scale(b, z):
                reused(dve, b_qexp, b, 2)
                nc.vector.tensor_scalar(qsc[:, z, :], qT[:, b, :], invtT[:, bass.ds(b, 1)], None, ALU.mult
                                        ).then_inc(b_qsc, 1)

            def b_expand(half):
                def run(b, z):
                    dve.wait_ge(b_qsc, b + 1)
                    reused(dve, b_s, b, 2)
                    heads = slice(half * HALF0, (half + 1) * HALF0)
                    nc.vector.tensor_tensor(qexp[:, z, heads, :],
                                            qsc[:, z, :].unsqueeze(1).to_broadcast([P, HALF0, LQ]),
                                            headmask[:, heads].unsqueeze(2).to_broadcast([P, HALF0, LQ]), ALU.mult
                                            ).then_inc(b_qexp, 1)
                return run

            def b_recip(b, z):
                dve.wait_ge(b_od, b + 1)
                reused(dve, b_oT, b)
                nc.vector.reciprocal(rden[:, z, :], psum[:, 4, LQ:2 * LQ]).then_inc(b_rden, 1)

            def b_norm(b, z):
                dve.wait_ge(b_rden, b + 1)
                reused(dve, b_y, b)
                nc.vector.tensor_tensor(oT[:, z, :], psum[:, 4, 0:LQ], rden[:, z, :], ALU.mult).then_inc(b_oT, 1)

            def b_residual(b, z):
                dve.wait_ge(b_y, b + 1)
                nc.vector.tensor_tensor(x[:, b, :], psum[:, 5, 0:D], x[:, b, :], ALU.add).then_inc(b_x1, 1)

            def tail_stats(ph, ready):
                s, stats_wait = tails[ph], carrier()

                def run(b, z, count=None):
                    stats_wait(b, (ready, b + 1 if count is None else count), (s["ag"], b - 1))
                    nc.vector.bn_stats(bn6[:, z, :], x[:, b, :]).then_inc(s["bn"], 1)
                return run

            def tail_aggr(ph):
                s, stats_wait, pool_per = tails[ph], carrier(), 6 if ph == "b" else 2

                def run(b, z):
                    stats_wait(b, (s["bn"], b + 1), (s["pool"], (b - 1) * pool_per), (s["xn"], b - 1))
                    nc.vector.bn_aggr(mv[:, z, :], bn6[:, z, :]).then_inc(s["ag"], 1)
                return run

            def tail_norm(ph):
                s, pool_per = tails[ph], 6 if ph == "b" else 2

                def run(b, z):
                    dve.wait_ge(s["pool"], (b + 1) * pool_per)
                    reused(dve, s["tp"], b)
                    if ph == "b":
                        reused(dve, s["xr"], b)
                    i = nc.vector.tensor_scalar(xn[:, z, :], x[:, b, :], mv[:, z, 0:1], rstd[:, z, 1:2],
                                                ALU.subtract, ALU.mult)
                    i.then_inc(s["xn"], 1)
                return run

            def tail_rms(b, z):
                s = tails["b"]
                dve.wait_ge(s["xn"], b + 1)
                nc.vector.tensor_scalar(xr[:, z, :], xn[:, z, :], rstd[:, z, 3:4], None, ALU.mult).then_inc(s["xr"], 1)
                nc.vector.tensor_tensor(x[:, b, :], x[:, b, :], xn[:, z, :], ALU.add).then_inc(b_x, 1)

            software_pipeline(dve, [(0, b_scale), (4, tail_norm("b")), (0, b_expand(0)), (4, tail_rms),
                                    (3, b_residual), (0, b_expand(1)), (3, tail_stats("b", b_x1)), (2, b_recip),
                                    (3, tail_aggr("b")), (2, b_norm)], peel=8)

            def route(n, logits, bias):
                at = n * R_COUNT
                count = [at]

                def done(ins):
                    count[0] += 1
                    ins.then_inc(r_dve, 1)

                def after_all():
                    dve.wait_ge(r_dve, count[0])

                if bias is None:
                    done(nc.vector.tensor_copy(lg[:, :, :], logits))
                else:
                    done(nc.vector.tensor_tensor(lg[:, :, :], logits, bias.unsqueeze(1).to_broadcast([P, NB, NE]),
                                                 ALU.add))
                after_all()
                for b in range(NB):
                    i = nc.vector.max(mx8[:, b, :], lg[:, b, :])
                done(i)
                after_all()
                for b in range(NB):
                    i = nc.vector.max_index(ix8[:, b, :], mx8[:, b, :], lg[:, b, :])
                done(i)
                done(nc.vector.tensor_tensor(rt[:, 0, :], mx8[:, :, 1], mx8[:, :, 0], ALU.subtract))
                after_all()
                done(nc.vector.tensor_copy(rt[:, 4:6, :].rearrange("p j b -> p b j"), ix8[:, :, 0:2]))
                dve.wait_ge(r_act, n + 1)
                done(nc.vector.tensor_scalar(rt[:, 2, :], rt[:, 1, :], 1.0, None, ALU.add))
                after_all()
                done(nc.vector.reciprocal(rt[:, 3, :], rt[:, 2, :]))
                after_all()
                done(nc.vector.tensor_tensor(rt[:, 2, :], rt[:, 1, :], rt[:, 3, :], ALU.mult))
                experts = iota.unsqueeze(1).to_broadcast([P, NB, NE])
                for j in range(2):
                    done(nc.vector.tensor_tensor(oh[:, j], experts, rt[:, 4 + j, :].unsqueeze(2).to_broadcast([P, NB, NE]),
                                                 ALU.is_equal))
                after_all()
                for j in range(2):
                    done(nc.vector.tensor_tensor(oh[:, j], oh[:, j], rt[:, 3 - j, :].unsqueeze(2).to_broadcast([P, NB, NE]),
                                                 ALU.mult))
                after_all()
                done(nc.vector.tensor_tensor(gate[:, :, :], oh[:, 0], oh[:, 1], ALU.add))
                after_all()
                assert count[0] == at + R_COUNT

            def route_experts():
                dve.wait_ge(tails["b"]["lg"], NB)
                dve.wait_ge(b_x, NB)
                route(0, logits0, None)

            def c_hidden(g, e):
                u = g * NE + e
                for j in range(DN_TILES):
                    v = u * DN_TILES + j
                    dve.wait_ge(c_silu, v + 1)
                    dve.wait_ge(c_up, v + 1)
                    if not isinstance(u, int) or u >= 2:
                        dve.wait_ge(c_dn, u - 1)
                    nc.vector.tensor_tensor(hT[:, e % 2, j, :], psum[:, 2 * j, :], silu[:, j, :], ALU.mult
                                            ).then_inc(c_h, 1)

            def c_accumulate(g, e):
                u = g * NE + e
                dve.wait_ge(c_dn, u + 1)
                if e:
                    dve.wait_ge(c_acc, u)
                for sq in range(SEQS):
                    b = g * SEQS + sq
                    i = nc.vector.scalar_tensor_tensor(out=x[:, b, :], in0=psum[:, 4 + e % 2, sq * D:(sq + 1) * D],
                                                       scalar=gate[:, b, e:e + 1], in1=x[:, b, :],
                                                       op0=ALU.mult, op1=ALU.add)
                i.then_inc(c_acc, 1)

            c_stats, c_aggr, c_norm = tail_stats("c", c_acc), tail_aggr("c"), tail_norm("c")

            def c_tail(g, stage, sq):
                b, z = g * SEQS + sq, sq % 2
                if stage is c_stats:
                    stage(b, z, (g + 1) * NE)
                    c_aggr(b, z)
                else:
                    stage(b, z)

            def c_slot(g, e):
                c_hidden(g, e)
                if isinstance(g, int) and g == 0 and e == ROUTE_SLOT:
                    route_experts()
                if e:
                    c_accumulate(g, e - 1)
                elif not isinstance(g, int) or g:
                    c_accumulate(g - 1, NE - 1)
                if not isinstance(g, int) or g:
                    if e in NORM_SLOTS:
                        c_tail(g - 1, c_norm, e - NORM_SLOTS[0])
                    if e in STATS_SLOTS:
                        c_tail(g - 1, c_stats, e - STATS_SLOTS[0])

            expert_slots(dve, c_slot)
            c_accumulate(GROUPS - 1, NE - 1)
            for stage, sq in ((c_stats, 0), (c_stats, 1), (c_norm, 0), (c_stats, 2), (c_norm, 1), (c_stats, 3),
                              (c_norm, 2), (c_norm, 3)):
                c_tail(GROUPS - 1, stage, sq)

            def d_queries(b, z):
                dve.wait_ge(d_q, b + 1)
                reused(dve, d_s, b)
                nc.vector.tensor_tensor(q2[:, z].rearrange("p (a h) q -> p a h q", a=2),
                                        psum[:, 0:2, :].rearrange("p a (h q) -> p a h q", q=LQ),
                                        cvec.rearrange("p (a h) -> p a h", a=2).unsqueeze(3).to_broadcast([P, 2, 4, LQ]),
                                        ALU.add).then_inc(d_q2, 1)

            def d_scores(b, z):
                dve.wait_ge(d_s, b + 1)
                reused(dve, d_exp, b)
                for a in range(2):
                    i = nc.vector.tensor_tensor(
                        s1[:, z, 4 * a:4 * a + 4, :].rearrange("p (n i) k -> p n i k", n=2),
                        psum[:, 2 + a, 0:4 * LK].rearrange("p (n i k) -> p n i k", n=2, i=2),
                        window[:, 2 * a:2 * a + 2, :].unsqueeze(2).to_broadcast([P, 2, 2, LK]), ALU.add)
                i.then_inc(d_sm, 1)
                dve.wait_ge(d_sm, b + 1)
                reused(dve, d_mu, b)
                nc.vector.tensor_reduce(d8[:, z, 0, :], s1[:, z], AX_X, ALU.max, negate=True).then_inc(d_max, 1)
                dve.wait_ge(d_max, b + 1)
                reused(dve, d_sh, b)
                nc.vector.tensor_tensor(d8[:, z, 2, :], u1s[:, b, :], d8[:, z, 0, :], ALU.subtract).then_inc(d_mu, 1)
                dve.wait_ge(d_mu, b + 1)
                nc.vector.tensor_tensor(d8[:, z, 3, :], u1s[:, b, :], d8[:, z, 2, :], ALU.subtract).then_inc(d_sh, 1)

            def d_weights(b, z):
                dve.wait_ge(d_exp, b + 1)
                reused(dve, d_a, b)
                nc.vector.reciprocal(d8[:, z, 1, :], d8[:, z, 4, :]).then_inc(d_rs, 1)
                dve.wait_ge(d_rs, b + 1)
                reused(dve, d_tp, b)
                nc.vector.tensor_tensor(a1[:, z], e1[:, z], d8[:, z, 1, :].unsqueeze(2).to_broadcast([P, H1, LK]),
                                        ALU.mult).then_inc(d_a, 1)

            def d_residual(b, z):
                dve.wait_ge(d_y, b + 1)
                nc.vector.tensor_tensor(x[:, b, :], psum[:, BANK_TAIL, 128:128 + D], x[:, b, :], ALU.add
                                        ).then_inc(d_x, 1)

            dve.wait_ge(tails["c"]["lg"], NB)
            nc.vector.tensor_tensor(u1s[:, :, :], u1, ubias.unsqueeze(1).to_broadcast([P, NB, H1]), ALU.add
                                    ).then_inc(d_u, 1)
            dve.wait_ge(d_u, 1)
            software_pipeline(dve, [(5, tail_norm("d")), (1, d_scores), (0, d_queries), (2, d_weights),
                                    (4, d_residual), (4, tail_stats("d", d_x)), (4, tail_aggr("d"))], peel=8)

            dve.wait_ge(tails["d"]["lg"], NB)
            route(1, logits1, rb1)
            dve.wait_ge(e_gt, 1)
            nc.vector.tensor_copy(gateT[:, :], psum[:, BANK_TAIL, 0:P]).then_inc(e_gts, 1)

            dve.wait_ge(e_gts, 1)

            def e_mask(b, z):
                reused(dve, e_y, b)
                nc.vector.tensor_scalar(gm[:, z, :], gateT[:, :], headmask[:, bass.ds(b, 1)], None, ALU.mult
                                        ).then_inc(e_gm, 1)

            def e_weigh(b, z):
                dve.wait_ge(e_g, b + 1)
                dve.wait_ge(e_gps, b + 1)
                reused(dve, e_y, b)
                nc.vector.tensor_tensor(hg[:, z].rearrange("p m q -> p (m q)"), psum[:, 2 + z, :],
                                        h1[:, z].rearrange("p m q -> p (m q)"), ALU.mult).then_inc(e_hg, 1)

            def e_residual(b, z):
                dve.wait_ge(e_y, b + 1)
                if not isinstance(b, int) or b >= 2:
                    dve.wait_ge(e_out[z], (b - z) * 8)
                nc.vector.tensor_tensor(yacc[:, z, :], psum[:, 4 + z, 0:D], x[:, b, :], ALU.add).then_inc(e_acc, 1)

            software_pipeline(dve, [(0, e_mask), (1, e_weigh), (2, e_residual)])

        @block.tensor
        def _(pe):
            def turn(dst, src, k):
                return nc.tensor.transpose(dst, src, ident[0:k, 0:k])

            pe.wait_ge(ld_first, 16 * N_FIRST)
            for i in range(4):
                m = turn(psum[:, 0, i * D:(i + 1) * D], nat0[:, i, :], P)
            m.then_inc(w0_ps, 1)
            pe.wait_ge(consts_set, 5)
            turn(psum[:, 4, 0:NE], nat0[0:NE, 4, :], NE)
            turn(psum[0:3, 4, 8:8 + DH0], wsm[0:DH0, 0:3], DH0)
            turn(psum[0:DH0, 4, 128:128 + DH0], wsm[0:DH0, 3:3 + DH0], DH0)
            nc.tensor.matmul(psum[0:DH0, 4, 256:256 + P], wsm[0:1, 3 + DH0:3 + 2 * DH0], ones[0:1, :],
                             start=True, stop=True).then_inc(w0_ps, 1)
            pe.wait_ge(w0_sb, 2)
            for c in range(3):
                nc.tensor.matmul(psum[:, 5, c * DH0:(c + 1) * DH0], sel[0:3, c, :], w1T[:, :], start=True, stop=True)
            nc.tensor.matmul(psum[0:1, 5, 256:256 + D], bv0, w4T[:, 3, :], start=True, stop=False)
            nc.tensor.matmul(psum[0:1, 5, 256:256 + D], ones[0:1, 0:1], bo0[:, :], start=False, stop=True
                             ).then_inc(w0_ps, 1)

            def a_turn(b, z):
                pe.wait_ge(a_xn, b + 1)
                pe.wait_ge(ld_ctx[z], (b - z + 2) * 8)
                if not isinstance(b, int) or b >= 1:
                    pe.wait_ge(a_xc, b)
                turn(psum[:, 0, 0:LQ], xn[:, z, :], P)
                turn(psum[:, 0, LQ:LQ + LK], craw[:, z, :], LK).then_inc(a_tps, 1)

            def a_project(b, z):
                pe.wait_ge(a_xc, b + 1)
                if not isinstance(b, int) or b >= 1:
                    pe.wait_ge(a_k, b)
                    pe.wait_ge(a_v, b)
                nc.tensor.matmul(psum[:, 1, 0:LQ], w4T[:, 0, :], xc[:, z, 0:LQ], start=True, stop=True)
                nc.tensor.matmul(psum[:, 1, LQ:LQ + LK], w4T[:, 1, :], xc[:, z, LQ:LQ + LK], start=True, stop=True)
                nc.tensor.matmul(psum[0:LK, 2, 0:D], xc[:, z, LQ:LQ + LK], w4T[:, 2, :], start=True, stop=True
                                 ).then_inc(a_qkv, 1)

            def a_scores(half):
                def run(b, z):
                    pe.wait_ge(a_q, b + 1)
                    pe.wait_ge(a_kexp, b + 1)
                    if not isinstance(b, int) or b >= 1:
                        pe.wait_ge(a_exp, b * 2 + half - 1)
                    for j in range(2):
                        h = half * HALF0 + 4 * j
                        m = nc.tensor.matmul(psum[:, 3 + 2 * half + j, 0:4 * LK], qs[:, z, :],
                                             kexp[:, z, h:h + 4, :].rearrange("p h k -> p (h k)"), start=True, stop=True)
                    m.then_inc(a_s, 1)
                return run

            software_pipeline(pe, [(3, a_scores(0)), (1, a_turn), (3, a_scores(1)), (1, a_project)], peel=6)

            pe.wait_ge(ld_w, 16 * N_W)
            small1 = keep[:, 384:384 + 2 * H1]
            for h in range(H1):
                nc.tensor.matmul(small1[:, h:h + 1], l1N[:, 1, h, :], bqk1[:, 0, h:h + 1], start=True, stop=True)
                m = nc.tensor.matmul(small1[:, H1 + h:H1 + h + 1], l1N[:, 0, h, :], bqk1[:, 1, h:h + 1],
                                     start=True, stop=True)
            m.then_inc(l1_pe, 1)
            pe.wait_ge(a_exp, 2 * NB)
            pe.wait_ge(a_xc, NB)
            pe.wait_ge(a_k, NB)
            pe.wait_ge(a_v, NB)
            def weights(groups):
                for g in groups:
                    if g >= RING_W:
                        group_copied(pe, g - RING_W)
                    if g == WC_GROUPS[-1] + 3:
                        group_copied(pe, WC_GROUPS[-1])
                    for i, ops in enumerate(weight_groups()[g][1]):
                        dst = psum[:, g % RING_W, i * D:(i + 1) * D]
                        m = turn(dst, ops[1], P) if ops[0] == "turn" else \
                            nc.tensor.matmul(dst, ops[1], ops[2], start=True, stop=True)
                    m.then_inc(wt_ps, 1)

            weights(range(ACT_GROUPS))
            pe.wait_ge(f_dve, 5)
            for c, feature in enumerate((small[:, 4, :], rowneg[:, :], small[:, 2, :])):
                m = nc.tensor.matmul(psum[0:DH0, 4, 0:BH], w1f[:, c, :], feature, start=(c == 0), stop=(c == 2))
            m.then_inc(mlp_pe, 1)
            weights(range(ACT_GROUPS, ACT_GROUPS + 3))
            pe.wait_ge(mlp_act, 1)
            nc.tensor.matmul(psum[0:DH0, 5, 0:BH], w2T[:, :], small[0:DH0, 6, :], start=True, stop=True
                             ).then_inc(mlp_pe, 1)
            weights(range(ACT_GROUPS + 3, N_GROUPS - 3))
            pe.wait_ge(mlp_act, 2)
            nc.tensor.matmul(psum[:, 4, 256:512], w3c[:, :], small[0:DH0, 7, :], start=True, stop=True
                             ).then_inc(mlp_pe, 1)
            weights(range(N_GROUPS - 3, N_GROUPS))
            pe.wait_ge(l1_dve, 1)
            nc.tensor.matmul(psum[:, 6, 2 * H1:3 * H1], ones[:, :], bqk[:, :], start=True, stop=True)
            nc.tensor.matmul(psum[0:1, 6, 256:256 + D], ones[0:1, 0:1], bc1[:, :], start=True, stop=False)
            for h in range(H1):
                m = nc.tensor.matmul(psum[0:1, 6, 256:256 + D], bqk1[:, 2, h:h + 1], wcT[:, h, :],
                                     start=False, stop=(h == H1 - 1))
            m.then_inc(l1_pe, 1)

            pe.wait_ge(temp_dve, T_SCALED)
            for half in range(2):
                m = turn(psum[:, 5, half * P:(half + 1) * P], small[:, 2, half * P:(half + 1) * P], P)
            m.then_inc(mlp_pe, 1)

            def tail_turn(ph):
                s = tails[ph]

                def run(b, z):
                    pe.wait_ge(s["xr" if ph == "b" else "xn"], b + 1)
                    if not isinstance(b, int) or b >= 1:
                        pe.wait_ge(s["ev"], b)
                    if ph == "d":
                        pe.wait_ge(d_x, min(b + 2, NB) if isinstance(b, int) else b + 2)
                    turn(tail_ps, (xr if ph == "b" else xn)[:, z, :], P).then_inc(s["tp"], 1)
                return run

            def tail_logits(ph, dst, weights):
                s = tails[ph]

                def run(b, z):
                    pe.wait_ge(s["ev"], b + 1)
                    nc.tensor.matmul(dst[:, b, :], xnT[:, z, :], weights, start=True, stop=True).then_inc(s["lg"], 1)
                return run

            def b_scores(half):
                def run(b, z):
                    pe.wait_ge(b_qexp, b * 2 + half + 1)
                    pe.wait_ge(b_kt, b + 1)
                    if not isinstance(b, int) or b >= 1:
                        pe.wait_ge(b_exp, b * 2 + half - 1)
                    for j in range(2):
                        h = half * HALF0 + 4 * j
                        nc.tensor.matmul(psum[0:LK, 2 * half + j, :], ktS[:, z, :],
                                         qexp[:, z, h:h + 4, :].rearrange("p h q -> p (h q)"), start=True, stop=False)
                    pe.wait_ge(ld_m[z], (b - z + 2) * 8)
                    for j in range(2):
                        h, dst = half * HALF0 + 4 * j, psum[0:LK, 2 * half + j, :]
                        m = nc.tensor.matmul(dst, onesb[:, :], mrow[:, z, h * LQ:(h + 4) * LQ], start=False, stop=True)
                    m.then_inc(b_s, 1)
                return run

            def b_output(b, z):
                pe.wait_ge(b_exp, b * 2 + 2)
                pe.wait_ge(b_v, b + 1)
                if not isinstance(b, int) or b >= 1:
                    pe.wait_ge(b_oT, b)
                for c, pad in ((0, None), (1, opad)):
                    for g in range(4):
                        for i in range(4):
                            w = vpad[:, z, g, 32 * i:32 * i + 32] if pad is None else pad[:, 32 * i:32 * i + 32]
                            m = nc.tensor.matmul(psum[32 * g:32 * g + 32, 4, c * LQ:(c + 1) * LQ], w,
                                                 probT[:, z, 4 * g + i, :], start=(i == 0), stop=(i == 3))
                m.then_inc(b_od, 1)

            def b_project(b, z):
                pe.wait_ge(b_oT, b + 1)
                if not isinstance(b, int) or b >= 1:
                    pe.wait_ge(b_x1, b)
                nc.tensor.matmul(psum[:, 5, 0:D], oT[:, z, :], w4T[:, 3, :], start=True, stop=False)
                nc.tensor.matmul(psum[:, 5, 0:D], ones[0:1, :], bout0[:, :], start=False, stop=True).then_inc(b_y, 1)

            pe.wait_ge(temp_dve, T_PARTS)
            software_pipeline(pe, [(5, tail_turn("b")), (1, b_scores(0)), (3, b_project), (2, b_output),
                                   (5, tail_logits("b", logits0, routerT)), (1, b_scores(1))], peel=8)

            def c_up_project(g, e):
                columns = lambda a: a[:, bass.ds(g * SEQS, SEQS), :].rearrange("p b q -> p (b q)")
                for j in range(DN_TILES):
                    v = (g * NE + e) * DN_TILES + j
                    if not isinstance(v, int) or v >= DN_TILES:
                        pe.wait_ge(c_h, v - 1)
                    for bank, tile, done in ((2 * j + 1, DN_TILES + j, c_gate), (2 * j, j, c_up)):
                        w = e * UP_TILES + tile
                        nc.tensor.matmul(psum[:, bank, :], up_hi[:, w, :], columns(x_hi), start=True, stop=False)
                        nc.tensor.matmul(psum[:, bank, :], up_hi[:, w, :], columns(x_lo), start=False, stop=False)
                        nc.tensor.matmul(psum[:, bank, :], up_lo[:, w, :], columns(x_hi), start=False, stop=True
                                         ).then_inc(done, 1)

            def c_down_project(g, e):
                u = g * NE + e
                pe.wait_ge(c_h, (u + 1) * DN_TILES)
                if not isinstance(u, int) or u >= 2:
                    pe.wait_ge(c_acc, u - 1)
                for sq in range(SEQS):
                    for j in range(DN_TILES):
                        m = nc.tensor.matmul(psum[:, 4 + e % 2, sq * D:(sq + 1) * D],
                                             hT[:, e % 2, j, sq * LQ:(sq + 1) * LQ], dnT[:, e * DN_TILES + j, :],
                                             start=(j == 0), stop=(j == DN_TILES - 1))
                m.then_inc(c_dn, 1)

            c_turn, c_logits = tail_turn("c"), tail_logits("c", u1, uvec)

            def c_slot(g, e):
                tails_too = not isinstance(g, int) or g > 0
                c_up_project(g, e)
                if e:
                    c_down_project(g, e - 1)
                elif tails_too:
                    c_down_project(g - 1, NE - 1)
                if tails_too and e in LOGITS_SLOTS:
                    c_logits((g - 1) * SEQS + e - LOGITS_SLOTS[0], (e - LOGITS_SLOTS[0]) % 2)
                if tails_too and e in TURN_SLOTS:
                    c_turn((g - 1) * SEQS + e - TURN_SLOTS[0], (e - TURN_SLOTS[0]) % 2)

            pe.wait_ge(tails["b"]["keep"], NB)
            pe.wait_ge(b_lo, NB)
            expert_slots(pe, c_slot)
            c_down_project(GROUPS - 1, NE - 1)
            for stage, sq in ((c_turn, 0), (c_turn, 1), (c_logits, 0), (c_turn, 2), (c_logits, 1), (c_turn, 3),
                              (c_logits, 2), (c_logits, 3)):
                stage((GROUPS - 1) * SEQS + sq, sq % 2)

            def d_queries(b, z):
                if not isinstance(b, int) or b >= 1:
                    pe.wait_ge(d_q2, b)
                for h in range(H1):
                    m = nc.tensor.matmul(psum[:, h // 4, (h % 4) * LQ:(h % 4 + 1) * LQ], qk1[:, h, :], xT[:, b, :],
                                         start=True, stop=True)
                m.then_inc(d_q, 1)

            def d_scores(b, z):
                pe.wait_ge(d_q2, b + 1)
                if not isinstance(b, int) or b >= 1:
                    pe.wait_ge(d_sm, b)
                for h in range(H1):
                    m = nc.tensor.matmul(psum[:, 2 + h // 4, (h % 4) * LK:(h % 4 + 1) * LK], q2[:, z, h, :],
                                         ctxT[:, b, :], start=True, stop=True)
                m.then_inc(d_s, 1)

            def d_values(b, z):
                pe.wait_ge(d_cs, b + 1)
                if not isinstance(b, int) or b >= 1:
                    pe.wait_ge(d_aT, b)
                for a in range(2):
                    m = nc.tensor.matmul(psum[0:LK, 4 + a, :], cS[:, z, :],
                                         vo1[:, 4 * a:4 * a + 4, :].rearrange("p h d -> p (h d)"), start=True, stop=True)
                m.then_inc(d_vwp, 1)

            def d_turn(b, z):
                pe.wait_ge(d_a, b + 1)
                pe.wait_ge(d_vw, b + 1)
                for h in range(H1):
                    m = turn(psum[0:LK, 4 + h // 4, (h % 4) * LQ:(h % 4 + 1) * LQ], a1[:, z, h, :], P)
                m.then_inc(d_tp, 1)

            def d_output(b, z):
                pe.wait_ge(d_aT, b + 1)
                pe.wait_ge(d_vw, b + 1)
                if not isinstance(b, int) or b >= 1:
                    pe.wait_ge(d_x, b)
                reused(pe, tails["d"]["ev"], b)
                dst = psum[:, BANK_TAIL, 128:128 + D]
                nc.tensor.matmul(dst, ones[0:1, :], bout1[:, :], start=True, stop=False)
                for h in range(H1):
                    m = nc.tensor.matmul(dst, a1T[:, z, h, :], vw[:, z, h, :], start=False, stop=(h == H1 - 1))
                m.then_inc(d_y, 1)

            pe.wait_ge(tails["c"]["keep"], NB)
            pe.wait_ge(ld_late, 16 * (N_LATE + 1))
            software_pipeline(pe, [(1, d_scores), (6, tail_turn("d")), (3, d_values), (0, d_queries), (3, d_turn),
                                   (4, d_output), (6, tail_logits("d", logits1, router1))], peel=8)

            pe.wait_ge(r_dve, 2 * R_COUNT)
            turn(psum[:, BANK_TAIL, 0:P], gate.rearrange("p b e -> p (b e)"), P).then_inc(e_gt, 1)
            pe.wait_ge(e_gts, 1)
            pe.wait_ge(tails["d"]["keep"], NB)

            def e_hidden(b, z):
                reused(pe, e_g, b)
                for m_ in range(H1_TILES):
                    m = nc.tensor.matmul(psum[:, z, m_ * LQ:(m_ + 1) * LQ],
                                         ew1[:, 2 * m_:2 * m_ + 2, :].rearrange("p n f -> p (n f)"), xT[:, b, :],
                                         start=True, stop=True)
                m.then_inc(e_h, 1)

            def e_gates(b, z):
                pe.wait_ge(e_gm, b + 1)
                reused(pe, e_hg, b)
                for m_ in range(H1_TILES):
                    m = nc.tensor.matmul(psum[:, 2 + z, m_ * LQ:(m_ + 1) * LQ], expert_rows[:, m_, :], gm[:, z, :],
                                         start=True, stop=True)
                m.then_inc(e_gps, 1)

            def e_output(b, z):
                pe.wait_ge(e_hg, b + 1)
                reused(pe, e_acc, b)
                dst = psum[:, 4 + z, 0:D]
                nc.tensor.matmul(dst, gm[:, z, :], b2rows[:, :], start=True, stop=False)
                for m_ in range(H1_TILES):
                    m = nc.tensor.matmul(dst, hg[:, z, m_, :], ew2[:, m_, :], start=False, stop=(m_ == H1_TILES - 1))
                m.then_inc(e_y, 1)

            software_pipeline(pe, [(0, e_hidden), (0, e_gates), (1, e_output)])


_INS = ['x', 'ctx_1024', 'L0_xattn_Wq', 'L0_xattn_bq', 'L0_xattn_Wk', 'L0_xattn_bk', 'L0_xattn_Wv', 'L0_xattn_bv',
        'L0_xattn_Wo', 'L0_xattn_bo', 'L0_xattn_w1', 'L0_xattn_b1', 'L0_xattn_w2', 'L0_xattn_b2', 'L0_xattn_w3',
        'L0_xattn_b3', 'L0_ffn_norm_scale', 'L0_ffn_w_router', 'L0_ffn_w_up', 'L0_ffn_w_down', 'L1_xattn_Wq',
        'L1_xattn_bq', 'L1_xattn_Wk', 'L1_xattn_bk', 'L1_xattn_Wv', 'L1_xattn_bv', 'L1_xattn_Wc', 'L1_xattn_bc',
        'L1_ffn_router_w', 'L1_ffn_router_b', 'L1_ffn_W1', 'L1_ffn_b1', 'L1_ffn_W2', 'L1_ffn_b2']


def kernel(**inputs):
    import numpy as _np
    import concourse.bacc as _bacc
    from concourse import mybir as _mybir
    from concourse.bass_utils import run_bass_kernel_spmd as _run

    nc = _bacc.Bacc("TRN2", target_bir_lowering=False, num_devices=1)
    cols, consts = shape_constants()
    arrays, t = {}, {}
    for name, value in [(n, inputs[n]) for n in _INS] + [("consts", consts)]:
        a = _np.ascontiguousarray(value)
        arrays[f"in_{name}_dram"] = a
        t[name] = nc.dram_tensor(f"in_{name}_dram", a.shape, _mybir.dt.from_np(a.dtype), kind="ExternalInput").ap()
    out = nc.dram_tensor("out_0_dram", (NB, LQ, D), F32, kind="ExternalOutput").ap()
    build(nc, cols, t, out)
    r = _run(nc, [arrays], core_ids=[0])
    return r.results[0]["out_0_dram"]
```

```python
import math
from contextlib import ExitStack

import numpy as np

import concourse.bass as bass
from concourse import mybir

F32 = mybir.dt.float32
F32R = mybir.dt.float32r
BF16 = mybir.dt.bfloat16
U32 = mybir.dt.uint32
ALU = mybir.AluOpType
ACT = mybir.ActivationFunctionType
AX_X = mybir.AxisListType.X

P = 128

NB, LQ, LK, D = 16, 128, 120, 128
H0, DK0 = 16, 8
DH0 = 64
NE = 8
HID0 = 256
H1, E1 = 8, 128
K1, DILATIONS = 64, (1, 2, 4, 8)
F1 = 64
LOG_T_MIN, LOG_T_MAX = math.log(0.1), math.log(10.0)
LN_EPS, RMS_EPS = 1e-5, 1e-6
NEG = -1.0e9
BH = NB * H0
X_GROUPS = 4
HALF0 = H0 // 2
UP_TILES = 2 * HID0 // P
DN_TILES = HID0 // P
H1_TILES = NE * F1 // P
SEQS = 4
GROUPS = NB // SEQS


def shape_constants():
    ident = np.eye(P, dtype=np.float32)
    part = np.arange(P)[:, None]
    headmask = (part // DK0 == np.arange(H0)[None, :]).astype(np.float32)
    mask = np.full((LQ, len(DILATIONS), LK), NEG, np.float64)
    for n, dil in enumerate(DILATIONS):
        count = np.zeros((LQ, LK))
        for l in range(LQ):
            for o in range(K1):
                at = l + (o - (K1 - 1) // 2) * dil
                if 0 <= at < LQ:
                    count[l, min(at, LK - 1)] += 1
        mask[:, n][count > 0] = np.log(count[count > 0])
    iota = np.tile(np.arange(NE, dtype=np.float32), (P, 1))
    sel = np.zeros((P, 3, P), np.float32)
    for c, w in enumerate((1.0 / (LQ * LK * math.sqrt(DK0)), -1.0 / LQ, 1.0 / LQ)):
        sel[c, c, :] = w
    expert_rows = ((part % NE)[:, :, None] == (2 * np.arange(H1_TILES)[:, None] + np.arange(P)[None, :] // F1)[None]
                   ).astype(np.float32)
    cols, at, parts = {}, 0, []
    for name, a in (("ident", ident), ("headmask", headmask), ("headscale", headmask / math.sqrt(DK0)),
                    ("iota", iota), ("sel", sel.reshape(P, -1)), ("window", mask.reshape(LQ, -1)),
                    ("expert_rows", expert_rows.reshape(P, -1))):
        cols[name] = (at, at + a.shape[1])
        at += a.shape[1]
        parts.append(a.astype(np.float32))
    return cols, np.ascontiguousarray(np.concatenate(parts, axis=1))


def software_pipeline(eng, stages, n=NB, peel=4):
    assert all(lag <= peel - 2 for lag, _ in stages) and (n - peel) % 2 == 0

    def step(b, parity):
        for lag, stage in stages:
            if not isinstance(b, int) or 0 <= b - lag < n:
                stage(b - lag, (parity - lag) % 2)

    for b in range(peel):
        step(b, b % 2)
    with eng.Fori(0, (n - peel) // 2) as i:
        for parity in range(2):
            step(i * 2 + (peel + parity), parity)
    for b in range(n, n + peel):
        step(b, b % 2)


def slots(eng, slot, per, n=GROUPS):
    for g in range(2):
        for e in range(per):
            slot(g, e)
    with eng.Fori(2, n) as g:
        for e in range(per):
            slot(g, e)


def reused(eng, sem, b, per=1):
    if not isinstance(b, int) or b >= 2:
        eng.wait_ge(sem, (b - 1) * per)


def build(nc, cols, t, out):
    with ExitStack() as ctx:
        def sb(name, shape, dt=F32):
            return ctx.enter_context(nc.sbuf_tensor(name, shape, dt))[:]

        def shared(name, shape, parts):
            with nc.sbuf_tensor(name, shape, F32) as a:
                whole = a[:]
            return whole, [sb(*part) for part in parts]

        def sem(name):
            return ctx.enter_context(nc.semaphore(name))

        psum = ctx.enter_context(nc.psum_tensor("psum", [P, 8, 512], F32))
        BANK_KEEP, BANK_TAIL = 7, 6

        cst = sb("cst", [P, cols["window"][1]])
        ident = cst[:, slice(*cols["ident"])]
        headmask = cst[:, slice(*cols["headmask"])]
        headscale = cst[:, slice(*cols["headscale"])]
        window = cst[:, slice(*cols["window"])].rearrange("p (n k) -> p n k", n=len(DILATIONS))
        iota = cst[:, slice(*cols["iota"])]
        sel = cst[:, slice(*cols["sel"])].rearrange("p (c q) -> p c q", c=3)
        x = sb("x", [P, NB, D])
        ctxT = sb("ctxT", [P, NB, LK])
        qT, (vo_hi, vo_lo) = shared("qT", [P, NB, LQ], [("vo_hi", [P, H1, D], F32R), ("vo_lo", [P, H1, D], F32R)])
        kT, (c_hi, c_lo) = shared("kT", [P, NB, LK], [("c_hi", [P, 2, LK], F32R), ("c_lo", [P, 2, LK], F32R)])
        w1_hi, w1_lo = sb("w1_hi", [P, NE * F1], F32R), sb("w1_lo", [P, NE * F1], F32R)
        sb("kT_rest", [P, (NB - 4) * LK - 2 * NE * F1])
        v0 = sb("v0", [LK, NB, D])
        xT, (x_hi,) = shared("xT", [P, NB, LQ], [("x_hi", [P, NB, LQ], F32R)])
        scored, (x_lo,) = shared("scored", [P, 8 * BH], [("x_lo", [P, NB, LQ], F32R)])
        gate = sb("gate", [P, NB, NE])
        bnout = scored[:, 0:6 * BH].rearrange("p (r s) -> p r s", s=6)
        rowneg = scored[:, 6 * BH:7 * BH]
        negmax = sb("negmax", [P, 2, H0])
        qsum = sb("qsum", [P, NB])
        ksum = sb("ksum", [P, NB])
        invt = scored[:, 7 * BH:8 * BH]
        invtT = sb("invtT", [P, NB])
        small = sb("small", [P, 8, BH])
        ones = sb("ones", [P, P])
        onesb = sb("onesb", [P, LK], BF16)
        w4T = sb("w4T", [P, 4, D])
        upT = sb("upT", [P, NE * UP_TILES, P])
        dnT = sb("dnT", [P, NE * DN_TILES, D])
        routerT = sb("routerT", [P, NE])
        w1f = sb("w1f", [P, 3, DH0])
        w1T = sb("w1T", [3, DH0])
        w2T = sb("w2T", [DH0, DH0])
        w3c = sb("w3c", [DH0, P])
        qk1 = sb("qk1", [P, H1, D])
        vo1 = sb("vo1", [P, H1, D])
        cvec = sb("cvec", [P, H1])
        uvec = sb("uvec", [P, H1])
        ubias = sb("ubias", [P, H1])
        bout1 = sb("bout1", [1, D])
        router1 = sb("router1", [P, NE])
        ew1 = sb("ew1", [P, NE, F1])
        ew2 = sb("ew2", [P, H1_TILES, D])
        b2rows = sb("b2rows", [P, D])
        gateT = sb("gateT", [P, P])
        vecs = sb("vecs", [P, 16])
        bq0, bk0, b1c, b2c, b3c, nscale, bv0 = (vecs[:, i:i + 1] for i in range(7))
        b1e = vecs[:, 7:7 + H1_TILES]
        bo0 = sb("bo0", [1, D])
        bout0 = sb("bout0", [1, D])
        bc1 = sb("bc1", [1, D])
        rb1 = sb("rb1", [P, NE])
        bqk1 = sb("bqk1", [P, 3, H1])
        bqk = sb("bqk", [P, H1])
        nat0 = sb("nat0", [P, 5, D])
        wsm = sb("wsm", [P, 3 + DH0 + DH0])
        eps = sb("eps", [P, 4])
        carried = sb("carried", [P, 8])
        bn6 = sb("bn6", [P, 2, 6])
        mv = sb("mv", [P, 2, 2])
        rstd = sb("rstd", [P, 2, 4])
        mean0 = sb("mean0", [P, NB, 2])
        rstd0 = sb("rstd0", [P, NB])
        xn = sb("xn", [P, 2, D])
        xnT = sb("xnT", [P, 2, LQ])
        work, (gm_hi, gm_lo, gT_hi, gT_lo, _, up_lo) = shared("work", [P, 13552], [
            ("gm_hi", [P, SEQS, LQ], F32R), ("gm_lo", [P, SEQS, LQ], F32R), ("gT_hi", [P, P], F32R),
            ("gT_lo", [P, P], F32R), ("work_head", [P, 9456 - 2 * SEQS * LQ - 2 * P], F32),
            ("up_lo", [P, NE * UP_TILES, P], F32R)])

        def area(at, n):
            return work[:, at:at + n]

        W_UP, W_DN, W_L1, W_C = 2048, 6144, 8192, 11264
        upN = area(W_UP, 4096).rearrange("p (t d) -> p t d", d=D)
        dnN = area(W_DN, 2048).rearrange("p (e h) -> p e h", e=NE)
        l1N = area(W_L1, 3072).rearrange("p (w h d) -> p w h d", w=3, h=H1)
        wcN = area(W_C, 1024).rearrange("p (h e) -> p h e", h=H1)
        wcT = area(W_C + 1024, 1024).rearrange("p (h o) -> p h o", h=H1)
        wa, (_, up_hi, _, rows_r, _) = shared("wa", [P, 8688], [
            ("wa_head", [P, 3328], F32), ("up_hi", [P, NE * UP_TILES, P], F32R), ("wa_rows", [P, H1_TILES * P], F32),
            ("rows_r", [P, H1_TILES, P], F32R), ("wa_rest", [P, 8688 - 3328 - 4096 - 2 * H1_TILES * P], F32)])
        kexp = wa[:, 0:3840].rearrange("p (z h k) -> p z h k", z=2, h=H0)
        prob = wa[:, 3840:7680].rearrange("p (z h k) -> p z h k", z=2, h=H0)
        craw = wa[0:LK, 7680:7936].rearrange("p (z d) -> p z d", z=2)
        xc = wa[:, 7936:8432].rearrange("p (z c) -> p z c", z=2)
        qs = wa[:, 8432:8688].rearrange("p (z q) -> p z q", z=2)
        mrow = wa[:, 0:H0 * LQ].bitcast(BF16).rearrange("p (z c) -> p z c", z=2)
        vpad = wa[0:LK, 2048:3328].rearrange("p (z g c) -> p z g c", z=2, g=4)
        opad = sb("opad", [LK, 160])
        qexp = area(0, 4096).rearrange("p (z h q) -> p z h q", z=2, h=H0)
        probT = area(4096, 4096)[0:LK].rearrange("p (z h q) -> p z h q", z=2, h=H0)
        ktS = area(8192, 240).rearrange("p (z k) -> p z k", z=2)
        qsc = area(8432, 256).rearrange("p (z q) -> p z q", z=2)
        rden = area(8688, 256).rearrange("p (z q) -> p z q", z=2)
        oT = area(8944, 256).rearrange("p (z q) -> p z q", z=2)
        xr = area(9200, 256).rearrange("p (z d) -> p z d", z=2)
        mparts = sb("mparts", [P, 2, 2, LQ], BF16)
        silu = area(0, 1024).rearrange("p (j c) -> p j c", j=DN_TILES)
        hT = area(1024, 2048).rearrange("p (z j c) -> p z j c", z=2, j=DN_TILES)
        q2 = area(1024, 2048).rearrange("p (z h q) -> p z h q", z=2, h=H1)
        s1 = area(3072, 1920).rearrange("p (z h k) -> p z h k", z=2, h=H1)
        e1 = area(4992, 1920).rearrange("p (z h k) -> p z h k", z=2, h=H1)
        a1 = area(6912, 1920).rearrange("p (z h k) -> p z h k", z=2, h=H1)
        a1T = area(8832, 2048)[0:LK].rearrange("p (z h q) -> p z h q", z=2, h=H1)
        vw = area(10880, 2048)[0:LK].rearrange("p (z h d) -> p z h d", z=2, h=H1)
        cS = area(12928, 240).rearrange("p (z k) -> p z k", z=2)
        d8 = sb("d8", [P, 2, 6, H1])
        h1 = wa[:, 0:1024].rearrange("p (z c) -> p z c", z=2)
        b2blk = wa[:, 1024:1536].rearrange("p (s d) -> p s d", s=SEQS)
        yacc = wa[:, 1536:2048].rearrange("p (s d) -> p s d", s=SEQS)
        hg = area(2048, 2048).rearrange("p (m c) -> p m c", m=H1_TILES)
        expert_rows = wa[:, 7424:7936].rearrange("p (m c) -> p m c", m=H1_TILES)
        lg = small[:, 1, 0:P].rearrange("p (b e) -> p b e", b=NB)
        mx8 = small[:, 1, P:2 * P].rearrange("p (b e) -> p b e", b=NB)
        ix8 = sb("ix8", [P, NB, 8], U32)
        rt = sb("rt", [P, 6, NB])
        u1s = small[:, 2, 0:P].rearrange("p (b h) -> p b h", b=NB)
        bias_rows = small[:, 3, :].rearrange("p (i d) -> p i d", i=2)
        oh = small[:, 0, :].rearrange("p (j b e) -> p j b e", j=2, b=NB)
        mscratch = nc.dram_tensor("mscratch", (2, NB, H0, LQ), BF16, kind="Internal").ap()

        def banks(a, n, parts=P):
            return psum[0:parts, a:a + n, :]

        keep = psum[:, BANK_KEEP, :]
        logits0 = keep[:, 0:128].rearrange("p (b e) -> p b e", b=NB)
        u1 = keep[:, 128:256].rearrange("p (b e) -> p b e", b=NB)
        logits1 = keep[:, 256:384].rearrange("p (b e) -> p b e", b=NB)
        tail_ps = psum[:, BANK_TAIL, 0:LQ]

        ld_first, ld_w, ld_late, ld_ctx = sem("ld_first"), sem("ld_w"), sem("ld_late"), [sem("ld_ctx0"), sem("ld_ctx1")]
        ld_m = [sem("ld_m0"), sem("ld_m1")]
        ld_x = [sem(f"ld_x{g}") for g in range(X_GROUPS)]
        consts_set = sem("consts_set")
        w0_ps, w0_sb = sem("w0_ps"), sem("w0_sb")
        wt_ps, wt_act, wt_dve = sem("wt_ps"), sem("wt_act"), sem("wt_dve")
        f_dve, f_pe, mlp_pe, mlp_act, temp_dve, l1_pe, l1_dve = (
            sem(n) for n in ("f_dve", "f_pe", "mlp_pe", "mlp_act", "temp_dve", "l1_pe", "l1_dve"))
        ln0_st, ln0_ag, ln0_eps, ln0_r = sem("ln0_st"), sem("ln0_ag"), sem("ln0_eps"), sem("ln0_r")
        a_xn, a_tps, a_xc, a_ctx, a_qkv, a_q, a_k, a_v, a_kexp, a_qkeep = (
            sem("a_" + n) for n in ("xn", "tps", "xc", "ctx", "qkv", "q", "k", "v", "kexp", "qkeep"))
        a_nkeep = sem("a_nkeep")
        a_s, a_max, a_neg, a_exp, a_bn = (sem("a_" + n) for n in ("s", "max", "neg", "exp", "bn"))
        m_store = sem("m_store")
        b_kt, b_v, b_qsc, b_qexp, b_s, b_exp, b_od, b_rden, b_oT, b_y, b_x1, b_x = (
            sem("b_" + n) for n in ("kt", "v", "qsc", "qexp", "s", "exp", "od", "rden", "oT", "y", "x1", "x"))
        tails = {ph: {n: sem(f"{ph}t_{n}") for n in ("bn", "ag", "pool", "r", "xn", "xr", "tp", "ev", "lg", "keep")}
                 for ph in "bcd"}
        mrow_zero = sem("mrow_zero")
        r_dve, r_act, gates_set = sem("r_dve"), sem("r_act"), sem("gates_set")
        b_hi, b_lo, c_gate = sem("b_hi"), sem("b_lo"), sem("c_gate")
        x_rounded = {ph: sem(f"{ph}_x_rounded") for ph in "bd"}
        c_up, c_silu, c_h, c_dn, c_acc = (sem("c_" + n) for n in ("up", "silu", "h", "dn", "acc"))
        d_cs, d_q, d_q2, d_s, d_sm, d_max, d_mu, d_sh, d_exp, d_rs, d_a, d_tp, d_aT, d_vwp, d_vw, d_y, d_x = (
            sem("d_" + n) for n in ("cs", "q", "q2", "s", "sm", "max", "mu", "sh", "exp", "rs", "a", "tp",
                                    "aT", "vwp", "vw", "y", "x"))
        b_xb, d_xb = sem("b_xb"), sem("d_xb")
        d_u, d_chi, rounded, halved = sem("d_u"), sem("d_chi"), sem("rounded"), sem("halved")
        e_gt, e_gts, e_h, e_g, e_gm, e_gps, e_hg, e_y, e_acc = (
            sem("e_" + n) for n in ("gt", "gts", "h", "g", "gm", "gps", "hg", "y", "acc"))
        e_out, e_b2, e_gm1 = sem("e_out"), sem("e_b2"), sem("e_gm1")

        N_FIRST, N_W, N_LATE = 13, 15, 8 + NB
        block = ctx.enter_context(nc.Block())

        @block.sync
        def _(sp):
            first = [
                (cst[:, 0:cols["sel"][1]], t["consts"][:, 0:cols["sel"][1]]),
                (nat0[:, 0, :], t["L0_xattn_Wq"]),
                (nat0[:, 1, :], t["L0_xattn_Wk"]),
                (nat0[:, 2, :], t["L0_xattn_Wv"]),
                (nat0[:, 3, :], t["L0_xattn_Wo"]),
                (bq0, t["L0_xattn_bq"].rearrange("(p c) -> p c", c=1)),
                (bk0, t["L0_xattn_bk"].rearrange("(p c) -> p c", c=1)),
                (bv0, t["L0_xattn_bv"].rearrange("(p c) -> p c", c=1)),
                (bo0[:, :], t["L0_xattn_bo"].rearrange("(a d) -> a d", a=1)),
                (wsm[0:DH0, 0:3], t["L0_xattn_w1"]),
                (wsm[0:DH0, 3:3 + DH0], t["L0_xattn_w2"]),
                (wsm[0:1, 3 + DH0:3 + 2 * DH0], t["L0_xattn_w3"]),
                (nat0[0:NE, 4, :], t["L0_ffn_w_router"]),
            ]
            assert len(first) == N_FIRST
            for dst, src in first:
                sp.dma_start(dst, src, allow_slow_non_contiguous=True).then_inc(ld_first, 16)

            def load_ctx(b, z):
                reused(sp, a_tps, b)
                sp.dma_start(craw[:, z, :], t["ctx_1024"][b]).then_inc(ld_ctx[z], 16)

            for b in range(2):
                load_ctx(b, b)
            small_loads = [
                (b1c[0:DH0], t["L0_xattn_b1"].rearrange("(p c) -> p c", c=1)),
                (b2c[0:DH0], t["L0_xattn_b2"].rearrange("(p c) -> p c", c=1)),
                (b3c, t["L0_xattn_b3"].rearrange("(a c) -> a c", a=1).to_broadcast([P, 1])),
                (nscale, t["L0_ffn_norm_scale"].rearrange("(p c) -> p c", c=1)),
                (bqk1[:, 0], t["L1_xattn_bq"].rearrange("h e -> e h")),
                (bqk1[:, 1], t["L1_xattn_bk"].rearrange("h e -> e h")),
                (bqk1[:, 2], t["L1_xattn_bv"].rearrange("h e -> e h")),
                (bc1[:, :], t["L1_xattn_bc"].rearrange("(a d) -> a d", a=1)),
            ]
            up_rows = t["L0_ffn_w_up"].rearrange("e (t p) d -> p (e t) d", p=P)
            large_loads = [
                (upN[:, 0:16], up_rows[:, 0:16]),
                (upN[:, 16:32], up_rows[:, 16:32]),
                (dnN, t["L0_ffn_w_down"].rearrange("e p h -> p e h")),
                (l1N[:, 0], t["L1_xattn_Wq"].rearrange("h e d -> e h d")),
                (l1N[:, 1], t["L1_xattn_Wk"].rearrange("h e d -> e h d")),
                (l1N[:, 2], t["L1_xattn_Wv"].rearrange("h e d -> e h d")),
                (wcN, t["L1_xattn_Wc"].rearrange("o (h e) -> o h e", h=H1)),
            ]
            assert len(small_loads) + len(large_loads) == N_W
            for dst, src in small_loads:
                sp.dma_start(dst, src, allow_slow_non_contiguous=True).then_inc(ld_w, 16)
            for b in range(2, 4):
                for dst, src in large_loads[2 * (b - 2):2 * (b - 1)]:
                    sp.dma_start(dst, src).then_inc(ld_w, 16)
                load_ctx(b, b % 2)
            for dst, src in large_loads[4:]:
                sp.dma_start(dst, src).then_inc(ld_w, 16)
            with sp.Fori(2, NB // 2) as i:
                for z in range(2):
                    load_ctx(i * 2 + z, z)

            late = [
                (cst[:, slice(*cols["window"])], t["consts"][:, slice(*cols["window"])]),
                (router1[:, :], t["L1_ffn_router_w"]),
                (rb1[:, :], t["L1_ffn_router_b"].rearrange("(a d) -> a d", a=1).to_broadcast([P, NE])),
                (ew1[:, :, :], t["L1_ffn_W1"].rearrange("n d e -> d n e")),
                (ew2[0:F1], t["L1_ffn_W2"].rearrange("(m j) f d -> j f m d", j=2)[0]),
                (ew2[F1:P], t["L1_ffn_W2"].rearrange("(m j) f d -> j f m d", j=2)[1]),
                (b1e[0:F1], t["L1_ffn_b1"].rearrange("(m j) f -> j f m", j=2)[0]),
                (b1e[F1:P], t["L1_ffn_b1"].rearrange("(m j) f -> j f m", j=2)[1]),
            ] + [(b2rows[NE * b:NE * (b + 1), :], t["L1_ffn_b2"]) for b in range(NB)]
            assert len(late) == N_LATE
            for dst, src in late:
                sp.dma_start(dst, src, allow_slow_non_contiguous=True).then_inc(ld_late, 16)

            sp.wait_ge(m_store, 32)
            sp.dma_start(expert_rows.rearrange("p m c -> p (m c)"), t["consts"][:, slice(*cols["expert_rows"])]
                         ).then_inc(ld_late, 16)
            sp.wait_ge(mrow_zero, 1)

            def load_m(b, z):
                reused(sp, b_s, b, 2)
                sp.dma_start(mrow[0:2, z, :], mscratch[:, b].rearrange("c h q -> c (h q)")).then_inc(ld_m[z], 16)

            software_pipeline(sp, [(0, load_m)])

            with sp.Fori(0, GROUPS) as g:
                sp.wait_ge(e_acc, g + 1)
                sp.dma_start(out[bass.ds(g * SEQS, SEQS)].rearrange("b t d -> t b d"), yacc[:, :, :]).then_inc(e_out, 16)
            sp.wait_ge(e_out, 16 * GROUPS)

        def weight_groups():
            groups = []
            for g in range(NE * UP_TILES // 4):
                groups.append((upT[:, 4 * g:4 * g + 4, :], [("turn", upN[:, 4 * g + i, :]) for i in range(4)]))
            for g in range(NE * DN_TILES // 4):
                groups.append((dnT[:, 4 * g:4 * g + 4, :],
                               [("turn", dnN[:, 2 * g + i // 2, (i % 2) * P:(i % 2 + 1) * P]) for i in range(4)]))
            for g in range(H1 // 4):
                groups.append((wcT[:, 4 * g:4 * g + 4, :], [("turn", wcN[:, 4 * g + i, :]) for i in range(4)]))
            for g in range(H1 // 4):
                groups.append((qk1[:, 4 * g:4 * g + 4, :],
                               [("prod", l1N[:, 0, 4 * g + i, :], l1N[:, 1, 4 * g + i, :]) for i in range(4)]))
            for g in range(H1 // 4):
                groups.append((vo1[:, 4 * g:4 * g + 4, :],
                               [("prod", l1N[:, 2, 4 * g + i, :], wcT[:, 4 * g + i, :]) for i in range(4)]))
            return groups

        WC_GROUPS = range(12, 14)
        N_GROUPS = 18
        RING_W = 4
        ACT_GROUPS = 9

        def weight_copies(ns, eng, groups):
            for g in groups:
                eng.wait_ge(wt_ps, g + 1)
                src = psum[:, g % RING_W, :].rearrange("p (i d) -> p i d", d=D)
                if g < ACT_GROUPS:
                    ns.copy(weight_groups()[g][0], src).then_inc(wt_act, 1)
                else:
                    ns.tensor_copy(weight_groups()[g][0], src).then_inc(wt_dve, 1)

        def group_copied(eng, g):
            if g < ACT_GROUPS:
                eng.wait_ge(wt_act, g + 1)
            else:
                eng.wait_ge(wt_dve, g - ACT_GROUPS + 1)

        T_CLIPPED, T_SCALED, T_PARTS = 2, 3, 7
        ROUTE_SLOT = 1
        STATS_SLOTS, NORM_SLOTS, TURN_SLOTS, LOGITS_SLOTS = (range(a, a + SEQS) for a in (1, 2, 3, 4))
        R_DIFF, R_COUNT = 4, 13

        @block.scalar
        def _(act):
            for g in range(X_GROUPS):
                act.dma_start(x[:, 4 * g:4 * g + 4, :], t["x"][4 * g:4 * g + 4].rearrange("b t d -> t b d")
                              ).then_inc(ld_x[g], 16)

            act.wait_ge(ld_first, 16 * N_FIRST)

            def a_project(b, z):
                act.wait_ge(a_qkv, b + 1)
                reused(act, a_s, b, 2)
                reused(act, a_qkeep, b)
                nc.scalar.activation(qs[:, z, :], psum[:, 1, 0:LQ], ACT.Identity, bias=bq0,
                                     accum_out=qsum[:, bass.ds(b, 1)]).then_inc(a_q, 1)
                nc.scalar.activation(kT[:, b, :], psum[:, 1, LQ:LQ + LK], ACT.Identity, bias=bk0,
                                     accum_out=ksum[:, bass.ds(b, 1)]).then_inc(a_k, 1)

            def a_turned(b, z):
                act.wait_ge(a_tps, b + 1)
                reused(act, a_qkv, b)
                reused(act, a_ctx, b)
                nc.scalar.copy(xc[:, z, :], psum[:, 0, 0:LQ + LK]).then_inc(a_xc, 1)

            def a_values(b, z):
                act.wait_ge(a_qkv, b + 1)
                nc.scalar.copy(v0[:, b, :], psum[0:LK, 2, 0:D]).then_inc(a_v, 1)

            def a_softmax(half):
                def run(b, z):
                    act.wait_ge(a_neg, b * 2 + half + 1)
                    if half == 0:
                        reused(act, a_bn, b, 2)
                    for h in range(HALF0):
                        hh = half * HALF0 + h
                        e = nc.scalar.activation(
                            prob[:, z, hh, :], psum[:, 3 + 2 * half + h // 4, (h % 4) * LK:(h % 4 + 1) * LK],
                            ACT.Exp, bias=negmax[:, z, hh:hh + 1])
                    e.then_inc(a_exp, 1)
                return run

            software_pipeline(act, [(1, a_turned), (3, a_softmax(0)), (3, a_softmax(1)), (1, a_project), (1, a_values)],
                              peel=6)

            weight_copies(nc.scalar, act, range(ACT_GROUPS))

            act.wait_ge(ld_w, 16 * N_W)
            act.wait_ge(mlp_pe, 1)
            nc.scalar.activation(small[0:DH0, 6, :], psum[0:DH0, 4, 0:BH], ACT.Gelu, bias=b1c[0:DH0]
                                 ).then_inc(mlp_act, 1)
            act.wait_ge(mlp_pe, 2)
            nc.scalar.activation(small[0:DH0, 7, :], psum[0:DH0, 5, 0:BH], ACT.Gelu, bias=b2c[0:DH0]
                                 ).then_inc(mlp_act, 1)
            act.wait_ge(temp_dve, T_CLIPPED)
            nc.scalar.activation(invt[:, :], small[:, 1, :], ACT.Exp, scale=-1.0).then_inc(mlp_act, 1)
            act.wait_ge(temp_dve, T_PARTS)
            for half in range(2):
                act.dma_start(mscratch[:, 8 * half:8 * half + 8].rearrange("c b h q -> (b h) c q"),
                              mparts[:, half, :, :]).then_inc(m_store, 16)

            def b_softmax(half):
                def run(b, z):
                    act.wait_ge(b_s, b * 2 + half + 1)
                    if half == 0:
                        reused(act, b_od, b)
                    nc.scalar.activation(
                        probT[:, z, half * HALF0:(half + 1) * HALF0, :].rearrange("p h q -> p (h q)"),
                        psum[0:LK, 2 * half:2 * half + 2, :].rearrange("p a c -> p (a c)"), ACT.Exp
                    ).then_inc(b_exp, 1)
                return run

            def tail_evict(ph):
                s = tails[ph]

                def run(b, z):
                    act.wait_ge(s["tp"], b + 1)
                    reused(act, s["keep"], b)
                    reused(act, s["lg"], b)
                    if ph == "b":
                        nc.scalar.mul(xnT[:, z, :], tail_ps, nscale).then_inc(s["ev"], 1)
                    else:
                        nc.scalar.copy(xnT[:, z, :], tail_ps).then_inc(s["ev"], 1)
                return run

            def b_split(b, z):
                tiles = bass.ds(b * 2, 2)
                nc.scalar.copy(up_hi[:, tiles, :], upT[:, tiles, :]).then_inc(b_hi, 1)

            act.wait_ge(l1_pe, 2)
            act.wait_ge(wt_dve, N_GROUPS - ACT_GROUPS)
            software_pipeline(act, [(5, tail_evict("b")), (1, b_softmax(0)), (1, b_softmax(1)), (1, b_split)], peel=8)

            def route_exp(n):
                act.wait_ge(r_dve, R_DIFF + n * R_COUNT)
                nc.scalar.activation(rt[:, 1, :], rt[:, 0, :], ACT.Exp).then_inc(r_act, 1)

            def c_slot(g, e):
                for j in range(DN_TILES):
                    v = (g * NE + e) * DN_TILES + j
                    act.wait_ge(c_gate, v + 1)
                    nc.scalar.activation(silu[:, j, :], psum[:, 2 * j + 1, :], ACT.Silu).then_inc(c_silu, 1)
                if isinstance(g, int) and g == 0:
                    if e == ROUTE_SLOT:
                        route_exp(0)
                    if e == NE - 1:
                        nc.scalar.copy(vo_hi[:, :, :], vo1[:, :, :]).then_inc(rounded, 1)
                        act.wait_ge(ld_late, 16 * (N_LATE + 1))
                        nc.scalar.copy(w1_hi[:, :], ew1.rearrange("p n f -> p (n f)")).then_inc(rounded, 1)
                        nc.scalar.copy(rows_r[:, :, :], expert_rows).then_inc(rounded, 1)
                elif e in TURN_SLOTS:
                    sq = e - TURN_SLOTS[0]
                    tail_evict("c")((g - 1) * SEQS + sq, sq % 2)

            slots(act, c_slot, NE)
            for sq in range(SEQS):
                tail_evict("c")((GROUPS - 1) * SEQS + sq, sq % 2)

            def d_vw_copy(b, z):
                act.wait_ge(d_vwp, b + 1)
                reused(act, d_y, b)
                nc.scalar.copy(vw[:, z].rearrange("p h d -> p (h d)"),
                               psum[0:LK, 4:6, :].rearrange("p a c -> p (a c)")).then_inc(d_vw, 1)

            def d_softmax(b, z):
                act.wait_ge(d_sh, b + 1)
                reused(act, d_a, b)
                for h in range(H1):
                    e = nc.scalar.activation(e1[:, z, h, :], s1[:, z, h, :], ACT.Exp, bias=d8[:, z, 3, h:h + 1],
                                             accum_out=d8[:, z, 4, h:h + 1])
                e.then_inc(d_exp, 1)

            def d_aT_copy(b, z):
                act.wait_ge(d_tp, b + 1)
                nc.scalar.copy(a1T[:, z].rearrange("p h q -> p (h q)"),
                               psum[0:LK, 4:6, :].rearrange("p a c -> p (a c)")).then_inc(d_aT, 1)

            software_pipeline(act, [(6, tail_evict("d")), (3, d_vw_copy), (1, d_softmax), (3, d_aT_copy)], peel=8)
            route_exp(1)

            def e_slot(g, m):
                v = g * H1_TILES + m
                act.wait_ge(e_h, v + 1)
                if not isinstance(v, int) or v >= 2:
                    act.wait_ge(e_hg, v - 1)
                nc.scalar.activation(h1[:, m % 2, :], psum[:, m % 2, :], ACT.Gelu, bias=b1e[:, m:m + 1]
                                     ).then_inc(e_g, 1)

            slots(act, e_slot, H1_TILES)

        @block.gpsimd
        def _(pool):
            nc.gpsimd.memset(eps[:, 0:1], -0.5)
            nc.gpsimd.memset(eps[:, 1:2], LN_EPS)
            nc.gpsimd.memset(eps[:, 2:3], RMS_EPS).then_inc(consts_set, 1)
            nc.gpsimd.memset(onesb[:, :], 0.0).then_inc(consts_set, 1)
            nc.gpsimd.memset(opad[:, :], 0.0).then_inc(consts_set, 1)
            pool.wait_ge(consts_set, 4)
            nc.gpsimd.memset(onesb[0:2, :], 1.0)
            nc.gpsimd.memset(opad.rearrange("p (i c) -> p i c", c=40)[:, :, 0:DK0], 1.0).then_inc(consts_set, 1)
            half_power = eps[:, 0:1]

            for g in range(X_GROUPS):
                of = slice(4 * g, 4 * g + 4)
                pool.wait_ge(ln0_ag, g + 1)
                nc.gpsimd.tensor_scalar(rstd0[:, of], mean0[:, of, 1], LN_EPS, None, ALU.add).then_inc(ln0_eps, 1)
                pool.wait_ge(ln0_eps, g + 1)
                nc.gpsimd.tensor_tensor(rstd0[:, of], rstd0[:, of], half_power.to_broadcast([P, 4]), ALU.pow
                                        ).then_inc(ln0_r, 1)

            pool.wait_ge(ld_first, 16 * N_FIRST)

            def a_keep_context(b, z):
                pool.wait_ge(a_xc, b + 1)
                nc.gpsimd.tensor_copy(ctxT[:, b, :], xc[:, z, LQ:LQ + LK]).then_inc(a_ctx, 1)

            def a_keep(b, z):
                pool.wait_ge(a_q, b + 1)
                nc.gpsimd.tensor_copy(qT[:, b, :], qs[:, z, :]).then_inc(a_qkeep, 1)

            def a_keep_max(b, z):
                pool.wait_ge(a_neg, b * 2 + 2)
                nc.gpsimd.tensor_copy(rowneg[:, bass.ds(b * H0, H0)], negmax[:, z, :]).then_inc(a_nkeep, 1)

            def a_expand(b, z):
                pool.wait_ge(a_k, b + 1)
                reused(pool, a_s, b, 2)
                nc.gpsimd.tensor_tensor(kexp[:, z], kT[:, b, :].unsqueeze(1).to_broadcast([P, H0, LK]),
                                        headscale.unsqueeze(2).to_broadcast([P, H0, LK]), ALU.mult
                                        ).then_inc(a_kexp, 1)

            software_pipeline(pool, [(1, a_keep_context), (1, a_expand), (1, a_keep), (3, a_keep_max)], peel=6)

            def tail_rstd(ph):
                s, per = tails[ph], 6 if ph == "b" else 2

                def run(b, z):
                    pool.wait_ge(s["ag"], b + 1)
                    reused(pool, s["xr" if ph == "b" else "xn"], b)
                    r = [rstd[:, z, i:i + 1] for i in range(4)]
                    var = mv[:, z, 1:2]
                    nc.gpsimd.tensor_tensor(r[0], var, eps[:, 1:2], ALU.add).then_inc(s["pool"], 1)
                    pool.wait_ge(s["pool"], b * per + 1)
                    nc.gpsimd.tensor_tensor(r[1], r[0], half_power, ALU.pow).then_inc(s["pool"], 1)
                    if ph == "b":
                        pool.wait_ge(s["pool"], b * per + 2)
                        nc.gpsimd.tensor_tensor(r[2], r[1], r[1], ALU.mult).then_inc(s["pool"], 1)
                        pool.wait_ge(s["pool"], b * per + 3)
                        nc.gpsimd.tensor_tensor(r[0], r[2], var, ALU.mult).then_inc(s["pool"], 1)
                        pool.wait_ge(s["pool"], b * per + 4)
                        nc.gpsimd.tensor_tensor(r[2], r[0], eps[:, 2:3], ALU.add).then_inc(s["pool"], 1)
                        pool.wait_ge(s["pool"], b * per + 5)
                        nc.gpsimd.tensor_tensor(r[3], r[2], half_power, ALU.pow).then_inc(s["pool"], 1)
                return run

            def tail_keep(ph):
                s = tails[ph]

                def run(b, z):
                    pool.wait_ge(s["ev"], b + 1)
                    if ph != "c":
                        nc.gpsimd.tensor_copy(x_hi[:, b, :], xnT[:, z, :]).then_inc(x_rounded[ph], 1)
                        pool.wait_ge(x_rounded[ph], b + 1)
                        nc.gpsimd.tensor_tensor(x_lo[:, b, :], xnT[:, z, :], x_hi[:, b, :].bitcast(F32), ALU.subtract
                                                ).then_inc(s["keep"], 1)
                    else:
                        nc.gpsimd.tensor_copy(xT[:, b, :], xnT[:, z, :]).then_inc(s["keep"], 1)
                return run

            def b_stage(b, z):
                reused(pool, b_s, b, 2)
                nc.gpsimd.tensor_copy(ktS[:, z, :], kT[:, b, :]).then_inc(b_kt, 1)
                reused(pool, b_od, b)
                nc.gpsimd.tensor_copy(
                    vpad[:, z].rearrange("p g (i c) -> p g i c", c=40)[:, :, :, 0:DK0],
                    v0[:, b, :].rearrange("p (g i j) -> p g i j", g=4, j=DK0)).then_inc(b_v, 1)

            pool.wait_ge(a_s, 2 * NB)
            pool.wait_ge(a_bn, 2 * NB)
            pool.wait_ge(a_xc, NB)
            nc.gpsimd.memset(wa[:, 0:H0 * LQ], 0.0).then_inc(mrow_zero, 1)
            nc.gpsimd.memset(vpad[:, :, :, :], 0.0).then_inc(consts_set, 1)
            pool.wait_ge(consts_set, 6)
            pool.wait_ge(l1_pe, 2)
            def b_split(b, z):
                tiles = bass.ds(b * 2, 2)
                pool.wait_ge(b_hi, b + 1)
                nc.gpsimd.tensor_tensor(up_lo[:, tiles, :], upT[:, tiles, :], up_hi[:, tiles, :].bitcast(F32), ALU.subtract
                                        ).then_inc(b_lo, 1)

            software_pipeline(pool, [(0, b_stage), (3, tail_rstd("b")), (2, b_split), (5, tail_keep("b"))], peel=8)

            def c_tails(g):
                for stage, sq in ((tail_rstd, 0), (tail_rstd, 1), (tail_rstd, 2), (tail_keep, 0), (tail_rstd, 3),
                                  (tail_keep, 1), (tail_keep, 2), (tail_keep, 3)):
                    stage("c")(g * SEQS + sq, sq % 2)

            c_tails(0)
            pool.wait_ge(rounded, 3)
            nc.gpsimd.tensor_tensor(vo_lo[:, :, :], vo1[:, :, :], vo_hi[:, :, :].bitcast(F32), ALU.subtract
                                    ).then_inc(halved, 1)
            nc.gpsimd.tensor_tensor(w1_lo[:, :], ew1.rearrange("p n f -> p (n f)"), w1_hi[:, :].bitcast(F32), ALU.subtract
                                    ).then_inc(halved, 1)
            with pool.Fori(1, GROUPS) as g:
                c_tails(g)

            def d_stage(b, z):
                reused(pool, d_vwp, b)
                nc.gpsimd.tensor_copy(c_hi[:, z, :], ctxT[:, b, :]).then_inc(d_chi, 1)
                nc.gpsimd.tensor_copy(cS[:, z, :], ctxT[:, b, :]).then_inc(d_chi, 1)
                pool.wait_ge(d_chi, b * 2 + 2)
                nc.gpsimd.tensor_tensor(c_lo[:, z, :], cS[:, z, :], c_hi[:, z, :].bitcast(F32), ALU.subtract
                                        ).then_inc(d_cs, 1)

            software_pipeline(pool, [(2, d_stage), (4, tail_rstd("d")), (6, tail_keep("d"))], peel=8)

        @block.vector
        def _(dve):
            nc.vector.memset(ones[:, :], 1.0).then_inc(consts_set, 1)
            bn0 = wa[:, 0:NB * 6].rearrange("p (b s) -> p b s", b=NB)
            for g in range(X_GROUPS):
                dve.wait_ge(ld_x[g], 16)
                for b in range(4 * g, 4 * g + 4):
                    i = nc.vector.bn_stats(bn0[:, b, :], x[:, b, :])
                i.then_inc(ln0_st, 1)
                dve.wait_ge(ln0_st, g + 1)
                for b in range(4 * g, 4 * g + 4):
                    i = nc.vector.bn_aggr(mean0[:, b, :], bn0[:, b, :])
                i.then_inc(ln0_ag, 1)
            dve.wait_ge(w0_ps, 1)
            nc.vector.tensor_copy(w4T[:, :, :], psum[:, 0, :].rearrange("p (i d) -> p i d", i=4)).then_inc(w0_sb, 1)
            dve.wait_ge(w0_ps, 2)
            nc.vector.tensor_copy(w1T[:, :], psum[0:3, 4, 8:8 + DH0]).then_inc(w0_sb, 1)
            nc.vector.tensor_copy(w2T[:, :], psum[0:DH0, 4, 128:128 + DH0]).then_inc(w0_sb, 1)
            nc.vector.tensor_copy(w3c[:, :], psum[0:DH0, 4, 256:256 + P]).then_inc(w0_sb, 1)
            nc.vector.tensor_copy(routerT[:, :], psum[:, 4, 0:NE]).then_inc(w0_sb, 1)
            dve.wait_ge(ln0_r, 1)

            carriers = []

            def carrier():
                n = len(carriers)
                carriers.append(sem(f"carried{n}"))

                def stats_wait(b, *waits):
                    for s, v in waits + ((carriers[n], b),):
                        if not isinstance(v, int) or v > 0:
                            dve.wait_ge(s, v)
                    nc.vector.memset(carried[:, n:n + 1], 0.0).then_inc(carriers[n], 1)
                return stats_wait

            def a_norm(b, z):
                if isinstance(b, int) and b == 1:
                    dve.wait_ge(w0_ps, 3)
                    nc.vector.tensor_copy(w1f.rearrange("p c h -> p (c h)"), psum[:, 5, 0:3 * DH0]).then_inc(w0_sb, 1)
                    nc.vector.tensor_copy(bout0[:, :], psum[0:1, 5, 256:256 + D]).then_inc(w0_sb, 1)
                reused(dve, a_tps, b)
                if isinstance(b, int) and b % 4 == 0 and b < 4 * X_GROUPS:
                    dve.wait_ge(ln0_r, b // 4 + 1 if b == 0 else X_GROUPS)
                nc.vector.tensor_scalar(xn[:, z, :], x[:, b, :], mean0[:, b, 0:1], rstd0[:, bass.ds(b, 1)],
                                        ALU.subtract, ALU.mult).then_inc(a_xn, 1)

            def a_rowmax(half):
                def run(b, z):
                    dve.wait_ge(a_s, b * 2 + half + 1)
                    if half == 0:
                        reused(dve, a_exp, b, 2)
                        reused(dve, a_nkeep, b)
                    nc.vector.tensor_reduce(
                        negmax[:, z, half * HALF0:(half + 1) * HALF0].rearrange("p (a h) -> p a h", a=2),
                        psum[:, 3 + 2 * half:5 + 2 * half, 0:4 * LK].rearrange("p a (h k) -> p a h k", k=LK),
                        AX_X, ALU.max, negate=True).then_inc(a_neg, 1)
                return run

            def a_stats(half):
                stats_wait = carrier()

                def run(b, z):
                    stats_wait(b, (a_exp, b * 2 + half + 1))
                    for h in range(half * HALF0, (half + 1) * HALF0):
                        s = nc.vector.bn_stats(bnout[:, bass.ds(b * H0 + h, 1), :].rearrange("p a s -> p (a s)"),
                                               prob[:, z, h, :])
                    s.then_inc(a_bn, 1)
                return run

            software_pipeline(dve, [(0, a_norm), (3, a_rowmax(0)), (4, a_stats(1)), (3, a_rowmax(1)), (3, a_stats(0))], peel=6)

            dve.wait_ge(a_nkeep, NB)
            dve.wait_ge(a_k, NB)
            dve.wait_ge(a_bn, 2 * NB)
            mean_e, m2_e, mean_o, m2_o = (bnout[:, :, i] for i in (1, 2, 4, 5))
            HALF_KEYS = LK // 2
            nc.vector.tensor_tensor(small[:, 0, :], mean_e, mean_o, ALU.add)
            nc.vector.tensor_tensor(small[:, 1, :], mean_e, mean_o, ALU.subtract)
            nc.vector.tensor_tensor(small[:, 5, 0:NB], qsum[:, :], ksum[:, :], ALU.mult).then_inc(f_dve, 1)
            dve.wait_ge(f_dve, 1)
            nc.vector.tensor_tensor(small[:, 2, :], small[:, 0, :], small[:, 0, :], ALU.mult)
            nc.vector.tensor_tensor(small[:, 3, :], small[:, 1, :], small[:, 1, :], ALU.mult)
            nc.vector.tensor_tensor(small[:, 4, :].rearrange("p (b h) -> p b h", b=NB),
                                    small[:, 5, 0:NB].unsqueeze(2).to_broadcast([P, NB, H0]),
                                    headmask.unsqueeze(1).to_broadcast([P, NB, H0]), ALU.mult).then_inc(f_dve, 1)
            dve.wait_ge(f_dve, 2)
            nc.vector.scalar_tensor_tensor(out=small[:, 1, :], in0=small[:, 3, :], scalar=HALF_KEYS / 2.0, in1=m2_e,
                                           op0=ALU.mult, op1=ALU.add)
            nc.vector.reciprocal(small[:, 0, :], small[:, 2, :]).then_inc(f_dve, 1)
            dve.wait_ge(f_dve, 3)
            nc.vector.tensor_tensor(small[:, 3, :], small[:, 1, :], m2_o, ALU.add).then_inc(f_dve, 1)
            dve.wait_ge(f_dve, 4)
            nc.vector.scalar_tensor_tensor(out=small[:, 2, :], in0=small[:, 3, :],
                                           scalar=1.0 / ((LK - 1) * HALF_KEYS ** 2), in1=small[:, 0, :],
                                           op0=ALU.mult, op1=ALU.mult).then_inc(f_dve, 1)

            dve.wait_ge(ld_w, 16 * N_W)
            nc.vector.tensor_tensor(bqk[:, :], bqk1[:, 0], bqk1[:, 1], ALU.mult).then_inc(l1_dve, 1)
            weight_copies(nc.vector, dve, range(ACT_GROUPS, N_GROUPS - 3))

            dve.wait_ge(mlp_pe, 3)
            nc.vector.tensor_scalar(small[:, 0, :], psum[:, 4, 256:512], b3c, LOG_T_MIN, ALU.add, ALU.max
                                    ).then_inc(temp_dve, 1)
            dve.wait_ge(temp_dve, 1)
            nc.vector.tensor_scalar(small[:, 1, :], small[:, 0, :], LOG_T_MAX, math.log(2.0), ALU.min, ALU.add
                                    ).then_inc(temp_dve, 1)
            dve.wait_ge(mlp_act, 3)
            nc.vector.scalar_tensor_tensor(out=small[:, 2, :], in0=rowneg[:, :], scalar=math.sqrt(DK0),
                                           in1=invt[:, :], op0=ALU.mult, op1=ALU.mult).then_inc(temp_dve, 1)
            nc.vector.tensor_tensor(small[:, 3, :].rearrange("p (b h) -> p b h", b=NB),
                                    invt.rearrange("p (b h) -> p b h", b=NB),
                                    headmask.unsqueeze(1).to_broadcast([P, NB, H0]), ALU.mult).then_inc(temp_dve, 1)
            dve.wait_ge(temp_dve, 4)
            nc.vector.tensor_reduce(invtT[:, :], small[:, 3, :].rearrange("p (b h) -> p b h", b=NB), AX_X, ALU.add
                                    ).then_inc(temp_dve, 1)
            dve.wait_ge(mlp_pe, 4)
            turned = psum[:, 5, 0:BH].rearrange("p (a q) -> p a q", a=2)
            nc.vector.tensor_copy(mparts[:, :, 0, :], turned).then_inc(temp_dve, 1)
            dve.wait_ge(temp_dve, 6)
            nc.vector.tensor_tensor(mparts[:, :, 1, :], turned, mparts[:, :, 0, :], ALU.subtract
                                    ).then_inc(temp_dve, 1)
            weight_copies(nc.vector, dve, range(N_GROUPS - 3, N_GROUPS))
            dve.wait_ge(l1_pe, 2)
            nc.vector.tensor_copy(cvec[:, :], keep[:, 384:384 + H1]).then_inc(l1_dve, 1)
            nc.vector.tensor_copy(uvec[:, :], keep[:, 384 + H1:384 + 2 * H1]).then_inc(l1_dve, 1)
            nc.vector.tensor_copy(ubias[:, :], psum[:, 6, 2 * H1:3 * H1]).then_inc(l1_dve, 1)
            nc.vector.tensor_copy(bout1[:, :], psum[0:1, 6, 256:256 + D]).then_inc(l1_dve, 1)

            def b_scale(b, z):
                reused(dve, b_qexp, b, 2)
                nc.vector.tensor_scalar(qsc[:, z, :], qT[:, b, :], invtT[:, bass.ds(b, 1)], None, ALU.mult
                                        ).then_inc(b_qsc, 1)

            def b_expand(half):
                def run(b, z):
                    dve.wait_ge(b_qsc, b + 1)
                    reused(dve, b_s, b, 2)
                    heads = slice(half * HALF0, (half + 1) * HALF0)
                    nc.vector.tensor_tensor(qexp[:, z, heads, :],
                                            qsc[:, z, :].unsqueeze(1).to_broadcast([P, HALF0, LQ]),
                                            headmask[:, heads].unsqueeze(2).to_broadcast([P, HALF0, LQ]), ALU.mult
                                            ).then_inc(b_qexp, 1)
                return run

            def b_recip(b, z):
                dve.wait_ge(b_od, b + 1)
                reused(dve, b_oT, b)
                nc.vector.reciprocal(rden[:, z, :], psum[:, 4, LQ:2 * LQ]).then_inc(b_rden, 1)

            def b_norm(b, z):
                dve.wait_ge(b_rden, b + 1)
                reused(dve, b_y, b)
                nc.vector.tensor_tensor(oT[:, z, :], psum[:, 4, 0:LQ], rden[:, z, :], ALU.mult).then_inc(b_oT, 1)

            def add_bias(layer, done):
                def run(b, z):
                    if layer == 0 and isinstance(b, int) and b == 0:
                        dve.wait_ge(l1_pe, 3)
                        nc.vector.tensor_copy(bias_rows[:, :, :], psum[:, 6, 256:512].rearrange("p (i d) -> p i d", i=2)
                                              ).then_inc(l1_dve, 1)
                        dve.wait_ge(l1_dve, 6)
                    nc.vector.tensor_tensor(x[:, b, :], x[:, b, :], bias_rows[:, 1 - layer, :], ALU.add).then_inc(done, 1)
                return run

            def b_residual(b, z):
                dve.wait_ge(b_y, b + 1)
                dve.wait_ge(b_xb, b + 1)
                nc.vector.tensor_tensor(x[:, b, :], psum[:, 5, 0:D], x[:, b, :], ALU.add).then_inc(b_x1, 1)

            def tail_stats(ph, ready):
                s, stats_wait = tails[ph], carrier()

                def run(b, z, count=None):
                    stats_wait(b, (ready, b + 1 if count is None else count), (s["ag"], b - 1))
                    nc.vector.bn_stats(bn6[:, z, :], x[:, b, :]).then_inc(s["bn"], 1)
                return run

            def tail_aggr(ph):
                s, stats_wait, pool_per = tails[ph], carrier(), 6 if ph == "b" else 2

                def run(b, z):
                    stats_wait(b, (s["bn"], b + 1), (s["pool"], (b - 1) * pool_per), (s["xn"], b - 1))
                    nc.vector.bn_aggr(mv[:, z, :], bn6[:, z, :]).then_inc(s["ag"], 1)
                return run

            def tail_norm(ph):
                s, pool_per = tails[ph], 6 if ph == "b" else 2

                def run(b, z):
                    dve.wait_ge(s["pool"], (b + 1) * pool_per)
                    reused(dve, s["tp"], b)
                    if ph == "b":
                        reused(dve, s["xr"], b)
                    i = nc.vector.tensor_scalar(xn[:, z, :], x[:, b, :], mv[:, z, 0:1], rstd[:, z, 1:2],
                                                ALU.subtract, ALU.mult)
                    i.then_inc(s["xn"], 1)
                return run

            def tail_rms(b, z):
                s = tails["b"]
                dve.wait_ge(s["xn"], b + 1)
                nc.vector.tensor_scalar(xr[:, z, :], xn[:, z, :], rstd[:, z, 3:4], None, ALU.mult).then_inc(s["xr"], 1)
                nc.vector.tensor_tensor(x[:, b, :], x[:, b, :], xn[:, z, :], ALU.add).then_inc(b_x, 1)

            software_pipeline(dve, [(0, b_scale), (4, tail_norm("b")), (0, b_expand(0)), (4, tail_rms),
                                    (3, b_residual), (0, b_expand(1)), (3, tail_stats("b", b_x1)), (2, add_bias(0, b_xb)), (2, b_recip),
                                    (3, tail_aggr("b")), (2, b_norm)], peel=8)

            def route(n, logits, bias):
                at = n * R_COUNT
                count = [at]

                def done(ins):
                    count[0] += 1
                    ins.then_inc(r_dve, 1)

                def after_all():
                    dve.wait_ge(r_dve, count[0])

                if bias is None:
                    done(nc.vector.tensor_copy(lg[:, :, :], logits))
                else:
                    done(nc.vector.tensor_tensor(lg[:, :, :], logits, bias.unsqueeze(1).to_broadcast([P, NB, NE]),
                                                 ALU.add))
                after_all()
                for b in range(NB):
                    i = nc.vector.max(mx8[:, b, :], lg[:, b, :])
                done(i)
                after_all()
                for b in range(NB):
                    i = nc.vector.max_index(ix8[:, b, :], mx8[:, b, :], lg[:, b, :])
                done(i)
                done(nc.vector.tensor_tensor(rt[:, 0, :], mx8[:, :, 1], mx8[:, :, 0], ALU.subtract))
                after_all()
                done(nc.vector.tensor_copy(rt[:, 4:6, :].rearrange("p j b -> p b j"), ix8[:, :, 0:2]))
                dve.wait_ge(r_act, n + 1)
                done(nc.vector.tensor_scalar(rt[:, 2, :], rt[:, 1, :], 1.0, None, ALU.add))
                after_all()
                done(nc.vector.reciprocal(rt[:, 3, :], rt[:, 2, :]))
                after_all()
                done(nc.vector.tensor_tensor(rt[:, 2, :], rt[:, 1, :], rt[:, 3, :], ALU.mult))
                experts = iota.unsqueeze(1).to_broadcast([P, NB, NE])
                for j in range(2):
                    done(nc.vector.tensor_tensor(oh[:, j], experts, rt[:, 4 + j, :].unsqueeze(2).to_broadcast([P, NB, NE]),
                                                 ALU.is_equal))
                after_all()
                for j in range(2):
                    done(nc.vector.tensor_tensor(oh[:, j], oh[:, j], rt[:, 3 - j, :].unsqueeze(2).to_broadcast([P, NB, NE]),
                                                 ALU.mult))
                after_all()
                done(nc.vector.tensor_tensor(gate[:, :, :], oh[:, 0], oh[:, 1], ALU.add))
                after_all()
                assert count[0] == at + R_COUNT

            def route_experts():
                dve.wait_ge(tails["b"]["lg"], NB)
                dve.wait_ge(b_x, NB)
                route(0, logits0, None)

            def c_hidden(g, e):
                u = g * NE + e
                for j in range(DN_TILES):
                    v = u * DN_TILES + j
                    dve.wait_ge(c_silu, v + 1)
                    dve.wait_ge(c_up, v + 1)
                    if not isinstance(u, int) or u >= 2:
                        dve.wait_ge(c_dn, u - 1)
                    nc.vector.tensor_tensor(hT[:, e % 2, j, :], psum[:, 2 * j, :], silu[:, j, :], ALU.mult
                                            ).then_inc(c_h, 1)

            def c_accumulate(g, e):
                u = g * NE + e
                dve.wait_ge(c_dn, u + 1)
                if e:
                    dve.wait_ge(c_acc, u)
                for sq in range(SEQS):
                    b = g * SEQS + sq
                    i = nc.vector.scalar_tensor_tensor(out=x[:, b, :], in0=psum[:, 4 + e % 2, sq * D:(sq + 1) * D],
                                                       scalar=gate[:, b, e:e + 1], in1=x[:, b, :],
                                                       op0=ALU.mult, op1=ALU.add)
                i.then_inc(c_acc, 1)

            c_stats, c_aggr, c_norm = tail_stats("c", c_acc), tail_aggr("c"), tail_norm("c")

            def c_tail(g, stage, sq):
                b, z = g * SEQS + sq, sq % 2
                if stage is c_stats:
                    stage(b, z, (g + 1) * NE)
                    c_aggr(b, z)
                else:
                    stage(b, z)

            def c_slot(g, e):
                c_hidden(g, e)
                if isinstance(g, int) and g == 0 and e == ROUTE_SLOT:
                    route_experts()
                if e:
                    c_accumulate(g, e - 1)
                elif not isinstance(g, int) or g:
                    c_accumulate(g - 1, NE - 1)
                if not isinstance(g, int) or g:
                    if e in NORM_SLOTS:
                        c_tail(g - 1, c_norm, e - NORM_SLOTS[0])
                    if e in STATS_SLOTS:
                        c_tail(g - 1, c_stats, e - STATS_SLOTS[0])

            slots(dve, c_slot, NE)
            c_accumulate(GROUPS - 1, NE - 1)
            for stage, sq in ((c_stats, 0), (c_stats, 1), (c_norm, 0), (c_stats, 2), (c_norm, 1), (c_stats, 3),
                              (c_norm, 2), (c_norm, 3)):
                c_tail(GROUPS - 1, stage, sq)

            def d_queries(b, z):
                dve.wait_ge(d_q, b + 1)
                reused(dve, d_s, b)
                nc.vector.tensor_tensor(q2[:, z].rearrange("p (a h) q -> p a h q", a=2),
                                        psum[:, 0:2, :].rearrange("p a (h q) -> p a h q", q=LQ),
                                        cvec.rearrange("p (a h) -> p a h", a=2).unsqueeze(3).to_broadcast([P, 2, 4, LQ]),
                                        ALU.add).then_inc(d_q2, 1)

            def d_scores(b, z):
                dve.wait_ge(d_s, b + 1)
                reused(dve, d_exp, b)
                for a in range(2):
                    i = nc.vector.tensor_tensor(
                        s1[:, z, 4 * a:4 * a + 4, :].rearrange("p (n i) k -> p n i k", n=2),
                        psum[:, 2 + a, 0:4 * LK].rearrange("p (n i k) -> p n i k", n=2, i=2),
                        window[:, 2 * a:2 * a + 2, :].unsqueeze(2).to_broadcast([P, 2, 2, LK]), ALU.add)
                i.then_inc(d_sm, 1)
                dve.wait_ge(d_sm, b + 1)
                reused(dve, d_mu, b)
                nc.vector.tensor_reduce(d8[:, z, 0, :], s1[:, z], AX_X, ALU.max, negate=True).then_inc(d_max, 1)
                dve.wait_ge(d_max, b + 1)
                reused(dve, d_sh, b)
                nc.vector.tensor_tensor(d8[:, z, 2, :], u1s[:, b, :], d8[:, z, 0, :], ALU.subtract).then_inc(d_mu, 1)
                dve.wait_ge(d_mu, b + 1)
                nc.vector.tensor_tensor(d8[:, z, 3, :], u1s[:, b, :], d8[:, z, 2, :], ALU.subtract).then_inc(d_sh, 1)

            def d_weights(b, z):
                dve.wait_ge(d_exp, b + 1)
                reused(dve, d_a, b)
                nc.vector.reciprocal(d8[:, z, 1, :], d8[:, z, 4, :]).then_inc(d_rs, 1)
                dve.wait_ge(d_rs, b + 1)
                reused(dve, d_tp, b)
                nc.vector.tensor_tensor(a1[:, z], e1[:, z], d8[:, z, 1, :].unsqueeze(2).to_broadcast([P, H1, LK]),
                                        ALU.mult).then_inc(d_a, 1)

            def d_residual(b, z):
                dve.wait_ge(d_y, b + 1)
                dve.wait_ge(d_xb, b + 1)
                nc.vector.tensor_tensor(x[:, b, :], psum[:, BANK_TAIL, 128:128 + D], x[:, b, :], ALU.add
                                        ).then_inc(d_x, 1)

            dve.wait_ge(tails["c"]["lg"], NB)
            nc.vector.tensor_tensor(u1s[:, :, :], u1, ubias.unsqueeze(1).to_broadcast([P, NB, H1]), ALU.add
                                    ).then_inc(d_u, 1)
            dve.wait_ge(d_u, 1)
            software_pipeline(dve, [(5, tail_norm("d")), (1, d_scores), (0, d_queries), (2, d_weights),
                                    (2, add_bias(1, d_xb)), (4, d_residual), (4, tail_stats("d", d_x)), (4, tail_aggr("d"))], peel=8)

            def e_bias(g):
                for sq in range(SEQS):
                    i = nc.vector.tensor_scalar(b2blk[:, sq, :], b2rows[:, :], headmask[:, bass.ds(g * SEQS + sq, 1)],
                                                None, ALU.mult)
                i.then_inc(e_b2, 1)

            dve.wait_ge(tails["d"]["lg"], NB)
            route(1, logits1, rb1)
            dve.wait_ge(e_gt, 1)
            nc.vector.tensor_copy(gateT[:, :], psum[:, BANK_TAIL, 0:P]).then_inc(e_gts, 1)
            nc.vector.tensor_copy(gT_hi[:, :], psum[:, BANK_TAIL, 0:P]).then_inc(e_gts, 1)
            dve.wait_ge(e_gts, 2)
            nc.vector.tensor_tensor(gT_lo[:, :], gateT[:, :], gT_hi[:, :].bitcast(F32), ALU.subtract).then_inc(e_gts, 1)
            dve.wait_ge(e_gts, 3)

            def e_mask(g):
                if not isinstance(g, int) or g:
                    dve.wait_ge(e_gps, g * H1_TILES)
                for sq in range(SEQS):
                    row = headmask[:, bass.ds(g * SEQS + sq, 1)]
                    nc.vector.tensor_scalar(gm_hi[:, sq, :], gT_hi[:, :].bitcast(F32), row, None, ALU.mult)
                    i = nc.vector.tensor_scalar(gm_lo[:, sq, :], gT_lo[:, :].bitcast(F32), row, None, ALU.mult)
                i.then_inc(e_gm, 1)

            def e_residual(g):
                dve.wait_ge(e_y, g + 1)
                if not isinstance(g, int) or g:
                    dve.wait_ge(e_out, g * 16)
                nc.vector.tensor_tensor(yacc.rearrange("p s d -> p (s d)"), psum[:, 4, :],
                                        x[:, bass.ds(g * SEQS, SEQS), :].rearrange("p s d -> p (s d)"), ALU.add
                                        ).then_inc(e_acc, 1)

            def e_slot(g, m):
                v = g * H1_TILES + m
                if m == 0:
                    e_mask(g)
                    if not isinstance(g, int) or g:
                        e_residual(g - 1)
                    e_bias(g)
                dve.wait_ge(e_g, v + 1)
                dve.wait_ge(e_gps, v + 1)
                nc.vector.tensor_tensor(hg[:, m, :], psum[:, 2 + m % 2, :], h1[:, m % 2, :], ALU.mult).then_inc(e_hg, 1)

            slots(dve, e_slot, H1_TILES)
            e_residual(GROUPS - 1)

        @block.tensor
        def _(pe):
            def turn(dst, src, k):
                return nc.tensor.transpose(dst, src, ident[0:k, 0:k])

            pe.wait_ge(ld_first, 16 * N_FIRST)
            for i in range(4):
                m = turn(psum[:, 0, i * D:(i + 1) * D], nat0[:, i, :], P)
            m.then_inc(w0_ps, 1)
            pe.wait_ge(consts_set, 5)
            turn(psum[:, 4, 0:NE], nat0[0:NE, 4, :], NE)
            turn(psum[0:3, 4, 8:8 + DH0], wsm[0:DH0, 0:3], DH0)
            turn(psum[0:DH0, 4, 128:128 + DH0], wsm[0:DH0, 3:3 + DH0], DH0)
            nc.tensor.matmul(psum[0:DH0, 4, 256:256 + P], wsm[0:1, 3 + DH0:3 + 2 * DH0], ones[0:1, :],
                             start=True, stop=True).then_inc(w0_ps, 1)
            pe.wait_ge(w0_sb, 2)
            for c in range(3):
                nc.tensor.matmul(psum[:, 5, c * DH0:(c + 1) * DH0], sel[0:3, c, :], w1T[:, :], start=True, stop=True)
            nc.tensor.matmul(psum[0:1, 5, 256:256 + D], bv0, w4T[:, 3, :], start=True, stop=False)
            nc.tensor.matmul(psum[0:1, 5, 256:256 + D], ones[0:1, 0:1], bo0[:, :], start=False, stop=True
                             ).then_inc(w0_ps, 1)

            def a_turn(b, z):
                pe.wait_ge(a_xn, b + 1)
                pe.wait_ge(ld_ctx[z], (b - z + 2) * 8)
                if not isinstance(b, int) or b >= 1:
                    pe.wait_ge(a_xc, b)
                turn(psum[:, 0, 0:LQ], xn[:, z, :], P)
                turn(psum[:, 0, LQ:LQ + LK], craw[:, z, :], LK).then_inc(a_tps, 1)

            def a_project(b, z):
                pe.wait_ge(a_xc, b + 1)
                if not isinstance(b, int) or b >= 1:
                    pe.wait_ge(a_k, b)
                    pe.wait_ge(a_v, b)
                nc.tensor.matmul(psum[:, 1, 0:LQ], w4T[:, 0, :], xc[:, z, 0:LQ], start=True, stop=True)
                nc.tensor.matmul(psum[:, 1, LQ:LQ + LK], w4T[:, 1, :], xc[:, z, LQ:LQ + LK], start=True, stop=True)
                nc.tensor.matmul(psum[0:LK, 2, 0:D], xc[:, z, LQ:LQ + LK], w4T[:, 2, :], start=True, stop=True
                                 ).then_inc(a_qkv, 1)

            def a_scores(half):
                def run(b, z):
                    pe.wait_ge(a_q, b + 1)
                    pe.wait_ge(a_kexp, b + 1)
                    if not isinstance(b, int) or b >= 1:
                        pe.wait_ge(a_exp, b * 2 + half - 1)
                    for j in range(2):
                        h = half * HALF0 + 4 * j
                        m = nc.tensor.matmul(psum[:, 3 + 2 * half + j, 0:4 * LK], qs[:, z, :],
                                             kexp[:, z, h:h + 4, :].rearrange("p h k -> p (h k)"), start=True, stop=True)
                    m.then_inc(a_s, 1)
                return run

            software_pipeline(pe, [(3, a_scores(0)), (1, a_turn), (3, a_scores(1)), (1, a_project)], peel=6)

            pe.wait_ge(ld_w, 16 * N_W)
            small1 = keep[:, 384:384 + 2 * H1]
            for h in range(H1):
                nc.tensor.matmul(small1[:, h:h + 1], l1N[:, 1, h, :], bqk1[:, 0, h:h + 1], start=True, stop=True)
                m = nc.tensor.matmul(small1[:, H1 + h:H1 + h + 1], l1N[:, 0, h, :], bqk1[:, 1, h:h + 1],
                                     start=True, stop=True)
            m.then_inc(l1_pe, 1)
            pe.wait_ge(a_exp, 2 * NB)
            pe.wait_ge(a_xc, NB)
            pe.wait_ge(a_k, NB)
            pe.wait_ge(a_v, NB)
            def weights(groups):
                for g in groups:
                    if g >= RING_W:
                        group_copied(pe, g - RING_W)
                    if g == WC_GROUPS[-1] + 3:
                        group_copied(pe, WC_GROUPS[-1])
                    for i, ops in enumerate(weight_groups()[g][1]):
                        dst = psum[:, g % RING_W, i * D:(i + 1) * D]
                        m = turn(dst, ops[1], P) if ops[0] == "turn" else \
                            nc.tensor.matmul(dst, ops[1], ops[2], start=True, stop=True)
                    m.then_inc(wt_ps, 1)

            weights(range(ACT_GROUPS))
            pe.wait_ge(f_dve, 5)
            for c, feature in enumerate((small[:, 4, :], rowneg[:, :], small[:, 2, :])):
                m = nc.tensor.matmul(psum[0:DH0, 4, 0:BH], w1f[:, c, :], feature, start=(c == 0), stop=(c == 2))
            m.then_inc(mlp_pe, 1)
            weights(range(ACT_GROUPS, ACT_GROUPS + 3))
            pe.wait_ge(mlp_act, 1)
            nc.tensor.matmul(psum[0:DH0, 5, 0:BH], w2T[:, :], small[0:DH0, 6, :], start=True, stop=True
                             ).then_inc(mlp_pe, 1)
            weights(range(ACT_GROUPS + 3, N_GROUPS - 3))
            pe.wait_ge(mlp_act, 2)
            nc.tensor.matmul(psum[:, 4, 256:512], w3c[:, :], small[0:DH0, 7, :], start=True, stop=True
                             ).then_inc(mlp_pe, 1)
            pe.wait_ge(l1_dve, 1)
            group_copied(pe, WC_GROUPS[-1])
            nc.tensor.matmul(psum[:, 6, 2 * H1:3 * H1], ones[:, :], bqk[:, :], start=True, stop=True)
            nc.tensor.matmul(psum[0:1, 6, 256:256 + D], ones[0:1, 0:1], bc1[:, :], start=True, stop=False)
            for h in range(H1):
                m = nc.tensor.matmul(psum[0:1, 6, 256:256 + D], bqk1[:, 2, h:h + 1], wcT[:, h, :],
                                     start=False, stop=(h == H1 - 1))
            m.then_inc(l1_pe, 1)

            pe.wait_ge(temp_dve, T_SCALED)
            for half in range(2):
                m = turn(psum[:, 5, half * P:(half + 1) * P], small[:, 2, half * P:(half + 1) * P], P)
            m.then_inc(mlp_pe, 1)
            weights(range(N_GROUPS - 3, N_GROUPS))

            def tail_turn(ph):
                s = tails[ph]

                def run(b, z):
                    pe.wait_ge(s["xr" if ph == "b" else "xn"], b + 1)
                    if not isinstance(b, int) or b >= 1:
                        pe.wait_ge(s["ev"], b)
                    if ph == "d":
                        pe.wait_ge(d_x, min(b + 2, NB) if isinstance(b, int) else b + 2)
                    turn(tail_ps, (xr if ph == "b" else xn)[:, z, :], P).then_inc(s["tp"], 1)
                return run

            def tail_logits(ph, dst, weights):
                s = tails[ph]

                def run(b, z):
                    pe.wait_ge(s["ev"], b + 1)
                    nc.tensor.matmul(dst[:, b, :], xnT[:, z, :], weights, start=True, stop=True).then_inc(s["lg"], 1)
                return run

            def b_scores(half):
                def run(b, z):
                    pe.wait_ge(b_qexp, b * 2 + half + 1)
                    pe.wait_ge(b_kt, b + 1)
                    if not isinstance(b, int) or b >= 1:
                        pe.wait_ge(b_exp, b * 2 + half - 1)
                    for j in range(2):
                        h = half * HALF0 + 4 * j
                        nc.tensor.matmul(psum[0:LK, 2 * half + j, :], ktS[:, z, :],
                                         qexp[:, z, h:h + 4, :].rearrange("p h q -> p (h q)"), start=True, stop=False)
                    pe.wait_ge(ld_m[z], (b - z + 2) * 8)
                    for j in range(2):
                        h, dst = half * HALF0 + 4 * j, psum[0:LK, 2 * half + j, :]
                        m = nc.tensor.matmul(dst, onesb[:, :], mrow[:, z, h * LQ:(h + 4) * LQ], start=False, stop=True)
                    m.then_inc(b_s, 1)
                return run

            def b_output(b, z):
                pe.wait_ge(b_exp, b * 2 + 2)
                pe.wait_ge(b_v, b + 1)
                if not isinstance(b, int) or b >= 1:
                    pe.wait_ge(b_oT, b)
                for c, pad in ((0, None), (1, opad)):
                    for g in range(4):
                        for i in range(4):
                            w = vpad[:, z, g, 32 * i:32 * i + 32] if pad is None else pad[:, 32 * i:32 * i + 32]
                            m = nc.tensor.matmul(psum[32 * g:32 * g + 32, 4, c * LQ:(c + 1) * LQ], w,
                                                 probT[:, z, 4 * g + i, :], start=(i == 0), stop=(i == 3))
                m.then_inc(b_od, 1)

            def b_project(b, z):
                pe.wait_ge(b_oT, b + 1)
                if not isinstance(b, int) or b >= 1:
                    pe.wait_ge(b_x1, b)
                nc.tensor.matmul(psum[:, 5, 0:D], oT[:, z, :], w4T[:, 3, :], start=True, stop=True).then_inc(b_y, 1)

            pe.wait_ge(l1_dve, 5)
            for i, row in enumerate((bout1, bout0)):
                m = nc.tensor.matmul(psum[:, 6, 256 + i * D:256 + (i + 1) * D], ones[0:1, :], row[:, :],
                                     start=True, stop=True)
            m.then_inc(l1_pe, 1)
            pe.wait_ge(temp_dve, T_PARTS)
            software_pipeline(pe, [(5, tail_turn("b")), (1, b_scores(0)), (3, b_project), (2, b_output),
                                   (5, tail_logits("b", logits0, routerT)), (1, b_scores(1))], peel=8)

            def c_up_project(g, e):
                columns = lambda a: a[:, bass.ds(g * SEQS, SEQS), :].rearrange("p b q -> p (b q)")
                for j in range(DN_TILES):
                    v = (g * NE + e) * DN_TILES + j
                    if not isinstance(v, int) or v >= DN_TILES:
                        pe.wait_ge(c_h, v - 1)
                    for bank, tile, done in ((2 * j + 1, DN_TILES + j, c_gate), (2 * j, j, c_up)):
                        w = e * UP_TILES + tile
                        nc.tensor.matmul(psum[:, bank, :], up_hi[:, w, :], columns(x_hi), start=True, stop=False)
                        nc.tensor.matmul(psum[:, bank, :], up_hi[:, w, :], columns(x_lo), start=False, stop=False)
                        nc.tensor.matmul(psum[:, bank, :], up_lo[:, w, :], columns(x_hi), start=False, stop=True
                                         ).then_inc(done, 1)

            def c_down_project(g, e):
                u = g * NE + e
                pe.wait_ge(c_h, (u + 1) * DN_TILES)
                if not isinstance(u, int) or u >= 2:
                    pe.wait_ge(c_acc, u - 1)
                for sq in range(SEQS):
                    for j in range(DN_TILES):
                        m = nc.tensor.matmul(psum[:, 4 + e % 2, sq * D:(sq + 1) * D],
                                             hT[:, e % 2, j, sq * LQ:(sq + 1) * LQ], dnT[:, e * DN_TILES + j, :],
                                             start=(j == 0), stop=(j == DN_TILES - 1))
                m.then_inc(c_dn, 1)

            c_turn, c_logits = tail_turn("c"), tail_logits("c", u1, uvec)

            def c_slot(g, e):
                tails_too = not isinstance(g, int) or g > 0
                c_up_project(g, e)
                if e:
                    c_down_project(g, e - 1)
                elif tails_too:
                    c_down_project(g - 1, NE - 1)
                if tails_too and e in LOGITS_SLOTS:
                    c_logits((g - 1) * SEQS + e - LOGITS_SLOTS[0], (e - LOGITS_SLOTS[0]) % 2)
                if tails_too and e in TURN_SLOTS:
                    c_turn((g - 1) * SEQS + e - TURN_SLOTS[0], (e - TURN_SLOTS[0]) % 2)

            pe.wait_ge(tails["b"]["keep"], NB)
            pe.wait_ge(b_lo, NB)
            slots(pe, c_slot, NE)
            c_down_project(GROUPS - 1, NE - 1)
            for stage, sq in ((c_turn, 0), (c_turn, 1), (c_logits, 0), (c_turn, 2), (c_logits, 1), (c_turn, 3),
                              (c_logits, 2), (c_logits, 3)):
                stage((GROUPS - 1) * SEQS + sq, sq % 2)

            def d_queries(b, z):
                if not isinstance(b, int) or b >= 1:
                    pe.wait_ge(d_q2, b)
                for h in range(H1):
                    m = nc.tensor.matmul(psum[:, h // 4, (h % 4) * LQ:(h % 4 + 1) * LQ], qk1[:, h, :], xT[:, b, :],
                                         start=True, stop=True)
                m.then_inc(d_q, 1)

            def d_scores(b, z):
                pe.wait_ge(d_q2, b + 1)
                if not isinstance(b, int) or b >= 1:
                    pe.wait_ge(d_sm, b)
                for h in range(H1):
                    m = nc.tensor.matmul(psum[:, 2 + h // 4, (h % 4) * LK:(h % 4 + 1) * LK], q2[:, z, h, :],
                                         ctxT[:, b, :], start=True, stop=True)
                m.then_inc(d_s, 1)

            def d_values(b, z):
                pe.wait_ge(d_cs, b + 1)
                if not isinstance(b, int) or b >= 1:
                    pe.wait_ge(d_aT, b)
                parts = ((c_hi, vo_hi), (c_hi, vo_lo), (c_lo, vo_hi))
                for a in range(2):
                    for i, (c, vo) in enumerate(parts):
                        m = nc.tensor.matmul(psum[0:LK, 4 + a, :], c[:, z, :],
                                             vo[:, 4 * a:4 * a + 4, :].rearrange("p h d -> p (h d)"),
                                             start=(i == 0), stop=(i == len(parts) - 1))
                m.then_inc(d_vwp, 1)

            def d_turn(b, z):
                pe.wait_ge(d_a, b + 1)
                pe.wait_ge(d_vw, b + 1)
                for h in range(H1):
                    m = turn(psum[0:LK, 4 + h // 4, (h % 4) * LQ:(h % 4 + 1) * LQ], a1[:, z, h, :], P)
                m.then_inc(d_tp, 1)

            def d_output(b, z):
                pe.wait_ge(d_aT, b + 1)
                pe.wait_ge(d_vw, b + 1)
                if not isinstance(b, int) or b >= 1:
                    pe.wait_ge(d_x, b)
                reused(pe, tails["d"]["ev"], b)
                dst = psum[:, BANK_TAIL, 128:128 + D]
                for h in range(H1):
                    m = nc.tensor.matmul(dst, a1T[:, z, h, :], vw[:, z, h, :], start=(h == 0), stop=(h == H1 - 1))
                m.then_inc(d_y, 1)

            pe.wait_ge(tails["c"]["keep"], NB)
            pe.wait_ge(halved, 2)
            pe.wait_ge(ld_late, 16 * (N_LATE + 1))
            software_pipeline(pe, [(1, d_scores), (6, tail_turn("d")), (3, d_values), (0, d_queries), (3, d_turn),
                                   (4, d_output), (6, tail_logits("d", logits1, router1))], peel=8)

            pe.wait_ge(tails["d"]["keep"], NB)

            def e_hidden(g, m):
                v = g * H1_TILES + m
                if not isinstance(v, int) or v >= 2:
                    pe.wait_ge(e_g, v - 1)
                group = bass.ds(g * SEQS, SEQS)
                for i, (w, xs) in enumerate(((w1_hi, x_hi), (w1_hi, x_lo), (w1_lo, x_hi))):
                    mm = nc.tensor.matmul(psum[:, m % 2, :], w[:, m * P:(m + 1) * P],
                                          xs[:, group, :].rearrange("p b q -> p (b q)"), start=(i == 0), stop=(i == 2))
                mm.then_inc(e_h, 1)

            def e_gates(g, m):
                v = g * H1_TILES + m
                pe.wait_ge(e_gm, g + 1)
                if not isinstance(v, int) or v >= 2:
                    pe.wait_ge(e_hg, v - 1)
                for i, part in enumerate((gm_hi, gm_lo)):
                    mm = nc.tensor.matmul(psum[:, 2 + m % 2, :], rows_r[:, m, :], part.rearrange("p s q -> p (s q)"),
                                          start=(i == 0), stop=(i == 1))
                mm.then_inc(e_gps, 1)

            def e_output(g):
                pe.wait_ge(e_b2, g + 1)
                pe.wait_ge(e_hg, (g + 1) * H1_TILES)
                if not isinstance(g, int) or g:
                    pe.wait_ge(e_acc, g)
                for sq in range(SEQS):
                    dst = psum[:, 4, sq * D:(sq + 1) * D]
                    nc.tensor.matmul(dst, gateT[:, :], b2blk[:, sq, :], start=True, stop=False)
                    for m in range(H1_TILES):
                        mm = nc.tensor.matmul(dst, hg[:, m, sq * LQ:(sq + 1) * LQ], ew2[:, m, :],
                                              start=False, stop=(m == H1_TILES - 1))
                mm.then_inc(e_y, 1)

            for m in range(2):
                e_hidden(0, m)
            pe.wait_ge(r_dve, 2 * R_COUNT)
            turn(psum[:, BANK_TAIL, 0:P], gate.rearrange("p b e -> p (b e)"), P).then_inc(e_gt, 1)

            def e_slot(g, m):
                if not isinstance(g, int) or g or m >= 2:
                    e_hidden(g, m)
                if m == 0 and (not isinstance(g, int) or g):
                    e_output(g - 1)
                e_gates(g, m)

            slots(pe, e_slot, H1_TILES)
            e_output(GROUPS - 1)


_INS = ['x', 'ctx_1024', 'L0_xattn_Wq', 'L0_xattn_bq', 'L0_xattn_Wk', 'L0_xattn_bk', 'L0_xattn_Wv', 'L0_xattn_bv',
        'L0_xattn_Wo', 'L0_xattn_bo', 'L0_xattn_w1', 'L0_xattn_b1', 'L0_xattn_w2', 'L0_xattn_b2', 'L0_xattn_w3',
        'L0_xattn_b3', 'L0_ffn_norm_scale', 'L0_ffn_w_router', 'L0_ffn_w_up', 'L0_ffn_w_down', 'L1_xattn_Wq',
        'L1_xattn_bq', 'L1_xattn_Wk', 'L1_xattn_bk', 'L1_xattn_Wv', 'L1_xattn_bv', 'L1_xattn_Wc', 'L1_xattn_bc',
        'L1_ffn_router_w', 'L1_ffn_router_b', 'L1_ffn_W1', 'L1_ffn_b1', 'L1_ffn_W2', 'L1_ffn_b2']


def kernel(**inputs):
    import numpy as _np
    import concourse.bacc as _bacc
    from concourse import mybir as _mybir
    from concourse.bass_utils import run_bass_kernel_spmd as _run

    nc = _bacc.Bacc("TRN2", target_bir_lowering=False, num_devices=1)
    cols, consts = shape_constants()
    arrays, t = {}, {}
    for name, value in [(n, inputs[n]) for n in _INS] + [("consts", consts)]:
        a = _np.ascontiguousarray(value)
        arrays[f"in_{name}_dram"] = a
        t[name] = nc.dram_tensor(f"in_{name}_dram", a.shape, _mybir.dt.from_np(a.dtype), kind="ExternalInput").ap()
    out = nc.dram_tensor("out_0_dram", (NB, LQ, D), F32, kind="ExternalOutput").ap()
    build(nc, cols, t, out)
    r = _run(nc, [arrays], core_ids=[0])
    return r.results[0]["out_0_dram"]
```
